# Optimizing a Trainium2 kernel written in Bass

```python
import numpy as np
import jax
import jax.numpy as jnp

def _softmax(x, axis=-1):
    return jax.nn.softmax(x, axis=axis)

def _gelu(x):
    return jax.nn.gelu(x, approximate=True)

def _silu(x):
    return jax.nn.silu(x)

def _sigmoid(x):
    return jax.nn.sigmoid(x)

def _layernorm(x, axis=-1, eps=1e-05):
    m = jnp.mean(x, axis=axis, keepdims=True)
    v = jnp.var(x, axis=axis, keepdims=True)
    return (x - m) / jnp.sqrt(v + eps)

def _scatter_add(tgt, idx, src, axis=0):
    return tgt.at[idx].add(src)

def _segment_sum(src, seg, n):
    return jax.ops.segment_sum(src, seg, n)
kernel_name = 'mk_decoder_postln_d1_seqx_r8_d68129'

def setup_inputs(seed: int=0):
    np.random.seed(seed)
    _w = jnp.asarray

    def _rec_inputs():
        import jax
        import jax.numpy as jnp
        _rk = jax.random.key(seed)
        x = 7.22e-05 + 1 * jax.random.normal(jax.random.fold_in(_rk, 1), (4, 256, 256), jnp.float32)
        _lenS = 256 - jax.random.randint(jax.random.fold_in(_rk, 7), (4,), 0, max(1, 256 // 4) + 1, jnp.int32)
        _lenS2 = 256 - jax.random.randint(jax.random.fold_in(_rk, 8), (4,), 0, max(1, 256 // 4) + 1, jnp.int32)
        _ctx_1024P = jax.random.normal(jax.random.fold_in(_rk, 11), (4, 16, 128), jnp.float32)
        _ctx_1024c = jax.random.dirichlet(jax.random.fold_in(_rk, 511), 0.3 * jnp.ones((16,), jnp.float32), (4, 256))
        _ctx_1024t = jnp.einsum('bsk,bkd->bsd', _ctx_1024c, _ctx_1024P)
        _ctx_1024t = _ctx_1024t * jax.lax.rsqrt(jnp.mean(jnp.square(_ctx_1024t)) + 1e-12) * 0.953939
        ctx_1024 = 2.81802e-05 + 1.00001 * (_ctx_1024t + 0.3 * jax.random.normal(jax.random.fold_in(_rk, 611), (4, 256, 128), jnp.float32))
        return (x, ctx_1024)
    x, ctx_1024 = _rec_inputs()

    def _L0_attn_setup():
        import jax, jax.numpy as jnp
        import numpy as np
        B, T, C = (1, 512, 256)
        H, HK, D = (16, 4, 128)
        W = 128
        THETA = 10000.0

        def sine_table(features, length, max_timescale):
            fraction = jnp.arange(0, features, 2, dtype=jnp.float32) / features
            timescale = max_timescale ** fraction
            ang = jnp.arange(length, dtype=jnp.float32)[:, None] / timescale[None, :]
            ang = jnp.concatenate([ang, ang], axis=-1)
            return (jnp.sin(ang), jnp.cos(ang))

        def rotate_half(x):
            x1, x2 = jnp.split(x, 2, axis=-1)
            return jnp.concatenate([-x2, x1], axis=-1)

        def apply_rope(u, sin, cos):
            return u * cos[None, :, None, :] + rotate_half(u) * sin[None, :, None, :]
        key = jax.random.key(seed)
        ks = jax.random.split(key, 5)
        std = 0.02
        return {'x': jax.random.normal(ks[0], (B, T, C), jnp.float32), 'q_kernel': jax.random.normal(ks[1], (C, H * D), jnp.float32) * std, 'k_kernel': jax.random.normal(ks[2], (C, HK * D), jnp.float32) * std, 'v_kernel': jax.random.normal(ks[3], (C, HK * D), jnp.float32) * std, 'out_kernel': jax.random.normal(ks[4], (H * D, C), jnp.float32) * std}
    _L0_attn_all = _L0_attn_setup()
    _L0_attn_in = {k: v for k, v in _L0_attn_all.items() if k in ('q_kernel', 'k_kernel', 'v_kernel', 'out_kernel')}
    del _L0_attn_all

    def _L0_xattn_setup():
        import jax, jax.numpy as jnp
        import numpy as np
        key = jax.random.key(seed)
        ks = jax.random.split(key, 6)
        B, L, N, C, D = (8, 64, 256, 128, 128)
        return {'teacher_logits': jax.random.normal(ks[0], (B, L, N), dtype=jnp.float32), 'teacher_features': jax.random.normal(ks[1], (B, N, C), dtype=jnp.float32), 'Wq': jax.random.normal(ks[2], (D, C), dtype=jnp.float32) * (1.0 / np.sqrt(C)), 'bq': jnp.zeros((D,), dtype=jnp.float32), 'Wk': jax.random.normal(ks[3], (D, C), dtype=jnp.float32) * (1.0 / np.sqrt(C)), 'bk': jnp.zeros((D,), dtype=jnp.float32)}
    _L0_xattn_all = _L0_xattn_setup()
    _L0_xattn_in = {k: v for k, v in _L0_xattn_all.items() if k in ('Wq', 'bq', 'Wk', 'bk')}
    del _L0_xattn_all

    def _L0_ffn_setup():
        import jax, jax.numpy as jnp
        import numpy as np
        D_MODEL, D_FF, NS, NR, KR = (256, 176, 2, 16, 4)
        B, S = (4, 256)

        def _moe_forward(u, shared_w1, shared_b1, shared_w2, shared_b2, routed_w1, routed_b1, routed_w2, routed_b2, centroids, bias):
            b, s, d = u.shape
            flat = u.reshape(-1, d)
            T = flat.shape[0]
            h = jax.nn.relu(jnp.einsum('td,ndf->ntf', flat, shared_w1) + shared_b1[:, None, :])
            shared_out = jnp.einsum('ntf,nfd->td', h, shared_w2) + shared_b2.sum(0)
            out = flat + shared_out
            scores = jax.nn.sigmoid(flat @ centroids.T) + bias
            vals, idx = jax.lax.top_k(scores, KR)
            gating = jnp.zeros_like(scores).at[jnp.arange(T)[:, None], idx].set(vals)
            gating = gating / jnp.clip(gating.sum(-1, keepdims=True), 1e-08)

            def step(acc, ew):
                w1, b1, w2, b2, g = ew
                hj = jax.nn.relu(flat @ w1 + b1)
                yj = hj @ w2 + b2
                return (acc + yj * g[:, None], None)
            rout0 = jnp.zeros_like(flat)
            rout, _ = jax.lax.scan(step, rout0, (routed_w1, routed_b1, routed_w2, routed_b2, gating.T))
            return (out + rout).reshape(b, s, d)
        key = jax.random.key(seed)
        ks = jax.random.split(key, 10)
        s1 = 1.0 / np.sqrt(D_MODEL)
        s2 = 1.0 / np.sqrt(D_FF)
        return {'u': jax.random.normal(ks[0], (B, S, D_MODEL), dtype=jnp.float32), 'shared_w1': jax.random.normal(ks[1], (NS, D_MODEL, D_FF), dtype=jnp.float32) * s1, 'shared_b1': jnp.zeros((NS, D_FF), dtype=jnp.float32), 'shared_w2': jax.random.normal(ks[2], (NS, D_FF, D_MODEL), dtype=jnp.float32) * s2, 'shared_b2': jnp.zeros((NS, D_MODEL), dtype=jnp.float32), 'routed_w1': jax.random.normal(ks[3], (NR, D_MODEL, D_FF), dtype=jnp.float32) * s1, 'routed_b1': jnp.zeros((NR, D_FF), dtype=jnp.float32), 'routed_w2': jax.random.normal(ks[4], (NR, D_FF, D_MODEL), dtype=jnp.float32) * s2, 'routed_b2': jnp.zeros((NR, D_MODEL), dtype=jnp.float32), 'centroids': jax.random.normal(ks[5], (NR, D_MODEL), dtype=jnp.float32) * s1, 'bias': jnp.zeros((NR,), dtype=jnp.float32)}
    _L0_ffn_all = _L0_ffn_setup()
    _L0_ffn_in = {k: v for k, v in _L0_ffn_all.items() if k in ('shared_w1', 'shared_b1', 'shared_w2', 'shared_b2', 'routed_w1', 'routed_b1', 'routed_w2', 'routed_b2', 'centroids', 'bias')}
    del _L0_ffn_all
    return {'x': x, 'ctx_1024': ctx_1024, 'L0_attn_q_kernel': _L0_attn_in['q_kernel'], 'L0_attn_k_kernel': _L0_attn_in['k_kernel'], 'L0_attn_v_kernel': _L0_attn_in['v_kernel'], 'L0_attn_out_kernel': _L0_attn_in['out_kernel'], 'L0_xattn_Wq': _L0_xattn_in['Wq'], 'L0_xattn_bq': _L0_xattn_in['bq'], 'L0_xattn_Wk': _L0_xattn_in['Wk'], 'L0_xattn_bk': _L0_xattn_in['bk'], 'L0_ffn_shared_w1': _L0_ffn_in['shared_w1'], 'L0_ffn_shared_b1': _L0_ffn_in['shared_b1'], 'L0_ffn_shared_w2': _L0_ffn_in['shared_w2'], 'L0_ffn_shared_b2': _L0_ffn_in['shared_b2'], 'L0_ffn_routed_w1': _L0_ffn_in['routed_w1'], 'L0_ffn_routed_b1': _L0_ffn_in['routed_b1'], 'L0_ffn_routed_w2': _L0_ffn_in['routed_w2'], 'L0_ffn_routed_b2': _L0_ffn_in['routed_b2'], 'L0_ffn_centroids': _L0_ffn_in['centroids'], 'L0_ffn_bias': _L0_ffn_in['bias']}

def reference(x, ctx_1024, L0_attn_q_kernel, L0_attn_k_kernel, L0_attn_v_kernel, L0_attn_out_kernel, L0_xattn_Wq, L0_xattn_bq, L0_xattn_Wk, L0_xattn_bk, L0_ffn_shared_w1, L0_ffn_shared_b1, L0_ffn_shared_w2, L0_ffn_shared_b2, L0_ffn_routed_w1, L0_ffn_routed_b1, L0_ffn_routed_w2, L0_ffn_routed_b2, L0_ffn_centroids, L0_ffn_bias):
    import jax
    import jax.numpy as jnp

    def _L0_attn_ref(x, q_kernel, k_kernel, v_kernel, out_kernel):
        import jax, jax.numpy as jnp
        import numpy as np
        B, T, C = (1, 512, 256)
        H, HK, D = (16, 4, 128)
        W = 128
        THETA = 10000.0

        def sine_table(features, length, max_timescale):
            fraction = jnp.arange(0, features, 2, dtype=jnp.float32) / features
            timescale = max_timescale ** fraction
            ang = jnp.arange(length, dtype=jnp.float32)[:, None] / timescale[None, :]
            ang = jnp.concatenate([ang, ang], axis=-1)
            return (jnp.sin(ang), jnp.cos(ang))

        def rotate_half(x):
            x1, x2 = jnp.split(x, 2, axis=-1)
            return jnp.concatenate([-x2, x1], axis=-1)

        def apply_rope(u, sin, cos):
            return u * cos[None, :, None, :] + rotate_half(u) * sin[None, :, None, :]
        b, t, c = x.shape
        q = jnp.dot(x, q_kernel).reshape(b, t, H, D)
        k = jnp.dot(x, k_kernel).reshape(b, t, HK, D)
        v = jnp.dot(x, v_kernel).reshape(b, t, HK, D)
        sin, cos = sine_table(D, t, THETA)
        q = apply_rope(q, sin, cos)
        k = apply_rope(k, sin, cos)
        rep = H // HK
        k = jnp.repeat(k, rep, axis=2)
        v = jnp.repeat(v, rep, axis=2)
        nb = t // W
        qb = q.reshape(b, nb, W, H, D)
        kb = k.reshape(b, nb, W, H, D)
        vb = v.reshape(b, nb, W, H, D)
        pad = ((0, 0), (1, 0), (0, 0), (0, 0), (0, 0))
        kp = jnp.pad(kb, pad)
        vp = jnp.pad(vb, pad)
        kw = jnp.concatenate([kp[:, :-1], kp[:, 1:]], axis=2)
        vw = jnp.concatenate([vp[:, :-1], vp[:, 1:]], axis=2)
        scale = 1.0 / np.sqrt(D)
        scores = jnp.einsum('bnqhd,bnkhd->bnhqk', qb, kw).astype(jnp.float32) * scale
        p = jnp.arange(W)[:, None]
        j = jnp.arange(2 * W)[None, :]
        base = (j >= p) & (j <= p + W)
        blk = jnp.arange(nb)[:, None, None]
        mask = base[None] & ((blk > 0) | (j[None] >= W))
        scores = jnp.where(mask[None, :, None], scores, jnp.float32(-1e+30))
        probs = jax.nn.softmax(scores, axis=-1).astype(v.dtype)
        ob = jnp.einsum('bnhqk,bnkhd->bnqhd', probs, vw)
        out = ob.reshape(b, t, H * D)
        return jnp.dot(out, out_kernel)

    def _L0_xattn_ref(teacher_logits, teacher_features, Wq, bq, Wk, bk):
        import jax, jax.numpy as jnp
        import numpy as np
        query = jnp.einsum('bnc,dc->bnd', teacher_features, Wq) + bq
        key = jnp.einsum('bnc,dc->bnd', teacher_features, Wk) + bk
        energy = jnp.einsum('bnd,bmd->bnm', query, key)
        attention = jax.nn.softmax(energy, axis=-1)
        x_m = jnp.einsum('bln,bmn->blm', teacher_logits, attention)
        return x_m

    def _L0_ffn_ref(u, shared_w1, shared_b1, shared_w2, shared_b2, routed_w1, routed_b1, routed_w2, routed_b2, centroids, bias):
        import jax, jax.numpy as jnp
        import numpy as np
        D_MODEL, D_FF, NS, NR, KR = (256, 176, 2, 16, 4)
        B, S = (4, 256)

        def _moe_forward(u, shared_w1, shared_b1, shared_w2, shared_b2, routed_w1, routed_b1, routed_w2, routed_b2, centroids, bias):
            b, s, d = u.shape
            flat = u.reshape(-1, d)
            T = flat.shape[0]
            h = jax.nn.relu(jnp.einsum('td,ndf->ntf', flat, shared_w1) + shared_b1[:, None, :])
            shared_out = jnp.einsum('ntf,nfd->td', h, shared_w2) + shared_b2.sum(0)
            out = flat + shared_out
            scores = jax.nn.sigmoid(flat @ centroids.T) + bias
            vals, idx = jax.lax.top_k(scores, KR)
            gating = jnp.zeros_like(scores).at[jnp.arange(T)[:, None], idx].set(vals)
            gating = gating / jnp.clip(gating.sum(-1, keepdims=True), 1e-08)

            def step(acc, ew):
                w1, b1, w2, b2, g = ew
                hj = jax.nn.relu(flat @ w1 + b1)
                yj = hj @ w2 + b2
                return (acc + yj * g[:, None], None)
            rout0 = jnp.zeros_like(flat)
            rout, _ = jax.lax.scan(step, rout0, (routed_w1, routed_b1, routed_w2, routed_b2, gating.T))
            return (out + rout).reshape(b, s, d)
        return _moe_forward(u, shared_w1, shared_b1, shared_w2, shared_b2, routed_w1, routed_b1, routed_w2, routed_b2, centroids, bias)
    x = _layernorm(x + _L0_attn_ref(x, L0_attn_q_kernel, L0_attn_k_kernel, L0_attn_v_kernel, L0_attn_out_kernel), axis=-1)
    x = _layernorm(x + _L0_xattn_ref(x, ctx_1024, L0_xattn_Wq, L0_xattn_bq, L0_xattn_Wk, L0_xattn_bk), axis=-1)
    x = _layernorm(x + _L0_ffn_ref(x, L0_ffn_shared_w1, L0_ffn_shared_b1, L0_ffn_shared_w2, L0_ffn_shared_b2, L0_ffn_routed_w1, L0_ffn_routed_b1, L0_ffn_routed_w2, L0_ffn_routed_b2, L0_ffn_centroids, L0_ffn_bias), axis=-1)
    return x

_drawn_inputs = setup_inputs


def setup_inputs(seed=0):
    import zlib

    import numpy as np

    out = dict(_drawn_inputs(seed))
    spreads = {'L0_xattn_bq': (0.0, 0.1),
     'L0_xattn_bk': (0.0, 0.8),
     'L0_ffn_shared_b1': (0.0, 0.1),
     'L0_ffn_shared_b2': (0.0, 0.1),
     'L0_ffn_routed_b1': (0.0, 0.542),
     'L0_ffn_routed_b2': (0.0, 0.368),
     'L0_ffn_bias': (0.0, 0.1)}
    factors = {'L0_attn_q_kernel': 4.944, 'L0_attn_k_kernel': 5.504}
    for name, (base, spread) in spreads.items():
        noise = np.random.default_rng([zlib.crc32(name.encode()), seed]).standard_normal(out[name].shape)
        drawn = base * np.exp(spread * noise) if base else spread * noise
        out[name] = jnp.asarray(drawn.astype(out[name].dtype))
    for name, factor in factors.items():
        out[name] = (out[name] * factor).astype(out[name].dtype)
    return out
```

```python
from contextlib import ExitStack

import numpy as np

import concourse.bass as bass
from concourse import mybir

F32 = mybir.dt.float32
F32R = mybir.dt.float32r
ALU = mybir.AluOpType
ACT = mybir.ActivationFunctionType
AX = mybir.AxisListType

P = 128
B, T, C = 4, 256, 256
KC = C // P
TT = T // P
NT = B * TT
H, HK, D = 16, 4, 128
G = H // HK
W = 128
SCALE = float(1.0 / np.sqrt(D))
MASKED = -1e30
CX = 128
NS, NR, KR, FF = 2, 16, 4, 176
NE = NS + NR
F = NE * FF
NC = -(-F // P)
LAST = F - (NC - 1) * P
GB = 16
EPS = 1e-5
THETA = 10000.0
N = B * T
HALF = 512
NEVER = -3e38

SLOTS = ["x0", "x1", "k0", "k1", "q0", "q1", "v0", "v1", "q2", "q3", "q4", "q5", "q6", "q7"]
NSLOT = len(SLOTS)
ROPES = [s for s in SLOTS if s[0] in "kq"]
NROPE = len(ROPES)
SPLITS = [s for s in SLOTS if s[0] in "xv"]
NSPLIT = len(SPLITS)
STEP_SLOTS = {0: ["q2"], 2: ["q3"], 4: ["q4"], 6: ["q5"], 8: ["q6"], 10: ["q7"]}
NEXT_SLOTS = {12: ["x0"], 13: ["x1"], 16: ["k0"], 17: ["k1"], 18: ["q0"], 19: ["q1"], 20: ["v0"], 21: ["v1"]}
STEPS = H + 6
AHEAD = 2


def due(i, lag):
    g, rest = divmod(i - lag, G)
    return g if rest == 0 and 0 <= g < HK else None


def slot_count(b, s):
    return NSLOT * b + SLOTS.index(s) + 1


def rope_count(b, s):
    return NROPE * b + ROPES.index(s) + 1


def split_count(b, s):
    return NSPLIT * b + SPLITS.index(s) + 1


def head_count(b, h):
    return H * b + h + 1 + AHEAD


def place(engine, name):
    return ORDER[engine].index(name) + 1


def pv_count(b, g, blk):
    return 2 * HK * b + 2 * g + blk + 2


def rope_tables():
    fraction = np.arange(0, D, 2, dtype=np.float32) / np.float32(D)
    timescale = np.float32(THETA) ** fraction
    angle = np.arange(T, dtype=np.float32)[:, None] / timescale[None, :]
    cos, sin = np.cos(angle).T, np.sin(angle).T
    cos_t = np.concatenate([cos, cos], 0)
    sin_t = np.concatenate([-sin, sin], 0)
    two = lambda a: np.ascontiguousarray(np.concatenate([a, a], 1), dtype=np.float32)
    return two(cos_t), two(sin_t)


def window_mask():
    p, j = np.arange(W)[:, None], np.arange(2 * W)[None, :]
    return np.where((j >= p) & (j <= p + W), np.float32(0), np.float32(MASKED)).astype(np.float32)


def decoder_layer(nc, x, ctx_in, wq, wk, wv, wo, xwq, xbq, xwk, xbk, sw1, sb1, sw2, sb2,
                  rw1, rb1, rw2, rb2, cent, gbias, cos_c, sin_c, mask_c, ident_c, out, gates_d):
    es = ExitStack()
    with es:
        def sb(name, shape, dt=F32, where=es):
            return where.enter_context(nc.sbuf_tensor(name, shape, dt))

        def sem(name):
            return es.enter_context(nc.semaphore(name))

        bank = [es.enter_context(nc.psum_tensor(f"bank{i}", [P, HALF], F32)) for i in range(8)]
        proj_bank, score_bank, prob_bank = bank[0:2], bank[2:4], bank[4:6]
        pv_bank, attn_bank = bank[6], bank[7]

        ident = sb("ident", [P, P])
        res = sb("res", [P, NT, C])
        ln_stats = sb("ln_stats", [P, NT, 6])
        ln_mv = sb("ln_mv", [P, NT, 2])
        ln_var = sb("ln_var", [P, NT])
        ln_std = sb("ln_std", [P, NT])
        ln_rstd = sb("ln_rstd", [P, NT])

        att = ExitStack()
        stage = sb("stage", [P, 4, 1024], F32, att)
        wq_hi = sb("wq_hi", [P, KC, H * D], F32R, att)
        wq_lo = sb("wq_lo", [P, KC, H * D], F32R, att)
        wk_hi = sb("wk_hi", [P, KC, HK * D], F32R, att)
        wk_lo = sb("wk_lo", [P, KC, HK * D], F32R, att)
        wv_hi = sb("wv_hi", [P, KC, HK * D], F32R, att)
        wv_lo = sb("wv_lo", [P, KC, HK * D], F32R, att)
        wo_hi = sb("wo_hi", [P, H, C], F32R, att)
        wo_lo = sb("wo_lo", [P, H, C], F32R, att)
        cos_t = sb("cos_t", [P, HALF], F32, att)
        sin_t = sb("sin_t", [P, HALF], F32, att)
        mask = sb("mask", [P, 2 * W], F32, att)
        xb = sb("xb", [P, TT, C], F32, att)
        xT_hi = sb("xT_hi", [P, KC, T], F32R, att)
        xT_lo = sb("xT_lo", [P, KC, T], F32R, att)
        keyT = sb("keyT", [P, HK, T], F32, att)
        queryT = sb("queryT", [P, 4, 2, T], F32, att)
        v_hi = sb("v_hi", [P, TT, HK * D], F32R, att)
        v_lo = sb("v_lo", [P, TT, HK * D], F32R, att)
        swapped = sb("swapped", [P, 2, HALF], F32, att)
        by_cos = sb("by_cos", [P, 2, HALF], F32, att)
        by_sin = sb("by_sin", [P, 2, HALF], F32, att)
        scores = sb("scores", [P, 2, 3 * W], F32, att)
        top = sb("top", [P, 2, 2], F32, att)
        ntop = sb("ntop", [P, 2, 2], F32, att)
        probs = sb("probs", [P, 2, 3 * W], F32, att)
        psums = sb("psums", [P, 2, 2], F32, att)
        rsums = sb("rsums", [P, 2, 2], F32, att)
        nprobs = sb("nprobs", [P, 2, 3 * W], F32, att)
        pT_hi = sb("pT_hi", [P, 2, 3, G, W], F32R, att)
        pT_lo = sb("pT_lo", [P, 2, 3, G, W], F32R, att)
        oT_hi = sb("oT_hi", [P, 2, HALF], F32R, att)
        oT_lo = sb("oT_lo", [P, 2, HALF], F32R, att)
        att.close()

        w1_raw = sb("w1_raw", [P, KC, F])
        w2_raw = sb("w2_raw", [P, NC, C])
        assert KC * F + NC * C <= 4096 + 2 * KC * (H + 2 * HK) * D
        ctx_sb = sb("ctx_sb", [P, NT, CX])
        xw = sb("xw", [P, 2, CX])
        xb_cols = sb("xb_cols", [P, 2])
        ctxT = sb("ctxT", [P, N])
        xwT = sb("xwT", [P, 2, D])
        xqT = sb("xqT", [P, N])
        xkT = sb("xkT", [P, N])
        e_ntop = sb("e_ntop", [P, B, 2])
        e_exp = sb("e_exp", [P, B, 2, T])
        e_sum = sb("e_sum", [P, B, 2])
        e_rsum = sb("e_rsum", [P, B, 2])
        attT = sb("attT", [P, B, KC, T])
        x1 = sb("x1", [P, NT, C])
        x1T = sb("x1T", [P, B, KC, T])
        x2 = sb("x2", [P, NT, C])
        x2T = sb("x2T", [P, KC, N])
        x2T_hi = sb("x2T_hi", [P, KC, N], F32R)
        x2T_lo = sb("x2T_lo", [P, KC, N], F32R)
        cent_sb = sb("cent_sb", [NR, C])
        centT = sb("centT", [P, KC, NR])
        gbias_sb = sb("gbias_sb", [P, NR])
        sig = sb("sig", [P, NT, NR])
        SC = NR + 4
        choice = sb("choice", [P, NT, SC])
        taken = sb("taken", [P, NT, SC])
        best = sb("best", [P, NT, 8])
        chosen = sb("chosen", [P, NT, NR])
        gate_sum = sb("gate_sum", [P, NT])
        gate_rsum = sb("gate_rsum", [P, NT])
        gates = sb("gates", [P, NT, NR])
        gatesT = sb("gatesT", [NR + NS, N])
        b2_rows = sb("b2_rows", [NR + NS, C])
        b1_rows = sb("b1_rows", [NC, P])
        b1_cols = sb("b1_cols", [P, NC])
        w1_hi = sb("w1_hi", [P, 2, KC, P], F32R)
        w1_lo = sb("w1_lo", [P, 2, KC, P], F32R)
        w2_hi = sb("w2_hi", [P, 2, C], F32R)
        w2_lo = sb("w2_lo", [P, 2, C], F32R)
        gate_rows = sb("gate_rows", [P, 2, N])
        hid = sb("hid", [P, 2, N])
        hid_hi = sb("hid_hi", [P, 2, N], F32R)
        hid_lo = sb("hid_lo", [P, 2, N], F32R)
        yT = sb("yT", [P, KC, N])
        x3 = sb("x3", [P, NT, C])

        ld_ident, ld_tables, ld_res = sem("ld_ident"), sem("ld_tables"), sem("ld_res")
        ld_xb = sem("ld_xb")
        ld_stage = [sem(f"ld_stage{i}") for i in range(4)]
        w_hi, w_lo = sem("w_hi"), sem("w_lo")
        projected, emptied = sem("projected"), sem("emptied")
        swap_done, rope_mul, rope_add = sem("swap_done"), sem("rope_mul"), sem("rope_add")
        split_hi = sem("split_hi")
        scored, score_read, top_done = sem("scored"), sem("score_read"), sem("top_done")
        exp_done, rsum_done, norm_done = sem("exp_done"), sem("rsum_done"), sem("norm_done")
        turned, pT_hi_done, pT_done = sem("turned"), sem("pT_hi_done"), sem("pT_done")
        pv_done, oT_hi_done, oT_done = sem("pv_done"), sem("oT_hi_done"), sem("oT_done")
        attn_done, res_done = sem("attn_done"), sem("res_done")
        ld_ctx, ld_w1, ld_w2, ld_small = sem("ld_ctx"), sem("ld_w1"), sem("ld_w2"), sem("ld_small")
        pe, act, dve = sem("pe_step"), sem("act_step"), sem("dve_step")
        ln_a = sem("ln_a")
        gates_out, ld_gates = sem("gates_out"), [sem("ld_gates0"), sem("ld_gates1")]
        w1_hi_done, w1_done = sem("w1_hi_done"), sem("w1_done")
        w2_hi_done, w2_done = sem("w2_hi_done"), sem("w2_done")
        z_done, relu_done, gated, hid_hi_done, hid_done = (
            sem("z_done"), sem("relu_done"), sem("gated"), sem("hid_hi_done"), sem("hid_done"))
        y_done = sem("y_done")
        stored = sem("stored")
        dve_passed, pool_passed, act_passed = sem("dve_passed"), sem("pool_passed"), sem("act_passed")

        x_tiles = x.rearrange("b (t p) c -> p (b t) c", p=P)
        wq_v = wq.rearrange("(k p) n -> p k n", p=P)
        wk_v = wk.rearrange("(k p) n -> p k n", p=P)
        wv_v = wv.rearrange("(k p) n -> p k n", p=P)
        wo_v = wo.rearrange("(h p) n -> p h n", p=P)
        ctx_v = ctx_in.rearrange("b (t p) c -> p (b t) c", p=P)
        out_v = out.rearrange("b (t p) c -> p (b t) c", p=P)

        def heads4(t, j):
            return t[:, :, j * HALF:(j + 1) * HALF]
        PIECES = [(wk_v, wk_hi[:], wk_lo[:], KC), (wv_v, wv_hi[:], wv_lo[:], KC)]
        PIECES += [(heads4(wq_v, j), heads4(wq_hi, j), heads4(wq_lo, j), KC) for j in range(4)]
        PIECES += [(wo_v[:, 4 * j:4 * j + 4, :], wo_hi[:, 4 * j:4 * j + 4, :],
                    wo_lo[:, 4 * j:4 * j + 4, :], 4) for j in range(4)]
        K_PIECE, V_PIECE, Q_PIECE, O_PIECE = 0, 1, 2, 6

        def stage_view(n):
            return stage[:, n % 4, :].rearrange("p (k n) -> p k n", k=PIECES[n][3])

        block = es.enter_context(nc.Block())

        @block.sync
        def _(sp):
            sp.dma_start(ident[:], ident_c).then_inc(ld_ident, 16)
            sp.dma_start(xb[:], x[0].rearrange("(t p) c -> p t c", p=P)).then_inc(ld_xb, 16)
            for n in range(4):
                sp.dma_start(stage_view(n), PIECES[n][0]).then_inc(ld_stage[n % 4], 16)
                if n == 0:
                    sp.dma_start(cos_t[:], cos_c).then_inc(ld_tables, 16)
                    sp.dma_start(sin_t[:], sin_c).then_inc(ld_tables, 16)
                    sp.dma_start(mask[:], mask_c).then_inc(ld_tables, 16)
            for n in range(4, len(PIECES)):
                sp.wait_ge(w_lo, n - 3)
                sp.dma_start(stage_view(n), PIECES[n][0]).then_inc(ld_stage[n % 4], 16)
            sp.dma_start(res[:], x_tiles).then_inc(ld_res, 16)
            with sp.Fori(0, B - 1) as b:
                sp.wait_ge(projected, slot_count(b, "x1"))
                sp.dma_start(xb[:], x[bass.ds(b + 1, 1)].rearrange("a (t p) c -> p (a t) c", p=P)).then_inc(ld_xb, 16)

            sp.wait_ge(projected, slot_count(B - 1, "q7"))
            s1 = sw1.rearrange("e (k p) f -> p k e f", p=P)
            r1 = rw1.rearrange("e (k p) f -> p k e f", p=P)
            w1_v = w1_raw[:].rearrange("p k (e f) -> p k e f", f=FF)
            for k in range(KC):
                sp.dma_start(w1_v[:, k, 0:NS], s1[:, k]).then_inc(ld_w1, 16)
                sp.dma_start(w1_v[:, k, NS:NE], r1[:, k]).then_inc(ld_w1, 16)
            s2 = sw2.rearrange("e f c -> (e f) c")
            r2 = rw2.rearrange("e f c -> (e f) c")
            SF = NS * FF
            full, part = SF // P, SF % P
            first = P - part
            mid = NC - 1 - (full + 1)
            sp.dma_start(w2_raw[:, 0:full, :], s2[0:full * P].rearrange("(n p) c -> p n c", p=P)).then_inc(ld_w2, 16)
            sp.dma_start(w2_raw[0:part, full, :], s2[full * P:SF]).then_inc(ld_w2, 16)
            sp.dma_start(w2_raw[part:P, full, :], r2[0:first]).then_inc(ld_w2, 16)
            sp.dma_start(w2_raw[:, full + 1:NC - 1, :],
                         r2[first:first + mid * P].rearrange("(n p) c -> p n c", p=P)).then_inc(ld_w2, 16)
            sp.dma_start(w2_raw[0:LAST, NC - 1, :], r2[first + mid * P:NR * FF]).then_inc(ld_w2, 16)
            sp.wait_ge(res_done, B + 1)
            sp.dma_start(ctx_sb[:], ctx_v).then_inc(ld_ctx, 16)
            sp.dma_start(xw[:, 0, :], xwq).then_inc(ld_ctx, 16)
            sp.dma_start(xw[:, 1, :], xwk).then_inc(ld_ctx, 16)
            sp.dma_start(xb_cols[:, 0:1], xbq.rearrange("(d a) -> d a", a=1)).then_inc(ld_ctx, 16)
            sp.dma_start(xb_cols[:, 1:2], xbk.rearrange("(d a) -> d a", a=1)).then_inc(ld_ctx, 16)
            sp.dma_start(cent_sb[:], cent).then_inc(ld_small, 16)
            sp.dma_start(gbias_sb[:], gbias.rearrange("(a n) -> a n", a=1).broadcast_to((P, NR))).then_inc(ld_small, 16)
            sp.dma_start(b2_rows[0:NR, :], rb2).then_inc(ld_small, 16)
            sp.dma_start(b2_rows[NR:NR + NS, :], sb2).then_inc(ld_small, 16)
            sp.wait_ge(dve, place("dve", "b1 cleared"))
            s_b, r_b = sb1.rearrange("e f -> (e f)"), rb1.rearrange("e f -> (e f)")
            row = lambda a: a.rearrange("(n p) -> n p", n=1)
            sp.dma_start(b1_rows[0:full, :], s_b[0:full * P].rearrange("(n p) -> n p", p=P)).then_inc(ld_small, 16)
            sp.dma_start(b1_rows[full:full + 1, 0:part], row(s_b[full * P:SF])).then_inc(ld_small, 16)
            sp.dma_start(b1_rows[full:full + 1, part:P], row(r_b[0:first])).then_inc(ld_small, 16)
            sp.dma_start(b1_rows[full + 1:NC - 1, :],
                         r_b[first:first + mid * P].rearrange("(n p) -> n p", p=P)).then_inc(ld_small, 16)
            sp.dma_start(b1_rows[NC - 1:NC, 0:LAST], row(r_b[first + mid * P:NR * FF])).then_inc(ld_small, 16)

            sp.wait_ge(dve, place("dve", "gatesT"))
            rows = FF // GB
            spread = lambda a, n: a.rearrange("e (r t) -> e r t", r=1).broadcast_to((n, rows, N))
            sp.dma_start(gates_d[0:NS * rows].rearrange("(e r) t -> e r t", r=rows),
                         spread(gatesT[NR:NR + NS, :], NS)).then_inc(gates_out, 16)
            sp.dma_start(gates_d[NS * rows:NE * rows].rearrange("(e r) t -> e r t", r=rows),
                         spread(gatesT[0:NR, :], NR)).then_inc(gates_out, 16)
            sp.wait_ge(gates_out, 32)

            def load_gates(c, par, n=P):
                src = gates_d[bass.ds(c * (P // GB), n // GB), :]
                src = src.rearrange("e (r t) -> e r t", r=1).broadcast_to((n // GB, GB, N))
                sp.dma_start(gate_rows[0:n, par, :], src).then_inc(ld_gates[par], 16)

            load_gates(0, 0)
            load_gates(1, 1)
            with sp.Fori(0, (NC - 3) // 2) as cc:
                for par in range(2):
                    sp.wait_ge(gated, 2 * (2 * cc + par + 1))
                    load_gates(2 * cc + par + 2, par)
            sp.wait_ge(gated, 2 * (NC - 2))
            load_gates(NC - 1, (NC - 1) % 2, LAST)

            for t in range(NT):
                sp.wait_ge(dve, place("dve", f"x3 {t}"))
                sp.dma_start(out_v[:, t, :], x3[:, t, :]).then_inc(stored, 16)
            sp.wait_ge(stored, 16 * NT)

        @block.tensor
        def _(e):
            def three(o, sh, sl, mh, ml, first, last, **kw):
                nc.tensor.matmul(o, sh, mh, start=first, stop=False, **kw)
                nc.tensor.matmul(o, sh, ml, start=False, stop=False, **kw)
                return nc.tensor.matmul(o, sl, mh, start=False, stop=last, **kw)

            def slot(b, s):
                n, kind, j = SLOTS.index(s), s[0], int(s[1])
                o = proj_bank[n % 2]
                if not (isinstance(b, int) and b == 0 and n < 2):
                    e.wait_ge(emptied, slot_count(b, s) - 2)
                if kind == "x":
                    e.wait_ge(ld_xb, 16 * (b + 1))
                    for t in range(TT):
                        mm = nc.tensor.transpose(o[:, t * P:(t + 1) * P], xb[:, t, j * P:(j + 1) * P], ident[:])
                elif kind == "v":
                    e.wait_ge(w_lo, V_PIECE + 1)
                    for k in range(KC):
                        tok = slice(j * P, (j + 1) * P)
                        mm = three(o[:], xT_hi[:, k, tok], xT_lo[:, k, tok], wv_hi[:, k, :], wv_lo[:, k, :],
                                   k == 0, k == KC - 1)
                else:
                    wh, wl = (wk_hi, wk_lo) if kind == "k" else (wq_hi, wq_lo)
                    e.wait_ge(w_lo, K_PIECE + 1 if kind == "k" else Q_PIECE + j // 2 + 1)
                    e.wait_ge(emptied, slot_count(b, "x1"))
                    for a in range(2):
                        for k in range(KC):
                            f = slice((2 * j + a) * D, (2 * j + a + 1) * D)
                            mm = three(o[:, a * T:(a + 1) * T], wh[:, k, f], wl[:, k, f],
                                       xT_hi[:, k, :], xT_lo[:, k, :], k == 0, k == KC - 1)
                mm.then_inc(projected, 1)

            def score(b, h):
                s = h // 2
                e.wait_ge(rope_add, rope_count(b, f"q{s}"))
                e.wait_ge(score_read, head_count(b, h - 2))
                q = queryT[:, s % 4, h % 2, :]
                o = score_bank[h % 2]
                nc.tensor.matmul(o[:, 0:W], q[:, 0:W], keyT[:, h // G, 0:W], start=True, stop=True)
                nc.tensor.matmul(o[:, W:3 * W], q[:, W:2 * W], keyT[:, h // G, :],
                                 start=True, stop=True).then_inc(scored, 1)

            def turn(b, h):
                e.wait_ge(norm_done, head_count(b, h))
                e.wait_ge(pT_done, head_count(b, h - 2))
                for k in range(3):
                    mm = nc.tensor.transpose(prob_bank[h % 2][:, k * W:(k + 1) * W],
                                             nprobs[:, h % 2, k * W:(k + 1) * W], ident[:])
                mm.then_inc(turned, 1)

            def values(b, g, blk):
                if blk == 0:
                    e.wait_ge(pT_done, head_count(b, G * g + G - 1))
                    e.wait_ge(emptied, slot_count(b, "v1"))
                e.wait_ge(oT_done, pv_count(b, g, blk) - 1)
                f = slice(g * D, (g + 1) * D)
                kinds = [0] if blk == 0 else [1, 2]
                for kind in kinds:
                    t = 0 if kind < 2 else 1
                    mm = three(pv_bank[:], v_hi[:, t, f], v_lo[:, t, f],
                               pT_hi[:, g % 2, kind, :, :].rearrange("p a q -> p (a q)"),
                               pT_lo[:, g % 2, kind, :, :].rearrange("p a q -> p (a q)"),
                               kind == kinds[0], kind == kinds[-1])
                mm.then_inc(pv_done, 1)

            def project_out(b, g, blk):
                if g == 0 and blk == 0:
                    e.wait_ge(res_done, b + 1)
                e.wait_ge(w_lo, O_PIECE + g + 1)
                e.wait_ge(oT_done, pv_count(b, g, blk))
                for a in range(G):
                    q = slice(a * W, (a + 1) * W)
                    mm = three(attn_bank[:, blk * C:(blk + 1) * C], oT_hi[:, blk, q], oT_lo[:, blk, q],
                               wo_hi[:, G * g + a, :], wo_lo[:, G * g + a, :],
                               g == 0 and blk == 0 and a == 0, g == HK - 1 and a == G - 1,
                               skip_group_check=True)
                if g == HK - 1 and blk == 1:
                    mm.then_inc(attn_done, 1)

            def batch(b, more):
                for i in range(STEPS):
                    if i < H:
                        score(b, i)
                    for s in STEP_SLOTS.get(i, []):
                        slot(b, s)
                    if more:
                        for s in NEXT_SLOTS.get(i, []):
                            slot(b + 1, s)
                    if 2 <= i < H + 2:
                        turn(b, i - 2)
                    for blk in range(2):
                        if (g := due(i, 6 + blk)) is not None:
                            values(b, g, blk)
                    for blk in range(2):
                        if (g := due(i, 8 + blk)) is not None:
                            project_out(b, g, blk)

            e.wait_ge(ld_ident, 16)
            for s in SLOTS[:8]:
                slot(0, s)
            with e.Fori(0, B - 1) as b:
                batch(b, True)
            batch(B - 1, False)

            n = [0]

            def step(mm, name):
                assert ORDER["pe"][n[0]] == name, (ORDER["pe"][n[0]], name)
                n[0] += 1
                mm.then_inc(pe, 1)

            def after(engine, name):
                e.wait_ge({'act': act, 'dve': dve}[engine], place(engine, name))

            e.wait_ge(ld_ctx, 16 * 5)
            e.wait_ge(res_done, B + 1)
            for h in range(2):
                for t in range(4):
                    mm = nc.tensor.transpose(bank[2 + h][:, t * P:(t + 1) * P], ctx_sb[:, 4 * h + t, :], ident[:])
                step(mm, f"ctxT {h}")
            for a in range(2):
                mm = nc.tensor.transpose(bank[0][:, a * D:(a + 1) * D], xw[:, a, :], ident[:])
            step(mm, "xwT")
            after("act", "ctxT 0"), after("act", "xwT"), after("dve", "ctxT 1")
            for a in range(2):
                for h in range(2):
                    o = bank[[0, 1, 4, 5][2 * a + h]]
                    mm = nc.tensor.matmul(o[:], xwT[:, a, :], ctxT[:, h * HALF:(h + 1) * HALF], start=True, stop=True)
                    step(mm, f"xp {a} {h}")
            after("act", "xqT 1"), after("dve", "xkT 1")
            E_BANK = [2, 3, 0, 1]
            for b in range(B):
                for t in range(TT):
                    r = slice(b * T + t * P, b * T + (t + 1) * P)
                    mm = nc.tensor.matmul(bank[E_BANK[b]][:, t * T:(t + 1) * T], xqT[:, r],
                                          xkT[:, b * T:(b + 1) * T], start=True, stop=True)
                step(mm, f"energy {b}")
            for b in range(B):
                after("dve", f"e_norm {b}")
                o = bank[[4, 5, 6, 7][b]]
                for k in range(KC):
                    for t in range(TT):
                        mm = nc.tensor.transpose(o[:, k * T + t * P:k * T + (t + 1) * P],
                                                 e_exp[:, b, t, k * P:(k + 1) * P], ident[:])
                step(mm, f"attT {b}")
            for b in range(B):
                after("dve", f"x1 {2 * b + 1}")
                for k in range(KC):
                    for t in range(TT):
                        mm = nc.tensor.transpose(bank[b][:, k * T + t * P:k * T + (t + 1) * P],
                                                 x1[:, TT * b + t, k * P:(k + 1) * P], ident[:])
                step(mm, f"x1T {b}")
            for b in range(B):
                after("act", f"x1T {b}"), after("act", f"attT {b}")
                for t in range(TT):
                    for k in range(KC):
                        mm = nc.tensor.matmul(bank[4 + b][:, t * T:(t + 1) * T], x1T[:, b, k, t * P:(t + 1) * P],
                                              attT[:, b, k, :], start=k == 0, stop=k == KC - 1)
                step(mm, f"xm {b}")
            e.wait_ge(ld_small, 16 * 9)
            after("dve", "gates ready")
            for k in range(KC):
                nc.tensor.transpose(bank[0][:, k * NR:(k + 1) * NR],
                                    cent_sb[:, k * P:(k + 1) * P], ident[0:NR, 0:NR])
            mm = nc.tensor.transpose(bank[0][:, 64:64 + NC], b1_rows[:], ident[0:NC, 0:NC])
            step(mm, "smallT")
            after("act", "smallT")
            for b in range(B):
                after("dve", f"x2 {2 * b + 1}")
                for k in range(KC):
                    for t in range(TT):
                        mm = nc.tensor.transpose(bank[b][:, k * T + t * P:k * T + (t + 1) * P],
                                                 x2[:, TT * b + t, k * P:(k + 1) * P], ident[:])
                step(mm, f"x2T {b}")
            for b in range(B):
                after("act", f"x2T {b}")
            for t in range(NT):
                for k in range(KC):
                    mm = nc.tensor.matmul(bank[4][:, t * NR:(t + 1) * NR], x2T[:, k, t * P:(t + 1) * P],
                                          centT[:, k, :], start=k == 0, stop=k == KC - 1)
            step(mm, "router")
            after("dve", "gates")
            for t in range(NT):
                mm = nc.tensor.transpose(bank[5 + t // 4][0:NR, (t % 4) * P:(t % 4 + 1) * P], gates[:, t, :], ident[:])
            step(mm, "gatesT")

            z_bank = [[bank[0], bank[1]], [bank[2], bank[3]]]
            y_bank = [[bank[4], bank[5]], [bank[6], bank[7]]]

            def hidden(c, par, n=P):
                e.wait_ge(w1_done, c + 1)
                for h in range(2):
                    cols = slice(h * HALF, (h + 1) * HALF)
                    for k in range(KC):
                        mm = three(z_bank[par][h][0:n, :], w1_hi[:, par, k, 0:n], w1_lo[:, par, k, 0:n],
                                   x2T_hi[:, k, cols], x2T_lo[:, k, cols], k == 0, k == KC - 1)
                    mm.then_inc(z_done, 1)

            def output(c, par, n=P, last=False):
                e.wait_ge(w2_done, c + 1)
                for h in range(2):
                    e.wait_ge(hid_done, 2 * c + h + 1)
                    cols = slice(h * HALF, (h + 1) * HALF)
                    for d in range(KC):
                        f = slice(d * P, (d + 1) * P)
                        mm = three(y_bank[d][h][:], w2_hi[0:n, par, f], w2_lo[0:n, par, f],
                                   hid_hi[0:n, par, cols], hid_lo[0:n, par, cols], False, last,
                                   skip_group_check=True)
                mm.then_inc(y_done, 1)

            after("dve", "x2T_lo")
            hidden(0, 0)
            hidden(1, 1)
            after("dve", "gatesT")
            for d in range(KC):
                for h in range(2):
                    nc.tensor.matmul(y_bank[d][h][:], b2_rows[:, d * P:(d + 1) * P],
                                     gatesT[:, h * HALF:(h + 1) * HALF], start=True, stop=False,
                                     skip_group_check=True)
            with e.Fori(0, (NC - 3) // 2) as cc:
                for par in range(2):
                    output(2 * cc + par, par)
                    e.wait_ge(relu_done, 2 * (2 * cc + par + 1))
                    hidden(2 * cc + par + 2, par)
            output(NC - 3, (NC - 3) % 2)
            e.wait_ge(relu_done, 2 * (NC - 2))
            hidden(NC - 1, (NC - 1) % 2, LAST)
            output(NC - 2, (NC - 2) % 2)
            output(NC - 1, (NC - 1) % 2, LAST, last=True)
            for t in range(NT):
                if t == 0:
                    after("act", "yT 0"), after("dve", "yT 0")
                if t == 4:
                    after("act", "yT 1"), after("dve", "yT 1")
                for d in range(KC):
                    mm = nc.tensor.transpose(bank[t // 2][:, (t % 2) * C + d * P:(t % 2) * C + (d + 1) * P],
                                             yT[:, d, t * P:(t + 1) * P], ident[:])
                if t % 2:
                    step(mm, f"y {t // 2}")

        @block.scalar
        def _(e):
            def piece(n):
                e.wait_ge(ld_stage[n % 4], 16 * (n // 4 + 1))
                nc.scalar.copy(PIECES[n][1], stage_view(n)).then_inc(w_hi, 1)

            def slot(b, s):
                n, kind, j = SLOTS.index(s), s[0], int(s[1])
                o = proj_bank[n % 2]
                e.wait_ge(projected, slot_count(b, s))
                if kind == "x":
                    nc.scalar.copy(xT_hi[:, j, :], o[:, 0:T]).then_inc(split_hi, 1)
                elif kind == "v":
                    nc.scalar.copy(v_hi[:, j, :], o[:]).then_inc(split_hi, 1)
                else:
                    r = ROPES.index(s)
                    if not (isinstance(b, int) and b == 0 and r < 2):
                        e.wait_ge(rope_mul, rope_count(b, s) - 2)
                    half = D // 2
                    nc.scalar.copy(swapped[0:half, r % 2, :], o[half:D, :])
                    nc.scalar.copy(swapped[half:D, r % 2, :], o[0:half, :]).then_inc(swap_done, 1)

            def softmax_exp(b, h):
                u = h % 2
                e.wait_ge(top_done, head_count(b, h))
                e.wait_ge(norm_done, head_count(b, h - 2))
                nc.scalar.activation(probs[:, u, 0:W], scores[:, u, 0:W], ACT.Exp, bias=ntop[:, u, 0:1],
                                     scale=SCALE, accum_out=psums[:, u, 0:1])
                nc.scalar.activation(probs[:, u, W:3 * W], scores[:, u, W:3 * W], ACT.Exp, bias=ntop[:, u, 1:2],
                                     scale=SCALE, accum_out=psums[:, u, 1:2]).then_inc(exp_done, 1)

            def probs_hi(b, h):
                e.wait_ge(turned, head_count(b, h))
                nc.scalar.copy(pT_hi[:, (h // G) % 2, :, h % G, :],
                               prob_bank[h % 2][:, 0:3 * W].rearrange("p (k q) -> p k q", k=3)).then_inc(pT_hi_done, 1)

            def heads_hi(b, g, blk):
                e.wait_ge(pv_done, pv_count(b, g, blk))
                nc.scalar.copy(oT_hi[:, blk, :], pv_bank[:]).then_inc(oT_hi_done, 1)

            def batch(b, more):
                for i in range(STEPS):
                    if i < H:
                        softmax_exp(b, i)
                    for s in STEP_SLOTS.get(i, []):
                        slot(b, s)
                    if more:
                        for s in NEXT_SLOTS.get(i, []):
                            slot(b + 1, s)
                    if 2 <= i < H + 2:
                        probs_hi(b, i - 2)
                    for blk in range(2):
                        if (g := due(i, 6 + blk)) is not None:
                            heads_hi(b, g, blk)

            e.sem_inc(exp_done, AHEAD)
            e.sem_inc(pT_hi_done, AHEAD)
            e.sem_inc(oT_hi_done, 1)
            e.sem_inc(pv_done, 1)
            slot(0, "x0"), slot(0, "x1")
            piece(0)
            piece(1)
            piece(2)
            for s in SLOTS[2:8]:
                slot(0, s)
            for m in range(3, len(PIECES)):
                piece(m)
            with e.Fori(0, B - 1) as b:
                batch(b, True)
            batch(B - 1, False)

            n = [0]

            def step(ins, name):
                assert ORDER["act"][n[0]] == name, (ORDER["act"][n[0]], name)
                n[0] += 1
                ins.then_inc(act, 1)

            def after(name):
                e.wait_ge(pe, place("pe", name))

            def after_dve(name):
                e.wait_ge(dve, place("dve", name))

            after("ctxT 0")
            step(nc.scalar.copy(ctxT[:, 0:HALF], bank[2][:]), "ctxT 0")
            after("xwT")
            step(nc.scalar.copy(xwT[:].rearrange("p a d -> p (a d)"), bank[0][:, 0:2 * D]), "xwT")
            for h in range(2):
                after(f"xp 0 {h}")
                step(nc.scalar.activation(xqT[:, h * HALF:(h + 1) * HALF], bank[h][:], ACT.Identity,
                                          bias=xb_cols[:, 0:1]), f"xqT {h}")
            for b in range(B):
                after_dve(f"e_top {b}")
                for t in range(TT):
                    ins = nc.scalar.activation(e_exp[:, b, t, :], bank[[2, 3, 0, 1][b]][:, t * T:(t + 1) * T], ACT.Exp,
                                               bias=e_ntop[:, b, t:t + 1], accum_out=e_sum[:, b, t:t + 1])
                step(ins, f"e_exp {b}")
            for b in range(B):
                after(f"attT {b}")
                step(nc.scalar.copy(attT[:, b, :, :].rearrange("p k r -> p (k r)"), bank[4 + b][:]), f"attT {b}")
            after_dve("var 1")
            step(nc.scalar.activation(ln_std[:], ln_var[:], ACT.Sqrt), "std 1")
            for b in range(B):
                after(f"x1T {b}")
                step(nc.scalar.copy(x1T[:, b, :, :].rearrange("p k r -> p (k r)"), bank[b][:]), f"x1T {b}")
            after("smallT")
            nc.scalar.copy(centT[:].rearrange("p k r -> p (k r)"), bank[0][:, 0:KC * NR])
            step(nc.scalar.copy(b1_cols[:], bank[0][:, 64:64 + NC]), "smallT")
            after_dve("var 2")
            step(nc.scalar.activation(ln_std[:], ln_var[:], ACT.Sqrt), "std 2")
            for b in range(B):
                after(f"x2T {b}")
                step(nc.scalar.copy(x2T[:, :, b * T:(b + 1) * T], bank[b][:].rearrange("p (k t) -> p k t", k=KC)), f"x2T {b}")
            after("router")
            step(nc.scalar.activation(sig[:].rearrange("p t r -> p (t r)"), bank[4][:, 0:NT * NR], ACT.Sigmoid), "sig")

            def split_w1(c, par, n=P):
                nc.scalar.copy(w1_hi[:, par, :, 0:n], w1_raw[:, :, bass.ds(c * P, n)]).then_inc(w1_hi_done, 1)

            def split_w2(c, par, n=P):
                nc.scalar.copy(w2_hi[0:n, par, :], w2_raw[0:n, bass.ds(c, 1), :].rearrange("p a c -> p (a c)")).then_inc(w2_hi_done, 1)

            def relu(c, par, h, n=P):
                e.wait_ge(z_done, 2 * c + h + 1)
                e.sem_inc(act_passed, 1)
                nc.scalar.activation(hid[0:n, par, h * HALF:(h + 1) * HALF], bank[2 * par + h][0:n, :], ACT.Relu,
                                     bias=b1_cols[0:n, bass.ds(c, 1)]).then_inc(relu_done, 1)

            def hid_high(c, par, h, n=P):
                e.wait_ge(gated, 2 * c + h + 1)
                cols = slice(h * HALF, (h + 1) * HALF)
                nc.scalar.copy(hid_hi[0:n, par, cols], hid[0:n, par, cols]).then_inc(hid_hi_done, 1)

            def high_parts(c, par, nxt=None, n=P, n_next=P):
                relu(c, par, 0, n), relu(c, par, 1, n)
                if nxt is not None:
                    split_w1(nxt, 1 - par, n_next)
                hid_high(c, par, 0, n), hid_high(c, par, 1, n)
                if nxt is not None:
                    e.wait_ge(y_done, nxt - 1)
                    split_w2(nxt, 1 - par, n_next)

            e.wait_ge(ld_w1, 16 * 4)
            e.wait_ge(ld_w2, 16 * 5)
            split_w1(0, 0), split_w1(1, 1)
            split_w2(0, 0), split_w2(1, 1)
            high_parts(0, 0)
            with e.Fori(0, (NC - 3) // 2) as cc:
                for par in range(2):
                    high_parts(2 * cc + par + 1, 1 - par, 2 * cc + par + 2)
            high_parts(NC - 2, 1, NC - 1, n_next=LAST)
            high_parts(NC - 1, 0, n=LAST)

            e.wait_ge(y_done, NC)
            for h in range(2):
                step(nc.scalar.copy(yT[:, 0, h * HALF:(h + 1) * HALF], bank[4 + h][:]), f"yT {h}")
            for q in range(2):
                after_dve(f"var 3 {q}")
                step(nc.scalar.activation(ln_std[:, 4 * q:4 * q + 4], ln_var[:, 4 * q:4 * q + 4], ACT.Sqrt), f"std 3 {q}")

        @block.vector
        def _(e):
            low = lambda o, full, hi: nc.vector.tensor_tensor(o, full, hi.bitcast(F32), ALU.subtract)

            def piece(n):
                e.wait_ge(w_hi, n + 1)
                low(PIECES[n][2], stage_view(n), PIECES[n][1]).then_inc(w_lo, 1)

            def slot(b, s):
                n, kind, j = SLOTS.index(s), s[0], int(s[1])
                o = proj_bank[n % 2]
                if kind in "xv":
                    e.wait_ge(split_hi, split_count(b, s))
                    if kind == "x":
                        low(xT_lo[:, j, :], o[:, 0:T], xT_hi[:, j, :]).then_inc(emptied, 1)
                    else:
                        low(v_lo[:, j, :], o[:], v_hi[:, j, :]).then_inc(emptied, 1)
                    return
                r = ROPES.index(s)
                e.wait_ge(swap_done, rope_count(b, s))
                if not (isinstance(b, int) and b == 0 and r < 2):
                    e.wait_ge(rope_add, rope_count(b, s) - 2)
                nc.vector.tensor_tensor(by_cos[:, r % 2, :], o[:], cos_t[:], ALU.mult).then_inc(emptied, 1)
                nc.vector.tensor_tensor(by_sin[:, r % 2, :], swapped[:, r % 2, :], sin_t[:], ALU.mult).then_inc(rope_mul, 1)

            def mask_and_top(b, h):
                u = h % 2
                e.wait_ge(scored, H * b + h + 1)
                e.wait_ge(exp_done, head_count(b, h - 2))
                e.sem_inc(dve_passed, 1)
                o = score_bank[u]
                nc.vector.tensor_tensor_reduce(scores[:, u, 0:W], o[:, 0:W], mask[:, W:2 * W], 1.0, NEVER,
                                               ALU.add, ALU.max, top[:, u, 0:1])
                nc.vector.tensor_tensor_reduce(scores[:, u, W:3 * W], o[:, W:3 * W], mask[:], 1.0, NEVER,
                                               ALU.add, ALU.max, top[:, u, 1:2]).then_inc(score_read, 1)
                e.wait_ge(score_read, head_count(b, h))
                nc.vector.tensor_scalar(ntop[:, u, :], top[:, u, :], -SCALE, None, ALU.mult).then_inc(top_done, 1)

            def recip(b, h):
                e.wait_ge(exp_done, head_count(b, h))
                nc.vector.reciprocal(rsums[:, h % 2, :], psums[:, h % 2, :]).then_inc(rsum_done, 1)

            def probs_lo(b, h):
                e.wait_ge(pT_hi_done, head_count(b, h))
                g = (h // G) % 2
                low(pT_lo[:, g, :, h % G, :], prob_bank[h % 2][:, 0:3 * W].rearrange("p (k q) -> p k q", k=3),
                    pT_hi[:, g, :, h % G, :]).then_inc(pT_done, 1)

            def heads_lo(b, g, blk):
                e.wait_ge(oT_hi_done, pv_count(b, g, blk))
                low(oT_lo[:, blk, :], pv_bank[:], oT_hi[:, blk, :]).then_inc(oT_done, 1)

            def residual(b):
                e.wait_ge(attn_done, b + 1)
                r = res[:, bass.ds(b * TT, TT), :]
                nc.vector.tensor_tensor(r, attn_bank[:].rearrange("p (t c) -> p t c", t=TT), r, ALU.add).then_inc(res_done, 1)

            def batch(b, more):
                for i in range(STEPS):
                    if i < H:
                        mask_and_top(b, i)
                    if 1 <= i < H + 1:
                        recip(b, i - 1)
                    for s in STEP_SLOTS.get(i, []):
                        slot(b, s)
                    if more:
                        for s in NEXT_SLOTS.get(i, []):
                            slot(b + 1, s)
                    if 2 <= i < H + 2:
                        probs_lo(b, i - 2)
                    for blk in range(2):
                        if (g := due(i, 6 + blk)) is not None:
                            heads_lo(b, g, blk)
                residual(b)

            for s in (score_read, top_done, rsum_done, pT_done):
                e.sem_inc(s, AHEAD)
            for s in (oT_done, res_done):
                e.sem_inc(s, 1)
            slot(0, "x0"), slot(0, "x1")
            piece(0)
            piece(1)
            piece(2)
            e.wait_ge(ld_tables, 48)
            for s in SLOTS[2:8]:
                slot(0, s)
            for m in range(3, len(PIECES)):
                piece(m)
            e.wait_ge(ld_res, 16)
            with e.Fori(0, B - 1) as b:
                batch(b, True)
            batch(B - 1, False)

            n = [0]

            def step(ins, name):
                assert ORDER["dve"][n[0]] == name, (ORDER["dve"][n[0]], name)
                n[0] += 1
                ins.then_inc(dve, 1)

            def after(name):
                e.wait_ge(pe, place("pe", name))

            def after_act(name):
                e.wait_ge(act, place("act", name))

            def settle():
                e.wait_ge(dve, n[0])

            def ln_sums(src, which, tiles, tag):
                for t in tiles:
                    step(nc.vector.bn_stats(ln_stats[:, t, :], src[:, t, :]), f"stats {which} {t}")
                settle()
                for t in tiles:
                    step(nc.vector.bn_aggr(ln_mv[:, t, :], ln_stats[:, t, :]), f"aggr {which} {t}")
                settle()
                a, z = tiles[0], tiles[-1] + 1
                step(nc.vector.tensor_scalar(ln_var[:, a:z], ln_mv[:, a:z, 1:2].rearrange("p t a -> p (t a)"),
                                             EPS, None, ALU.add), f"var {tag}")

            def ln_apply(dst, src, which, tiles, tag):
                after_act(f"std {tag}")
                a, z = tiles[0], tiles[-1] + 1
                step(nc.vector.reciprocal(ln_rstd[:, a:z], ln_std[:, a:z]), f"rstd {tag}")
                settle()
                for t in tiles:
                    step(nc.vector.tensor_scalar(dst[:, t, :], src[:, t, :], ln_mv[:, t, 0:1], ln_rstd[:, t:t + 1],
                                                 ALU.subtract, ALU.mult), f"x{which} {t}")

            e.wait_ge(res_done, B + 1)
            step(nc.vector.memset(b1_rows[:], 0.0), "b1 cleared")
            ln_sums(res, 1, range(NT), "1")
            after("ctxT 1")
            step(nc.vector.tensor_copy(ctxT[:, HALF:N], bank[3][:]), "ctxT 1")
            for h in range(2):
                after(f"xp 1 {h}")
                step(nc.vector.tensor_scalar(xkT[:, h * HALF:(h + 1) * HALF], bank[4 + h][:], xb_cols[:, 1:2], None,
                                             ALU.add), f"xkT {h}")
            for b in range(B):
                after(f"energy {b}")
                step(nc.vector.tensor_reduce(e_ntop[:, b, :], bank[[2, 3, 0, 1][b]][:].rearrange("p (t s) -> p t s", t=TT),
                                             AX.X, ALU.max, negate=True), f"e_top {b}")
            for b in range(B):
                after_act(f"e_exp {b}")
                step(nc.vector.reciprocal(e_rsum[:, b, :], e_sum[:, b, :]), f"e_rsum {b}")
                settle()
                for t in range(TT):
                    ins = nc.vector.tensor_scalar(e_exp[:, b, t, :], e_exp[:, b, t, :], e_rsum[:, b, t:t + 1], None, ALU.mult)
                step(ins, f"e_norm {b}")
            ln_apply(x1, res, 1, range(NT), "1")
            for b in range(B):
                after(f"xm {b}")
                tiles = slice(TT * b, TT * (b + 1))
                step(nc.vector.tensor_tensor(res[:, tiles, :], bank[4 + b][:].rearrange("p (t c) -> p t c", t=TT),
                                             x1[:, tiles, :], ALU.add), f"xres {b}")
            nc.vector.memset(choice[:, :, NR:SC], NEVER)
            step(nc.vector.memset(gatesT[:], 1.0), "gates ready")
            settle()
            ln_sums(res, 2, range(NT), "2")
            ln_apply(x2, res, 2, range(NT), "2")
            for b in range(B):
                after_act(f"x2T {b}")
            for h in range(2):
                step(nc.vector.tensor_copy(x2T_hi[:, :, h * HALF:(h + 1) * HALF], x2T[:, :, h * HALF:(h + 1) * HALF]), f"x2T_hi {h}")
            settle()
            step(low(x2T_lo[:], x2T[:], x2T_hi[:]), "x2T_lo")

            after_act("sig")
            e.wait_ge(ld_small, 16 * 9)
            step(nc.vector.tensor_tensor(choice[:, :, 0:NR], sig[:],
                                         gbias_sb[:].rearrange("p (a r) -> p a r", a=1).broadcast_to((P, NT, NR)), ALU.add), "choice")
            settle()
            for t in range(NT):
                ins = nc.vector.max(best[:, t, :], choice[:, t, 0:NR])
            step(ins, "best")
            settle()
            step(nc.vector.memset(best[:, :, KR:8], NEVER), "best four")
            settle()
            for t in range(NT):
                ins = nc.vector.match_replace(taken[:, t, :], best[:, t, :], choice[:, t, :], -NEVER)
            step(ins, "taken")
            settle()
            step(nc.vector.tensor_tensor(chosen[:], taken[:, :, 0:NR], choice[:, :, 0:NR], ALU.not_equal), "chosen")
            settle()
            step(nc.vector.tensor_tensor(gates[:], chosen[:], choice[:, :, 0:NR], ALU.mult), "open")
            settle()
            step(nc.vector.tensor_reduce(gate_sum[:], gates[:], AX.X, ALU.add), "gate sum")
            settle()
            step(nc.vector.tensor_scalar(gate_sum[:], gate_sum[:], 1e-8, None, ALU.max), "gate clip")
            settle()
            step(nc.vector.reciprocal(gate_rsum[:], gate_sum[:]), "gate rsum")
            settle()
            step(nc.vector.tensor_tensor(gates[:], gates[:], gate_rsum[:].rearrange("p (t a) -> p t a", a=1).broadcast_to((P, NT, NR)),
                                         ALU.mult), "gates")
            after("gatesT")
            for h in range(2):
                ins = nc.vector.tensor_copy(gatesT[0:NR, h * HALF:(h + 1) * HALF], bank[5 + h][0:NR, :])
            step(ins, "gatesT")

            def gate(c, par, h, n=P):
                e.wait_ge(relu_done, 2 * c + h + 1)
                if h == 0:
                    e.wait_ge(ld_gates[par], 8 * (c - par) + 16)
                cols = slice(h * HALF, (h + 1) * HALF)
                nc.vector.tensor_tensor(hid[0:n, par, cols], hid[0:n, par, cols], gate_rows[0:n, par, cols],
                                        ALU.mult).then_inc(gated, 1)

            def hid_low(c, par, h, n=P):
                e.wait_ge(hid_hi_done, 2 * c + h + 1)
                cols = slice(h * HALF, (h + 1) * HALF)
                low(hid_lo[0:n, par, cols], hid[0:n, par, cols], hid_hi[0:n, par, cols]).then_inc(hid_done, 1)

            def low_parts(c, par, n=P):
                gate(c, par, 0, n), gate(c, par, 1, n)
                hid_low(c, par, 0, n), hid_low(c, par, 1, n)

            low_parts(0, 0)
            with e.Fori(0, (NC - 3) // 2) as cc:
                for par in range(2):
                    low_parts(2 * cc + par + 1, 1 - par)
            low_parts(NC - 2, 1)
            low_parts(NC - 1, 0, LAST)

            e.wait_ge(y_done, NC)
            for h in range(2):
                step(nc.vector.tensor_copy(yT[:, 1, h * HALF:(h + 1) * HALF], bank[6 + h][:]), f"yT {h}")
            for q in range(2):
                tiles = range(4 * q, 4 * q + 4)
                for u in range(2 * q, 2 * q + 2):
                    after(f"y {u}")
                    pair = slice(2 * u, 2 * u + 2)
                    step(nc.vector.scalar_tensor_tensor(res[:, pair, :], x2[:, pair, :], 2.0,
                                                        bank[u][:].rearrange("p (t c) -> p t c", t=2),
                                                        ALU.mult, ALU.add), f"yres {u}")
                settle()
                ln_sums(res, 3, tiles, f"3 {q}")
            for q in range(2):
                ln_apply(x3, res, 3, range(4 * q, 4 * q + 4), f"3 {q}")

        @block.gpsimd
        def _(e):
            def slot(b, s):
                if s[0] not in "kq":
                    return
                r, j = ROPES.index(s), int(s[1])
                o = keyT[:, 2 * j:2 * j + 2, :] if s[0] == "k" else queryT[:, j % 4, :, :]
                e.wait_ge(rope_mul, rope_count(b, s))
                nc.gpsimd.tensor_tensor(o.rearrange("p a t -> p (a t)"), by_cos[:, r % 2, :], by_sin[:, r % 2, :],
                                        ALU.add).then_inc(rope_add, 1)

            def normalise(b, h):
                u = h % 2
                e.wait_ge(rsum_done, head_count(b, h))
                e.wait_ge(turned, head_count(b, h - 2))
                e.sem_inc(pool_passed, 1)
                nc.gpsimd.tensor_scalar(nprobs[:, u, 0:W], probs[:, u, 0:W], rsums[:, u, 0:1], 1.0, ALU.mult, ALU.mult)
                nc.gpsimd.tensor_scalar(nprobs[:, u, W:3 * W], probs[:, u, W:3 * W], rsums[:, u, 1:2], 1.0,
                                        ALU.mult, ALU.mult).then_inc(norm_done, 1)

            def batch(b, more):
                for i in range(STEPS):
                    if 1 <= i < H + 1:
                        normalise(b, i - 1)
                    for s in STEP_SLOTS.get(i, []):
                        slot(b, s)
                    if more:
                        for s in NEXT_SLOTS.get(i, []):
                            slot(b + 1, s)

            e.sem_inc(norm_done, AHEAD)
            e.sem_inc(turned, AHEAD)
            for s in SLOTS[2:8]:
                slot(0, s)
            with e.Fori(0, B - 1) as b:
                batch(b, True)
            batch(B - 1, False)

            def low_w1(c, par, n=P):
                e.wait_ge(w1_hi_done, c + 1)
                nc.gpsimd.tensor_tensor(w1_lo[:, par, :, 0:n], w1_raw[:, :, bass.ds(c * P, n)],
                                        w1_hi[:, par, :, 0:n].bitcast(F32), ALU.subtract).then_inc(w1_done, 1)

            def low_w2(c, par, n=P):
                e.wait_ge(w2_hi_done, c + 1)
                nc.gpsimd.tensor_tensor(w2_lo[0:n, par, :], w2_raw[0:n, bass.ds(c, 1), :].rearrange("p a c -> p (a c)"),
                                        w2_hi[0:n, par, :].bitcast(F32), ALU.subtract).then_inc(w2_done, 1)

            low_w1(0, 0), low_w1(1, 1)
            low_w2(0, 0), low_w2(1, 1)
            with e.Fori(0, (NC - 3) // 2) as cc:
                for par in range(2):
                    low_w1(2 * cc + par + 2, par)
                    low_w2(2 * cc + par + 2, par)
            low_w1(NC - 1, 0, LAST)
            low_w2(NC - 1, 0, LAST)


ORDER = {
    "pe": ["ctxT 0", "ctxT 1", "xwT"] + [f"xp {a} {h}" for a in range(2) for h in range(2)]
    + [f"{w} {b}" for w in ("energy", "attT", "x1T", "xm") for b in range(B)] + ["smallT"]
    + [f"x2T {b}" for b in range(B)] + ["router", "gatesT"] + [f"y {u}" for u in range(NT // 2)],
    "act": ["ctxT 0", "xwT", "xqT 0", "xqT 1"] + [f"e_exp {b}" for b in range(B)] + [f"attT {b}" for b in range(B)]
    + ["std 1"] + [f"x1T {b}" for b in range(B)] + ["smallT", "std 2"] + [f"x2T {b}" for b in range(B)]
    + ["sig", "yT 0", "yT 1", "std 3 0", "std 3 1"],
    "dve": ["b1 cleared"] + [f"{w} 1 {t}" for w in ("stats", "aggr") for t in range(NT)] + ["var 1", "ctxT 1", "xkT 0", "xkT 1"]
    + [f"e_top {b}" for b in range(B)] + [f"{w} {b}" for b in range(B) for w in ("e_rsum", "e_norm")]
    + ["rstd 1"] + [f"x1 {t}" for t in range(NT)] + [f"xres {b}" for b in range(B)] + ["gates ready"]
    + [f"{w} 2 {t}" for w in ("stats", "aggr") for t in range(NT)] + ["var 2", "rstd 2"] + [f"x2 {t}" for t in range(NT)]
    + ["x2T_hi 0", "x2T_hi 1", "x2T_lo", "choice", "best", "best four", "taken", "chosen", "open", "gate sum", "gate clip", "gate rsum",
       "gates", "gatesT", "yT 0", "yT 1"]
    + [n for q in range(2) for n in [f"yres {u}" for u in range(2 * q, 2 * q + 2)] + [f"{w} 3 {t}" for w in ("stats", "aggr") for t in range(4 * q, 4 * q + 4)] + [f"var 3 {q}"]]
    + [n for q in range(2) for n in [f"rstd 3 {q}"] + [f"x3 {t}" for t in range(4 * q, 4 * q + 4)]],
}

_INS = ["x", "ctx_1024", "L0_attn_q_kernel", "L0_attn_k_kernel", "L0_attn_v_kernel", "L0_attn_out_kernel",
        "L0_xattn_Wq", "L0_xattn_bq", "L0_xattn_Wk", "L0_xattn_bk", "L0_ffn_shared_w1", "L0_ffn_shared_b1",
        "L0_ffn_shared_w2", "L0_ffn_shared_b2", "L0_ffn_routed_w1", "L0_ffn_routed_b1", "L0_ffn_routed_w2",
        "L0_ffn_routed_b2", "L0_ffn_centroids", "L0_ffn_bias"]


def kernel(**inputs):
    import concourse.bacc as bacc
    from concourse.bass_utils import run_bass_kernel_spmd

    nc = bacc.Bacc("TRN2", target_bir_lowering=False, num_devices=1)
    cos_c, sin_c = rope_tables()
    consts = {"cos_c": cos_c, "sin_c": sin_c, "mask_c": window_mask(), "ident_c": np.eye(P, dtype=np.float32)}
    arrays, args = {}, []
    for name, a in [(n, inputs[n]) for n in _INS] + list(consts.items()):
        a = np.ascontiguousarray(a)
        arrays[f"in_{name}"] = a
        args.append(nc.dram_tensor(f"in_{name}", a.shape, mybir.dt.from_np(a.dtype), kind="ExternalInput").ap())
    out = nc.dram_tensor("out", (B, T, C), F32, kind="ExternalOutput").ap()
    gates_d = nc.dram_tensor("gates_d", (NE * FF // GB, N), F32, kind="Internal").ap()
    decoder_layer(nc, *args, out, gates_d)
    r = run_bass_kernel_spmd(nc, [arrays], core_ids=[0])
    return r.results[0]["out"]
```

```python
from contextlib import ExitStack

import numpy as np

import concourse.bass as bass
from concourse import mybir

F32 = mybir.dt.float32
F32R = mybir.dt.float32r
ALU = mybir.AluOpType
ACT = mybir.ActivationFunctionType
AX = mybir.AxisListType

P = 128
B, T, C = 4, 256, 256
KC = C // P
TT = T // P
NT = B * TT
H, HK, D = 16, 4, 128
G = H // HK
W = 128
SCALE = float(1.0 / np.sqrt(D))
MASKED = -1e30
CX = 128
NS, NR, KR, FF = 2, 16, 4, 176
NE = NS + NR
F = NE * FF
NC = -(-F // P)
LAST = F - (NC - 1) * P
GB = 16
EPS = 1e-5
THETA = 10000.0
N = B * T
HALF = 512
NEVER = -3e38

SLOT_AT = {"x0": -6, "x1": -6, "k0": -4, "q0": -3, "q1": -2.25, "q2": -1.5, "q3": 0.75, "q4": 2.25, "k1": 3.5,
           "q5": 4.25, "v0": 6, "v1": 6.75, "q6": 7.75, "q7": 8.5}
SLOTS = sorted(SLOT_AT, key=lambda s: SLOT_AT[s])
NSLOT = len(SLOTS)
ROPES = [s for s in SLOTS if s[0] in "kq"]
NROPE = len(ROPES)
SPLITS = [s for s in SLOTS if s[0] in "xv"]
NSPLIT = len(SPLITS)
WINDOW = -6
RING = 2
AHEAD = RING
WORK_AT = {
    "pe": {"slot": 0, "score": 0, "turn": 3.5, "values0": 8.25, "values1": 9.5, "out0": 10.5, "out1": 13},
    "act": {"slot": 0, "exp": 1, "probs_hi": 3, "heads_hi0": 7.75, "heads_hi1": 9},
    "dve": {"slot": 0, "top": -0.5, "recip": 1, "probs_lo": 3.25, "heads_lo0": 8, "heads_lo1": 9.25,
            "residual": 24.5},
    "pool": {"slot": 0, "normalise": 0.25},
}
PIECE_NAMES = ["k", "q0", "q1", "q2", "v", "q3", "o0", "o1", "o2", "o3"]
PIECE_AT = dict(zip(PIECE_NAMES, (-5.9, -5.0, -3.1, 0.5, 2.5, 5.0, 6.0, 7.0, 8.0, 9.0)))
ONCE_AT = {
    "pe": {"ctx turned": -5.5, "ctx projected": -3.5, "energy 0": -1.2, "energy 1": -1.1, "energy 2": -0.4,
           "energy 3": -0.3, "attT 0": 1.2, "attT 1": 1.4, "attT 2": 2.1, "attT 3": 2.3},
    "act": {"ctx turned": -4.9, "ctx projected": -3, "e_exp 0": -0.2, "e_exp 1": -0.1, "e_exp 2": 0.6,
            "e_exp 3": 0.7, "attT 0": 1.6, "attT 1": 1.8, "attT 2": 2.5, "attT 3": 2.8},
    "dve": {"ctx turned": -4.9, "ctx projected": -3, "e_top 0": -0.8, "e_top 1": -0.7, "e_top 2": -0.1,
            "e_top 3": 0.1, "e_norm 0": 0.8, "e_norm 1": 0.9, "e_norm 2": 1.5, "e_norm 3": 1.6},
    "pool": {},
}


def window_order(engine):
    events = []
    for work, lag in WORK_AT[engine].items():
        if work == "slot":
            events += [(SLOT_AT[s] + lag, work, s) for s in SLOTS if engine != "pool" or s in ROPES]
        elif work == "residual":
            events.append((lag, work, 0))
        elif work[-1] in "01":
            events += [(G * g + lag, work, g) for g in range(HK)]
        else:
            events += [(h + lag, work, h) for h in range(H)]
    turns = [(WINDOW + (at - WINDOW) % H, int((at - WINDOW) // H), work, of) for at, work, of in events]
    assert all(window in (0, 1) for _, window, _, _ in turns), engine
    turns += [(at, "once", name, 0) for name, at in ONCE_AT[engine].items()]
    if engine in ("act", "dve"):
        turns += [(at, "once", "piece", PIECE_NAMES.index(name)) for name, at in PIECE_AT.items()]
    return [(window, work, of) for _, window, work, of in sorted(turns, key=lambda e: e[0])]


def take_turn(engine, b, windows, doers):
    for window, work, of in window_order(engine):
        if window not in windows:
            continue
        if window == "once":
            doers["once"](work, of)
        else:
            doers[work](b - window, of)


def slot_count(b, s):
    return NSLOT * b + SLOTS.index(s) + 1


def rope_count(b, s):
    return NROPE * b + ROPES.index(s) + 1


def split_count(b, s):
    return NSPLIT * b + SPLITS.index(s) + 1


def head_count(b, h):
    return H * b + h + 1 + AHEAD


def place(engine, name):
    return ORDER[engine].index(name) + 1


def pv_count(b, g, blk):
    return 2 * HK * b + 2 * g + blk + 2


def rope_tables():
    fraction = np.arange(0, D, 2, dtype=np.float32) / np.float32(D)
    timescale = np.float32(THETA) ** fraction
    angle = np.arange(T, dtype=np.float32)[:, None] / timescale[None, :]
    cos, sin = np.cos(angle).T, np.sin(angle).T
    cos_t = np.concatenate([cos, cos], 0)
    sin_t = np.concatenate([-sin, sin], 0)
    two = lambda a: np.ascontiguousarray(np.concatenate([a, a], 1), dtype=np.float32)
    return two(cos_t), two(sin_t)


def window_mask():
    p, j = np.arange(W)[:, None], np.arange(2 * W)[None, :]
    return np.where((j >= p) & (j <= p + W), np.float32(0), np.float32(MASKED)).astype(np.float32)


def decoder_layer(nc, x, ctx_in, wq, wk, wv, wo, xwq, xbq, xwk, xbk, sw1, sb1, sw2, sb2,
                  rw1, rb1, rw2, rb2, cent, gbias, cos_c, sin_c, mask_c, ident_c, out, gates_d):
    es = ExitStack()
    with es:
        def sb(name, shape, dt=F32, where=es):
            return where.enter_context(nc.sbuf_tensor(name, shape, dt))

        def sem(name):
            return es.enter_context(nc.semaphore(name))

        bank = [es.enter_context(nc.psum_tensor(f"bank{i}", [P, HALF], F32)) for i in range(8)]
        proj_bank, score_bank, prob_bank = bank[0:2], bank[2:4], bank[4:6]
        pv_bank, attn_bank = bank[6], bank[7]

        ident = sb("ident", [P, P])
        res = sb("res", [P, NT, C])
        attT = sb("attT", [P, B, KC, T])
        ln_stats = sb("ln_stats", [P, NT, 6])
        ln_mv = sb("ln_mv", [P, NT, 2])
        ln_var = sb("ln_var", [P, NT])
        ln_std = sb("ln_std", [P, NT])
        ln_rstd = sb("ln_rstd", [P, NT])

        att = ExitStack()
        stage = sb("stage", [P, 4, 1024], F32, att)
        wq_hi = sb("wq_hi", [P, KC, H * D], F32R, att)
        wq_lo = sb("wq_lo", [P, KC, H * D], F32R, att)
        wk_hi = sb("wk_hi", [P, KC, HK * D], F32R, att)
        wk_lo = sb("wk_lo", [P, KC, HK * D], F32R, att)
        wv_hi = sb("wv_hi", [P, KC, HK * D], F32R, att)
        wv_lo = sb("wv_lo", [P, KC, HK * D], F32R, att)
        wo_hi = sb("wo_hi", [P, H, C], F32R, att)
        wo_lo = sb("wo_lo", [P, H, C], F32R, att)
        cos_t = sb("cos_t", [P, HALF], F32, att)
        sin_t = sb("sin_t", [P, HALF], F32, att)
        mask = sb("mask", [P, 2 * W], F32, att)
        xb = sb("xb", [P, TT, C], F32, att)
        xT_hi = sb("xT_hi", [P, KC, T], F32R, att)
        xT_lo = sb("xT_lo", [P, KC, T], F32R, att)
        keyT = sb("keyT", [P, HK, T], F32, att)
        queryT = sb("queryT", [P, 4, 2, T], F32, att)
        v_hi = sb("v_hi", [P, TT, HK * D], F32R, att)
        v_lo = sb("v_lo", [P, TT, HK * D], F32R, att)
        swapped = sb("swapped", [P, 2, HALF], F32, att)
        by_cos = sb("by_cos", [P, 2, HALF], F32, att)
        by_sin = sb("by_sin", [P, 2, HALF], F32, att)
        scores = sb("scores", [P, 2, 3 * W], F32, att)
        top = sb("top", [P, 2, 2], F32, att)
        ntop = sb("ntop", [P, 2, 2], F32, att)
        probs = sb("probs", [P, RING, 3 * W], F32, att)
        psums = sb("psums", [P, RING, 2], F32, att)
        rsums = sb("rsums", [P, RING, 2], F32, att)
        nprobs = sb("nprobs", [P, RING, 3 * W], F32, att)
        cross = ExitStack()
        ctx_sb = sb("ctx_sb", [P, NT, CX], F32, cross)
        xw = sb("xw", [P, 2, CX], F32, cross)
        xb_cols = sb("xb_cols", [P, 2], F32, cross)
        ctxT = sb("ctxT", [P, N], F32, cross)
        xwT = sb("xwT", [P, 2, D], F32, cross)
        xqT = sb("xqT", [P, N], F32, cross)
        xkT = sb("xkT", [P, N], F32, cross)
        e_ntop = sb("e_ntop", [P, B, 2], F32, cross)
        e_exp = sb("e_exp", [P, B, 2, T], F32, cross)
        e_sum = sb("e_sum", [P, B, 2], F32, cross)
        e_rsum = sb("e_rsum", [P, B, 2], F32, cross)
        cross.close()
        pT_hi = sb("pT_hi", [P, 2, 3, G, W], F32R, att)
        pT_lo = sb("pT_lo", [P, 2, 3, G, W], F32R, att)
        oT_hi = sb("oT_hi", [P, 2, HALF], F32R, att)
        oT_lo = sb("oT_lo", [P, 2, HALF], F32R, att)
        att.close()

        w1_raw = sb("w1_raw", [P, KC, F])
        w2_raw = sb("w2_raw", [P, NC, C])
        assert KC * F + NC * C <= 4096 + 2 * KC * (H + 2 * HK) * D
        x1 = sb("x1", [P, NT, C])
        x1T = sb("x1T", [P, B, KC, T])
        x2 = sb("x2", [P, NT, C])
        x2T = sb("x2T", [P, KC, N])
        x2T_hi = sb("x2T_hi", [P, KC, N], F32R)
        x2T_lo = sb("x2T_lo", [P, KC, N], F32R)
        cent_sb = sb("cent_sb", [NR, C])
        centT = sb("centT", [P, KC, NR])
        gbias_sb = sb("gbias_sb", [P, NR])
        sig = sb("sig", [P, NT, NR])
        SC = NR + 4
        choice = sb("choice", [P, NT, SC])
        taken = sb("taken", [P, NT, SC])
        best = sb("best", [P, NT, 8])
        chosen = sb("chosen", [P, NT, NR])
        gate_sum = sb("gate_sum", [P, NT])
        gate_rsum = sb("gate_rsum", [P, NT])
        gates = sb("gates", [P, NT, NR])
        gatesT = sb("gatesT", [NR + NS, N])
        b2_rows = sb("b2_rows", [NR + NS, C])
        b1_rows = sb("b1_rows", [NC, P])
        b1_cols = sb("b1_cols", [P, NC])
        w1_hi = sb("w1_hi", [P, 2, KC, P], F32R)
        w1_lo = sb("w1_lo", [P, 2, KC, P], F32R)
        w2_hi = sb("w2_hi", [P, 2, C], F32R)
        w2_lo = sb("w2_lo", [P, 2, C], F32R)
        gate_rows = sb("gate_rows", [P, 2, N])
        hid = sb("hid", [P, 2, N])
        hid_hi = sb("hid_hi", [P, 2, N], F32R)
        hid_lo = sb("hid_lo", [P, 2, N], F32R)
        yT = sb("yT", [P, KC, N])
        x3 = sb("x3", [P, NT, C])

        ld_ident, ld_tables, ld_res = sem("ld_ident"), sem("ld_tables"), sem("ld_res")
        ld_xb = sem("ld_xb")
        ld_stage = [sem(f"ld_stage{i}") for i in range(4)]
        w_hi, w_lo = sem("w_hi"), sem("w_lo")
        projected, emptied = sem("projected"), sem("emptied")
        swap_done, rope_mul, rope_add = sem("swap_done"), sem("rope_mul"), sem("rope_add")
        split_hi = sem("split_hi")
        scored, score_read, top_done = sem("scored"), sem("score_read"), sem("top_done")
        exp_done, rsum_done, norm_done = sem("exp_done"), sem("rsum_done"), sem("norm_done")
        turned, pT_hi_done, pT_done = sem("turned"), sem("pT_hi_done"), sem("pT_done")
        pv_done, oT_hi_done, oT_done = sem("pv_done"), sem("oT_hi_done"), sem("oT_done")
        attn_done, res_done = sem("attn_done"), sem("res_done")
        ld_ctx, ld_w1, ld_w2, ld_small = sem("ld_ctx"), sem("ld_w1"), sem("ld_w2"), sem("ld_small")
        pe, act, dve = sem("pe_step"), sem("act_step"), sem("dve_step")
        ln_a = sem("ln_a")
        gates_out, ld_gates = sem("gates_out"), [sem("ld_gates0"), sem("ld_gates1")]
        w1_hi_done, w1_done = sem("w1_hi_done"), sem("w1_done")
        w2_hi_done, w2_done = sem("w2_hi_done"), sem("w2_done")
        z_done, relu_done, gated, hid_hi_done, hid_done = (
            sem("z_done"), sem("relu_done"), sem("gated"), sem("hid_hi_done"), sem("hid_done"))
        y_done = sem("y_done")
        stored = sem("stored")
        dve_passed, pool_passed, act_passed = sem("dve_passed"), sem("pool_passed"), sem("act_passed")

        x_tiles = x.rearrange("b (t p) c -> p (b t) c", p=P)
        wq_v = wq.rearrange("(k p) n -> p k n", p=P)
        wk_v = wk.rearrange("(k p) n -> p k n", p=P)
        wv_v = wv.rearrange("(k p) n -> p k n", p=P)
        wo_v = wo.rearrange("(h p) n -> p h n", p=P)
        ctx_v = ctx_in.rearrange("b (t p) c -> p (b t) c", p=P)
        out_v = out.rearrange("b (t p) c -> p (b t) c", p=P)

        def heads4(t, j):
            return t[:, :, j * HALF:(j + 1) * HALF]
        by_name = {"k": (wk_v, wk_hi[:], wk_lo[:], KC), "v": (wv_v, wv_hi[:], wv_lo[:], KC)}
        for j in range(4):
            by_name[f"q{j}"] = (heads4(wq_v, j), heads4(wq_hi, j), heads4(wq_lo, j), KC)
            by_name[f"o{j}"] = (wo_v[:, 4 * j:4 * j + 4, :], wo_hi[:, 4 * j:4 * j + 4, :],
                                wo_lo[:, 4 * j:4 * j + 4, :], 4)
        PIECES = [by_name[name] for name in PIECE_NAMES]

        def piece_count(name):
            return PIECE_NAMES.index(name) + 1

        def stage_view(n):
            return stage[:, n % 4, :].rearrange("p (k n) -> p k n", k=PIECES[n][3])

        block = es.enter_context(nc.Block())

        @block.sync
        def _(sp):
            sp.dma_start(ident[:], ident_c).then_inc(ld_ident, 16)
            sp.dma_start(xb[:], x[0].rearrange("(t p) c -> p t c", p=P)).then_inc(ld_xb, 16)
            for n in range(4):
                sp.dma_start(stage_view(n), PIECES[n][0]).then_inc(ld_stage[n % 4], 16)
                if n == 0:
                    sp.dma_start(cos_t[:], cos_c).then_inc(ld_tables, 16)
                    sp.dma_start(sin_t[:], sin_c).then_inc(ld_tables, 16)
                    sp.dma_start(mask[:], mask_c).then_inc(ld_tables, 16)
                    sp.dma_start(xw[:, 0, :], xwq).then_inc(ld_ctx, 16)
                    sp.dma_start(xw[:, 1, :], xwk).then_inc(ld_ctx, 16)
                    sp.dma_start(xb_cols[:, 0:1], xbq.rearrange("(d a) -> d a", a=1)).then_inc(ld_ctx, 16)
                    sp.dma_start(xb_cols[:, 1:2], xbk.rearrange("(d a) -> d a", a=1)).then_inc(ld_ctx, 16)
                if n == 1:
                    sp.dma_start(ctx_sb[:], ctx_v).then_inc(ld_ctx, 16)
            for n in range(4, len(PIECES)):
                sp.wait_ge(w_lo, n - 3)
                sp.dma_start(stage_view(n), PIECES[n][0]).then_inc(ld_stage[n % 4], 16)
            sp.dma_start(res[:], x_tiles).then_inc(ld_res, 16)
            with sp.Fori(0, B - 1) as b:
                sp.wait_ge(projected, slot_count(b, "x1"))
                sp.dma_start(xb[:], x[bass.ds(b + 1, 1)].rearrange("a (t p) c -> p (a t) c", p=P)).then_inc(ld_xb, 16)

            sp.wait_ge(projected, slot_count(B - 1, SLOTS[-1]))
            s1 = sw1.rearrange("e (k p) f -> p k e f", p=P)
            r1 = rw1.rearrange("e (k p) f -> p k e f", p=P)
            w1_v = w1_raw[:].rearrange("p k (e f) -> p k e f", f=FF)
            for k in range(KC):
                sp.dma_start(w1_v[:, k, 0:NS], s1[:, k]).then_inc(ld_w1, 16)
                sp.dma_start(w1_v[:, k, NS:NE], r1[:, k]).then_inc(ld_w1, 16)
            s2 = sw2.rearrange("e f c -> (e f) c")
            r2 = rw2.rearrange("e f c -> (e f) c")
            SF = NS * FF
            full, part = SF // P, SF % P
            first = P - part
            mid = NC - 1 - (full + 1)
            sp.dma_start(w2_raw[:, 0:full, :], s2[0:full * P].rearrange("(n p) c -> p n c", p=P)).then_inc(ld_w2, 16)
            sp.dma_start(w2_raw[0:part, full, :], s2[full * P:SF]).then_inc(ld_w2, 16)
            sp.dma_start(w2_raw[part:P, full, :], r2[0:first]).then_inc(ld_w2, 16)
            sp.dma_start(w2_raw[:, full + 1:NC - 1, :],
                         r2[first:first + mid * P].rearrange("(n p) c -> p n c", p=P)).then_inc(ld_w2, 16)
            sp.dma_start(w2_raw[0:LAST, NC - 1, :], r2[first + mid * P:NR * FF]).then_inc(ld_w2, 16)
            sp.wait_ge(res_done, B + 1)
            sp.dma_start(cent_sb[:], cent).then_inc(ld_small, 16)
            sp.dma_start(gbias_sb[:], gbias.rearrange("(a n) -> a n", a=1).broadcast_to((P, NR))).then_inc(ld_small, 16)
            sp.dma_start(b2_rows[0:NR, :], rb2).then_inc(ld_small, 16)
            sp.dma_start(b2_rows[NR:NR + NS, :], sb2).then_inc(ld_small, 16)
            sp.wait_ge(dve, place("dve", "b1 cleared"))
            s_b, r_b = sb1.rearrange("e f -> (e f)"), rb1.rearrange("e f -> (e f)")
            row = lambda a: a.rearrange("(n p) -> n p", n=1)
            sp.dma_start(b1_rows[0:full, :], s_b[0:full * P].rearrange("(n p) -> n p", p=P)).then_inc(ld_small, 16)
            sp.dma_start(b1_rows[full:full + 1, 0:part], row(s_b[full * P:SF])).then_inc(ld_small, 16)
            sp.dma_start(b1_rows[full:full + 1, part:P], row(r_b[0:first])).then_inc(ld_small, 16)
            sp.dma_start(b1_rows[full + 1:NC - 1, :],
                         r_b[first:first + mid * P].rearrange("(n p) -> n p", p=P)).then_inc(ld_small, 16)
            sp.dma_start(b1_rows[NC - 1:NC, 0:LAST], row(r_b[first + mid * P:NR * FF])).then_inc(ld_small, 16)

            sp.wait_ge(dve, place("dve", "gatesT"))
            rows = FF // GB
            spread = lambda a, n: a.rearrange("e (r t) -> e r t", r=1).broadcast_to((n, rows, N))
            sp.dma_start(gates_d[0:NS * rows].rearrange("(e r) t -> e r t", r=rows),
                         spread(gatesT[NR:NR + NS, :], NS)).then_inc(gates_out, 16)
            sp.dma_start(gates_d[NS * rows:NE * rows].rearrange("(e r) t -> e r t", r=rows),
                         spread(gatesT[0:NR, :], NR)).then_inc(gates_out, 16)
            sp.wait_ge(gates_out, 32)

            def load_gates(c, par, n=P):
                src = gates_d[bass.ds(c * (P // GB), n // GB), :]
                src = src.rearrange("e (r t) -> e r t", r=1).broadcast_to((n // GB, GB, N))
                sp.dma_start(gate_rows[0:n, par, :], src).then_inc(ld_gates[par], 16)

            load_gates(0, 0)
            load_gates(1, 1)
            with sp.Fori(0, (NC - 3) // 2) as cc:
                for par in range(2):
                    sp.wait_ge(gated, 2 * (2 * cc + par + 1))
                    load_gates(2 * cc + par + 2, par)
            sp.wait_ge(gated, 2 * (NC - 2))
            load_gates(NC - 1, (NC - 1) % 2, LAST)

            for t in range(NT):
                sp.wait_ge(dve, place("dve", f"x3 {t}"))
                sp.dma_start(out_v[:, t, :], x3[:, t, :]).then_inc(stored, 16)
            sp.wait_ge(stored, 16 * NT)

        @block.tensor
        def _(e):
            def three(o, sh, sl, mh, ml, first, last, **kw):
                nc.tensor.matmul(o, sh, mh, start=first, stop=False, **kw)
                nc.tensor.matmul(o, sh, ml, start=False, stop=False, **kw)
                return nc.tensor.matmul(o, sl, mh, start=False, stop=last, **kw)

            def slot(b, s):
                n, kind, j = SLOTS.index(s), s[0], int(s[1])
                o = proj_bank[n % 2]
                if not (isinstance(b, int) and b == 0 and n < 2):
                    e.wait_ge(emptied, slot_count(b, s) - 2)
                if kind == "x":
                    e.wait_ge(ld_xb, 16 * (b + 1))
                    for t in range(TT):
                        mm = nc.tensor.transpose(o[:, t * P:(t + 1) * P], xb[:, t, j * P:(j + 1) * P], ident[:])
                elif kind == "v":
                    e.wait_ge(w_lo, piece_count("v"))
                    for k in range(KC):
                        tok = slice(j * P, (j + 1) * P)
                        mm = three(o[:], xT_hi[:, k, tok], xT_lo[:, k, tok], wv_hi[:, k, :], wv_lo[:, k, :],
                                   k == 0, k == KC - 1)
                else:
                    wh, wl = (wk_hi, wk_lo) if kind == "k" else (wq_hi, wq_lo)
                    e.wait_ge(w_lo, piece_count("k" if kind == "k" else f"q{j // 2}"))
                    e.wait_ge(emptied, slot_count(b, "x1"))
                    for a in range(2):
                        for k in range(KC):
                            f = slice((2 * j + a) * D, (2 * j + a + 1) * D)
                            mm = three(o[:, a * T:(a + 1) * T], wh[:, k, f], wl[:, k, f],
                                       xT_hi[:, k, :], xT_lo[:, k, :], k == 0, k == KC - 1)
                mm.then_inc(projected, 1)

            def score(b, h):
                s = h // 2
                e.wait_ge(rope_add, rope_count(b, f"q{s}"))
                e.wait_ge(score_read, head_count(b, h - 2))
                q = queryT[:, s % 4, h % 2, :]
                o = score_bank[h % 2]
                nc.tensor.matmul(o[:, 0:W], q[:, 0:W], keyT[:, h // G, 0:W], start=True, stop=True)
                nc.tensor.matmul(o[:, W:3 * W], q[:, W:2 * W], keyT[:, h // G, :],
                                 start=True, stop=True).then_inc(scored, 1)

            def turn(b, h):
                if isinstance(b, int) and b == 0 and h == 0:
                    after("act", "attT 3")
                e.wait_ge(norm_done, head_count(b, h))
                e.wait_ge(pT_done, head_count(b, h - 2))
                for k in range(3):
                    mm = nc.tensor.transpose(prob_bank[h % 2][:, k * W:(k + 1) * W],
                                             nprobs[:, h % RING, k * W:(k + 1) * W], ident[:])
                mm.then_inc(turned, 1)

            def values(b, g, blk):
                e.wait_ge(pT_done, head_count(b, G * g + G - 1))
                e.wait_ge(emptied, slot_count(b, "v1"))
                e.wait_ge(oT_done, pv_count(b, g, blk) - 1)
                f = slice(g * D, (g + 1) * D)
                kinds = [0] if blk == 0 else [1, 2]
                for kind in kinds:
                    t = 0 if kind < 2 else 1
                    mm = three(pv_bank[:], v_hi[:, t, f], v_lo[:, t, f],
                               pT_hi[:, g % 2, kind, :, :].rearrange("p a q -> p (a q)"),
                               pT_lo[:, g % 2, kind, :, :].rearrange("p a q -> p (a q)"),
                               kind == kinds[0], kind == kinds[-1])
                mm.then_inc(pv_done, 1)

            def project_out(b, g, blk):
                if g == 0 and blk == 0:
                    e.wait_ge(res_done, b + 1)
                e.wait_ge(w_lo, piece_count(f"o{g}"))
                e.wait_ge(oT_done, pv_count(b, g, blk))
                for a in range(G):
                    q = slice(a * W, (a + 1) * W)
                    mm = three(attn_bank[:, blk * C:(blk + 1) * C], oT_hi[:, blk, q], oT_lo[:, blk, q],
                               wo_hi[:, G * g + a, :], wo_lo[:, G * g + a, :],
                               g == 0 and blk == 0 and a == 0, g == HK - 1 and a == G - 1,
                               skip_group_check=True)
                if g == HK - 1 and blk == 1:
                    mm.then_inc(attn_done, 1)

            n = [0]

            def step(mm, name):
                assert ORDER["pe"][n[0]] == name, (ORDER["pe"][n[0]], name)
                n[0] += 1
                mm.then_inc(pe, 1)

            def after(engine, name):
                e.wait_ge({'act': act, 'dve': dve}[engine], place(engine, name))

            def once(work, of):
                if work == "ctx turned":
                    e.wait_ge(ld_ctx, 16 * 5)
                    for a in range(2):
                        mm = nc.tensor.transpose(bank[3][:, a * D:(a + 1) * D], xw[:, a, :], ident[:])
                    step(mm, "xwT")
                    for h in range(2):
                        for t in range(4):
                            mm = nc.tensor.transpose(bank[6 + h][:, t * P:(t + 1) * P], ctx_sb[:, 4 * h + t, :], ident[:])
                        step(mm, f"ctxT {h}")
                elif work == "ctx projected":
                    after("act", "ctxT 0"), after("dve", "ctxT 1")
                    for a in range(2):
                        for h in range(2):
                            mm = nc.tensor.matmul(bank[4 + 2 * a + h][:], xwT[:, a, :], ctxT[:, h * HALF:(h + 1) * HALF],
                                                  start=True, stop=True)
                            step(mm, f"xp {a} {h}")
                elif work[:-2] == "energy":
                    c = int(work[-1])
                    after("act", "xqT 1"), after("dve", "xkT 1")
                    for t in range(TT):
                        r = slice(c * T + t * P, c * T + (t + 1) * P)
                        mm = nc.tensor.matmul(bank[4 + c][:, t * T:(t + 1) * T], xqT[:, r],
                                              xkT[:, c * T:(c + 1) * T], start=True, stop=True)
                    step(mm, work)
                else:
                    c = int(work[-1])
                    after("dve", f"e_norm {c}")
                    for k in range(KC):
                        for t in range(TT):
                            mm = nc.tensor.transpose(bank[4 + c][:, k * T + t * P:k * T + (t + 1) * P],
                                                     e_exp[:, c, t, k * P:(k + 1) * P], ident[:])
                    step(mm, work)

            doers = {"slot": slot, "score": score, "turn": turn, "once": once,
                     "values0": lambda b, g: values(b, g, 0), "values1": lambda b, g: values(b, g, 1),
                     "out0": lambda b, g: project_out(b, g, 0), "out1": lambda b, g: project_out(b, g, 1)}
            e.wait_ge(ld_ident, 16)
            take_turn("pe", 0, (0, "once"), doers)
            with e.Fori(1, B) as b:
                take_turn("pe", b, (0, 1), doers)
            take_turn("pe", B, (1,), doers)

            e.wait_ge(res_done, B + 1)
            for b in range(B):
                after("dve", f"x1 {2 * b + 1}")
                for k in range(KC):
                    for t in range(TT):
                        mm = nc.tensor.transpose(bank[b][:, k * T + t * P:k * T + (t + 1) * P],
                                                 x1[:, TT * b + t, k * P:(k + 1) * P], ident[:])
                step(mm, f"x1T {b}")
            for b in range(B):
                after("act", f"x1T {b}"), after("act", f"attT {b}")
                for t in range(TT):
                    for k in range(KC):
                        mm = nc.tensor.matmul(bank[4 + b][:, t * T:(t + 1) * T], x1T[:, b, k, t * P:(t + 1) * P],
                                              attT[:, b, k, :], start=k == 0, stop=k == KC - 1)
                step(mm, f"xm {b}")
            e.wait_ge(ld_small, 16 * 9)
            after("dve", "gates ready")
            for k in range(KC):
                nc.tensor.transpose(bank[0][:, k * NR:(k + 1) * NR],
                                    cent_sb[:, k * P:(k + 1) * P], ident[0:NR, 0:NR])
            mm = nc.tensor.transpose(bank[0][:, 64:64 + NC], b1_rows[:], ident[0:NC, 0:NC])
            step(mm, "smallT")
            after("act", "smallT")
            for b in range(B):
                after("dve", f"x2 {2 * b + 1}")
                for k in range(KC):
                    for t in range(TT):
                        mm = nc.tensor.transpose(bank[b][:, k * T + t * P:k * T + (t + 1) * P],
                                                 x2[:, TT * b + t, k * P:(k + 1) * P], ident[:])
                step(mm, f"x2T {b}")
            for b in range(B):
                after("act", f"x2T {b}")
            for t in range(NT):
                for k in range(KC):
                    mm = nc.tensor.matmul(bank[4][:, t * NR:(t + 1) * NR], x2T[:, k, t * P:(t + 1) * P],
                                          centT[:, k, :], start=k == 0, stop=k == KC - 1)
            step(mm, "router")
            after("dve", "gates")
            for t in range(NT):
                mm = nc.tensor.transpose(bank[5 + t // 4][0:NR, (t % 4) * P:(t % 4 + 1) * P], gates[:, t, :], ident[:])
            step(mm, "gatesT")

            z_bank = [[bank[0], bank[1]], [bank[2], bank[3]]]
            y_bank = [[bank[4], bank[5]], [bank[6], bank[7]]]

            def hidden(c, par, n=P):
                e.wait_ge(w1_done, c + 1)
                for h in range(2):
                    cols = slice(h * HALF, (h + 1) * HALF)
                    for k in range(KC):
                        mm = three(z_bank[par][h][0:n, :], w1_hi[:, par, k, 0:n], w1_lo[:, par, k, 0:n],
                                   x2T_hi[:, k, cols], x2T_lo[:, k, cols], k == 0, k == KC - 1)
                    mm.then_inc(z_done, 1)

            def output(c, par, n=P, last=False):
                e.wait_ge(w2_done, c + 1)
                for h in range(2):
                    e.wait_ge(hid_done, 2 * c + h + 1)
                    cols = slice(h * HALF, (h + 1) * HALF)
                    for d in range(KC):
                        f = slice(d * P, (d + 1) * P)
                        mm = three(y_bank[d][h][:], w2_hi[0:n, par, f], w2_lo[0:n, par, f],
                                   hid_hi[0:n, par, cols], hid_lo[0:n, par, cols], False, last,
                                   skip_group_check=True)
                mm.then_inc(y_done, 1)

            after("dve", "x2T_lo")
            hidden(0, 0)
            hidden(1, 1)
            after("dve", "gatesT")
            for d in range(KC):
                for h in range(2):
                    nc.tensor.matmul(y_bank[d][h][:], b2_rows[:, d * P:(d + 1) * P],
                                     gatesT[:, h * HALF:(h + 1) * HALF], start=True, stop=False,
                                     skip_group_check=True)
            with e.Fori(0, (NC - 3) // 2) as cc:
                for par in range(2):
                    output(2 * cc + par, par)
                    e.wait_ge(relu_done, 2 * (2 * cc + par + 1))
                    hidden(2 * cc + par + 2, par)
            output(NC - 3, (NC - 3) % 2)
            e.wait_ge(relu_done, 2 * (NC - 2))
            hidden(NC - 1, (NC - 1) % 2, LAST)
            output(NC - 2, (NC - 2) % 2)
            output(NC - 1, (NC - 1) % 2, LAST, last=True)
            for t in range(NT):
                if t == 0:
                    after("act", "yT 0"), after("dve", "yT 0")
                if t == 4:
                    after("act", "yT 1"), after("dve", "yT 1")
                for d in range(KC):
                    mm = nc.tensor.transpose(bank[t // 2][:, (t % 2) * C + d * P:(t % 2) * C + (d + 1) * P],
                                             yT[:, d, t * P:(t + 1) * P], ident[:])
                if t % 2:
                    step(mm, f"y {t // 2}")

        @block.scalar
        def _(e):
            def piece(n):
                e.wait_ge(ld_stage[n % 4], 16 * (n // 4 + 1))
                nc.scalar.copy(PIECES[n][1], stage_view(n)).then_inc(w_hi, 1)

            def slot(b, s):
                n, kind, j = SLOTS.index(s), s[0], int(s[1])
                o = proj_bank[n % 2]
                e.wait_ge(projected, slot_count(b, s))
                if kind == "x":
                    nc.scalar.copy(xT_hi[:, j, :], o[:, 0:T]).then_inc(split_hi, 1)
                elif kind == "v":
                    nc.scalar.copy(v_hi[:, j, :], o[:]).then_inc(split_hi, 1)
                else:
                    r = ROPES.index(s)
                    if not (isinstance(b, int) and b == 0 and r < 2):
                        e.wait_ge(rope_mul, rope_count(b, s) - 2)
                    half = D // 2
                    nc.scalar.copy(swapped[0:half, r % 2, :], o[half:D, :])
                    nc.scalar.copy(swapped[half:D, r % 2, :], o[0:half, :]).then_inc(swap_done, 1)

            def softmax_exp(b, h):
                u, w = h % 2, h % RING
                e.wait_ge(top_done, head_count(b, h))
                e.wait_ge(norm_done, head_count(b, h - RING))
                nc.scalar.activation(probs[:, w, 0:W], scores[:, u, 0:W], ACT.Exp, bias=ntop[:, u, 0:1],
                                     scale=SCALE, accum_out=psums[:, w, 0:1])
                nc.scalar.activation(probs[:, w, W:3 * W], scores[:, u, W:3 * W], ACT.Exp, bias=ntop[:, u, 1:2],
                                     scale=SCALE, accum_out=psums[:, w, 1:2]).then_inc(exp_done, 1)

            def probs_hi(b, h):
                e.wait_ge(turned, head_count(b, h))
                nc.scalar.copy(pT_hi[:, (h // G) % 2, :, h % G, :],
                               prob_bank[h % 2][:, 0:3 * W].rearrange("p (k q) -> p k q", k=3)).then_inc(pT_hi_done, 1)

            def heads_hi(b, g, blk):
                e.wait_ge(pv_done, pv_count(b, g, blk))
                nc.scalar.copy(oT_hi[:, blk, :], pv_bank[:]).then_inc(oT_hi_done, 1)

            n = [0]

            def step(ins, name):
                assert ORDER["act"][n[0]] == name, (ORDER["act"][n[0]], name)
                n[0] += 1
                ins.then_inc(act, 1)

            def after(name):
                e.wait_ge(pe, place("pe", name))

            def after_dve(name):
                e.wait_ge(dve, place("dve", name))

            def once(work, of):
                if work == "piece":
                    piece(of)
                elif work == "ctx turned":
                    after("xwT")
                    step(nc.scalar.copy(xwT[:].rearrange("p a d -> p (a d)"), bank[3][:, 0:2 * D]), "xwT")
                    after("ctxT 0")
                    step(nc.scalar.copy(ctxT[:, 0:HALF], bank[6][:]), "ctxT 0")
                elif work == "ctx projected":
                    for h in range(2):
                        after(f"xp 0 {h}")
                        step(nc.scalar.activation(xqT[:, h * HALF:(h + 1) * HALF], bank[4 + h][:], ACT.Identity,
                                                  bias=xb_cols[:, 0:1]), f"xqT {h}")
                elif work[:-2] == "e_exp":
                    c = int(work[-1])
                    after_dve(f"e_top {c}")
                    for t in range(TT):
                        ins = nc.scalar.activation(e_exp[:, c, t, :], bank[4 + c][:, t * T:(t + 1) * T], ACT.Exp,
                                                   bias=e_ntop[:, c, t:t + 1], accum_out=e_sum[:, c, t:t + 1])
                    step(ins, work)
                else:
                    c = int(work[-1])
                    after(work)
                    step(nc.scalar.copy(attT[:, c, :, :].rearrange("p k r -> p (k r)"), bank[4 + c][:]), work)

            for s in (exp_done, pT_hi_done):
                e.sem_inc(s, AHEAD)
            for s in (oT_hi_done, pv_done):
                e.sem_inc(s, 1)
            doers = {"slot": slot, "exp": softmax_exp, "probs_hi": probs_hi, "once": once,
                     "heads_hi0": lambda b, g: heads_hi(b, g, 0), "heads_hi1": lambda b, g: heads_hi(b, g, 1)}
            take_turn("act", 0, (0, "once"), doers)
            with e.Fori(1, B) as b:
                take_turn("act", b, (0, 1), doers)
            take_turn("act", B, (1,), doers)

            after_dve("var 1")
            step(nc.scalar.activation(ln_std[:], ln_var[:], ACT.Sqrt), "std 1")
            for b in range(B):
                after(f"x1T {b}")
                step(nc.scalar.copy(x1T[:, b, :, :].rearrange("p k r -> p (k r)"), bank[b][:]), f"x1T {b}")
            after("smallT")
            nc.scalar.copy(centT[:].rearrange("p k r -> p (k r)"), bank[0][:, 0:KC * NR])
            step(nc.scalar.copy(b1_cols[:], bank[0][:, 64:64 + NC]), "smallT")
            after_dve("var 2")
            step(nc.scalar.activation(ln_std[:], ln_var[:], ACT.Sqrt), "std 2")
            for b in range(B):
                after(f"x2T {b}")
                step(nc.scalar.copy(x2T[:, :, b * T:(b + 1) * T], bank[b][:].rearrange("p (k t) -> p k t", k=KC)), f"x2T {b}")
            after("router")
            step(nc.scalar.activation(sig[:].rearrange("p t r -> p (t r)"), bank[4][:, 0:NT * NR], ACT.Sigmoid), "sig")

            def split_w1(c, par, n=P):
                nc.scalar.copy(w1_hi[:, par, :, 0:n], w1_raw[:, :, bass.ds(c * P, n)]).then_inc(w1_hi_done, 1)

            def split_w2(c, par, n=P):
                nc.scalar.copy(w2_hi[0:n, par, :], w2_raw[0:n, bass.ds(c, 1), :].rearrange("p a c -> p (a c)")).then_inc(w2_hi_done, 1)

            def relu(c, par, h, n=P):
                e.wait_ge(z_done, 2 * c + h + 1)
                e.sem_inc(act_passed, 1)
                nc.scalar.activation(hid[0:n, par, h * HALF:(h + 1) * HALF], bank[2 * par + h][0:n, :], ACT.Relu,
                                     bias=b1_cols[0:n, bass.ds(c, 1)]).then_inc(relu_done, 1)

            def hid_high(c, par, h, n=P):
                e.wait_ge(gated, 2 * c + h + 1)
                cols = slice(h * HALF, (h + 1) * HALF)
                nc.scalar.copy(hid_hi[0:n, par, cols], hid[0:n, par, cols]).then_inc(hid_hi_done, 1)

            def high_parts(c, par, nxt=None, n=P, n_next=P):
                relu(c, par, 0, n), relu(c, par, 1, n)
                if nxt is not None:
                    split_w1(nxt, 1 - par, n_next)
                hid_high(c, par, 0, n), hid_high(c, par, 1, n)
                if nxt is not None:
                    e.wait_ge(y_done, nxt - 1)
                    split_w2(nxt, 1 - par, n_next)

            e.wait_ge(ld_w1, 16 * 4)
            e.wait_ge(ld_w2, 16 * 5)
            split_w1(0, 0), split_w1(1, 1)
            split_w2(0, 0), split_w2(1, 1)
            high_parts(0, 0)
            with e.Fori(0, (NC - 3) // 2) as cc:
                for par in range(2):
                    high_parts(2 * cc + par + 1, 1 - par, 2 * cc + par + 2)
            high_parts(NC - 2, 1, NC - 1, n_next=LAST)
            high_parts(NC - 1, 0, n=LAST)

            e.wait_ge(y_done, NC)
            for h in range(2):
                step(nc.scalar.copy(yT[:, 0, h * HALF:(h + 1) * HALF], bank[4 + h][:]), f"yT {h}")
            for q in range(2):
                after_dve(f"var 3 {q}")
                step(nc.scalar.activation(ln_std[:, 4 * q:4 * q + 4], ln_var[:, 4 * q:4 * q + 4], ACT.Sqrt), f"std 3 {q}")

        @block.vector
        def _(e):
            low = lambda o, full, hi: nc.vector.tensor_tensor(o, full, hi.bitcast(F32), ALU.subtract)

            def piece(n):
                e.wait_ge(w_hi, n + 1)
                low(PIECES[n][2], stage_view(n), PIECES[n][1]).then_inc(w_lo, 1)

            def slot(b, s):
                n, kind, j = SLOTS.index(s), s[0], int(s[1])
                o = proj_bank[n % 2]
                if kind in "xv":
                    e.wait_ge(split_hi, split_count(b, s))
                    if kind == "x":
                        low(xT_lo[:, j, :], o[:, 0:T], xT_hi[:, j, :]).then_inc(emptied, 1)
                    else:
                        low(v_lo[:, j, :], o[:], v_hi[:, j, :]).then_inc(emptied, 1)
                    return
                r = ROPES.index(s)
                if isinstance(b, int) and b == 0 and r == 0:
                    e.wait_ge(ld_tables, 48)
                e.wait_ge(swap_done, rope_count(b, s))
                if not (isinstance(b, int) and b == 0 and r < 2):
                    e.wait_ge(rope_add, rope_count(b, s) - 2)
                nc.vector.tensor_tensor(by_cos[:, r % 2, :], o[:], cos_t[:], ALU.mult).then_inc(emptied, 1)
                nc.vector.tensor_tensor(by_sin[:, r % 2, :], swapped[:, r % 2, :], sin_t[:], ALU.mult).then_inc(rope_mul, 1)

            def mask_and_top(b, h):
                u = h % 2
                e.wait_ge(scored, H * b + h + 1)
                e.wait_ge(exp_done, head_count(b, h - 2))
                e.sem_inc(dve_passed, 1)
                o = score_bank[u]
                nc.vector.tensor_tensor_reduce(scores[:, u, 0:W], o[:, 0:W], mask[:, W:2 * W], 1.0, NEVER,
                                               ALU.add, ALU.max, top[:, u, 0:1])
                nc.vector.tensor_tensor_reduce(scores[:, u, W:3 * W], o[:, W:3 * W], mask[:], 1.0, NEVER,
                                               ALU.add, ALU.max, top[:, u, 1:2]).then_inc(score_read, 1)
                e.wait_ge(score_read, head_count(b, h))
                nc.vector.tensor_scalar(ntop[:, u, :], top[:, u, :], -SCALE, None, ALU.mult).then_inc(top_done, 1)

            def recip(b, h):
                e.wait_ge(exp_done, head_count(b, h))
                nc.vector.reciprocal(rsums[:, h % RING, :], psums[:, h % RING, :]).then_inc(rsum_done, 1)

            def probs_lo(b, h):
                e.wait_ge(pT_hi_done, head_count(b, h))
                g = (h // G) % 2
                low(pT_lo[:, g, :, h % G, :], prob_bank[h % 2][:, 0:3 * W].rearrange("p (k q) -> p k q", k=3),
                    pT_hi[:, g, :, h % G, :]).then_inc(pT_done, 1)

            def heads_lo(b, g, blk):
                e.wait_ge(oT_hi_done, pv_count(b, g, blk))
                low(oT_lo[:, blk, :], pv_bank[:], oT_hi[:, blk, :]).then_inc(oT_done, 1)

            def residual(b, _):
                e.wait_ge(attn_done, b + 1)
                r = res[:, bass.ds(b * TT, TT), :]
                nc.vector.tensor_tensor(r, attn_bank[:].rearrange("p (t c) -> p t c", t=TT), r, ALU.add).then_inc(res_done, 1)

            n = [0]

            def step(ins, name):
                assert ORDER["dve"][n[0]] == name, (ORDER["dve"][n[0]], name)
                n[0] += 1
                ins.then_inc(dve, 1)

            def after(name):
                e.wait_ge(pe, place("pe", name))

            def after_act(name):
                e.wait_ge(act, place("act", name))

            def settle():
                e.wait_ge(dve, n[0])

            def once(work, of):
                if work == "piece":
                    piece(of)
                elif work == "ctx turned":
                    after("ctxT 1")
                    step(nc.vector.tensor_copy(ctxT[:, HALF:N], bank[7][:]), "ctxT 1")
                elif work == "ctx projected":
                    for h in range(2):
                        after(f"xp 1 {h}")
                        step(nc.vector.tensor_scalar(xkT[:, h * HALF:(h + 1) * HALF], bank[6 + h][:], xb_cols[:, 1:2], None,
                                                     ALU.add), f"xkT {h}")
                elif work[:-2] == "e_top":
                    c = int(work[-1])
                    after(f"energy {c}")
                    step(nc.vector.tensor_reduce(e_ntop[:, c, :], bank[4 + c][:].rearrange("p (t s) -> p t s", t=TT),
                                                 AX.X, ALU.max, negate=True), work)
                else:
                    c = int(work[-1])
                    after_act(f"e_exp {c}")
                    step(nc.vector.reciprocal(e_rsum[:, c, :], e_sum[:, c, :]), f"e_rsum {c}")
                    settle()
                    for t in range(TT):
                        ins = nc.vector.tensor_scalar(e_exp[:, c, t, :], e_exp[:, c, t, :], e_rsum[:, c, t:t + 1], None,
                                                      ALU.mult)
                    step(ins, work)

            for s in (score_read, top_done, rsum_done, pT_done):
                e.sem_inc(s, AHEAD)
            for s in (oT_done, res_done):
                e.sem_inc(s, 1)
            doers = {"slot": slot, "top": mask_and_top, "recip": recip, "probs_lo": probs_lo, "once": once,
                     "heads_lo0": lambda b, g: heads_lo(b, g, 0), "heads_lo1": lambda b, g: heads_lo(b, g, 1),
                     "residual": residual}
            take_turn("dve", 0, (0, "once"), doers)
            e.wait_ge(ld_res, 16)
            with e.Fori(1, B) as b:
                take_turn("dve", b, (0, 1), doers)
            take_turn("dve", B, (1,), doers)

            def ln_sums(src, which, tiles, tag):
                for t in tiles:
                    step(nc.vector.bn_stats(ln_stats[:, t, :], src[:, t, :]), f"stats {which} {t}")
                settle()
                for t in tiles:
                    step(nc.vector.bn_aggr(ln_mv[:, t, :], ln_stats[:, t, :]), f"aggr {which} {t}")
                settle()
                a, z = tiles[0], tiles[-1] + 1
                step(nc.vector.tensor_scalar(ln_var[:, a:z], ln_mv[:, a:z, 1:2].rearrange("p t a -> p (t a)"),
                                             EPS, None, ALU.add), f"var {tag}")

            def ln_apply(dst, src, which, tiles, tag):
                after_act(f"std {tag}")
                a, z = tiles[0], tiles[-1] + 1
                step(nc.vector.reciprocal(ln_rstd[:, a:z], ln_std[:, a:z]), f"rstd {tag}")
                settle()
                for t in tiles:
                    step(nc.vector.tensor_scalar(dst[:, t, :], src[:, t, :], ln_mv[:, t, 0:1], ln_rstd[:, t:t + 1],
                                                 ALU.subtract, ALU.mult), f"x{which} {t}")

            e.wait_ge(res_done, B + 1)
            step(nc.vector.memset(b1_rows[:], 0.0), "b1 cleared")
            ln_sums(res, 1, range(NT), "1")
            ln_apply(x1, res, 1, range(NT), "1")
            for b in range(B):
                after(f"xm {b}")
                tiles = slice(TT * b, TT * (b + 1))
                step(nc.vector.tensor_tensor(res[:, tiles, :], bank[4 + b][:].rearrange("p (t c) -> p t c", t=TT),
                                             x1[:, tiles, :], ALU.add), f"xres {b}")
            nc.vector.memset(choice[:, :, NR:SC], NEVER)
            step(nc.vector.memset(gatesT[:], 1.0), "gates ready")
            settle()
            ln_sums(res, 2, range(NT), "2")
            ln_apply(x2, res, 2, range(NT), "2")
            for b in range(B):
                after_act(f"x2T {b}")
            for h in range(2):
                step(nc.vector.tensor_copy(x2T_hi[:, :, h * HALF:(h + 1) * HALF], x2T[:, :, h * HALF:(h + 1) * HALF]), f"x2T_hi {h}")
            settle()
            step(low(x2T_lo[:], x2T[:], x2T_hi[:]), "x2T_lo")

            after_act("sig")
            e.wait_ge(ld_small, 16 * 9)
            step(nc.vector.tensor_tensor(choice[:, :, 0:NR], sig[:],
                                         gbias_sb[:].rearrange("p (a r) -> p a r", a=1).broadcast_to((P, NT, NR)), ALU.add), "choice")
            settle()
            for t in range(NT):
                ins = nc.vector.max(best[:, t, :], choice[:, t, 0:NR])
            step(ins, "best")
            settle()
            step(nc.vector.memset(best[:, :, KR:8], NEVER), "best four")
            settle()
            for t in range(NT):
                ins = nc.vector.match_replace(taken[:, t, :], best[:, t, :], choice[:, t, :], -NEVER)
            step(ins, "taken")
            settle()
            step(nc.vector.tensor_tensor(chosen[:], taken[:, :, 0:NR], choice[:, :, 0:NR], ALU.not_equal), "chosen")
            settle()
            step(nc.vector.tensor_tensor(gates[:], chosen[:], choice[:, :, 0:NR], ALU.mult), "open")
            settle()
            step(nc.vector.tensor_reduce(gate_sum[:], gates[:], AX.X, ALU.add), "gate sum")
            settle()
            step(nc.vector.tensor_scalar(gate_sum[:], gate_sum[:], 1e-8, None, ALU.max), "gate clip")
            settle()
            step(nc.vector.reciprocal(gate_rsum[:], gate_sum[:]), "gate rsum")
            settle()
            step(nc.vector.tensor_tensor(gates[:], gates[:], gate_rsum[:].rearrange("p (t a) -> p t a", a=1).broadcast_to((P, NT, NR)),
                                         ALU.mult), "gates")
            after("gatesT")
            for h in range(2):
                ins = nc.vector.tensor_copy(gatesT[0:NR, h * HALF:(h + 1) * HALF], bank[5 + h][0:NR, :])
            step(ins, "gatesT")

            def gate(c, par, h, n=P):
                e.wait_ge(relu_done, 2 * c + h + 1)
                if h == 0:
                    e.wait_ge(ld_gates[par], 8 * (c - par) + 16)
                cols = slice(h * HALF, (h + 1) * HALF)
                nc.vector.tensor_tensor(hid[0:n, par, cols], hid[0:n, par, cols], gate_rows[0:n, par, cols],
                                        ALU.mult).then_inc(gated, 1)

            def hid_low(c, par, h, n=P):
                e.wait_ge(hid_hi_done, 2 * c + h + 1)
                cols = slice(h * HALF, (h + 1) * HALF)
                low(hid_lo[0:n, par, cols], hid[0:n, par, cols], hid_hi[0:n, par, cols]).then_inc(hid_done, 1)

            def low_parts(c, par, n=P):
                gate(c, par, 0, n), gate(c, par, 1, n)
                hid_low(c, par, 0, n), hid_low(c, par, 1, n)

            low_parts(0, 0)
            with e.Fori(0, (NC - 3) // 2) as cc:
                for par in range(2):
                    low_parts(2 * cc + par + 1, 1 - par)
            low_parts(NC - 2, 1)
            low_parts(NC - 1, 0, LAST)

            e.wait_ge(y_done, NC)
            for h in range(2):
                step(nc.vector.tensor_copy(yT[:, 1, h * HALF:(h + 1) * HALF], bank[6 + h][:]), f"yT {h}")
            for q in range(2):
                tiles = range(4 * q, 4 * q + 4)
                for u in range(2 * q, 2 * q + 2):
                    after(f"y {u}")
                    pair = slice(2 * u, 2 * u + 2)
                    step(nc.vector.scalar_tensor_tensor(res[:, pair, :], x2[:, pair, :], 2.0,
                                                        bank[u][:].rearrange("p (t c) -> p t c", t=2),
                                                        ALU.mult, ALU.add), f"yres {u}")
                settle()
                ln_sums(res, 3, tiles, f"3 {q}")
            for q in range(2):
                ln_apply(x3, res, 3, range(4 * q, 4 * q + 4), f"3 {q}")

        @block.gpsimd
        def _(e):
            def slot(b, s):
                if s[0] not in "kq":
                    return
                r, j = ROPES.index(s), int(s[1])
                o = keyT[:, 2 * j:2 * j + 2, :] if s[0] == "k" else queryT[:, j % 4, :, :]
                e.wait_ge(rope_mul, rope_count(b, s))
                nc.gpsimd.tensor_tensor(o.rearrange("p a t -> p (a t)"), by_cos[:, r % 2, :], by_sin[:, r % 2, :],
                                        ALU.add).then_inc(rope_add, 1)

            def normalise(b, h):
                u = h % RING
                e.wait_ge(rsum_done, head_count(b, h))
                e.wait_ge(turned, head_count(b, h - RING))
                e.sem_inc(pool_passed, 1)
                nc.gpsimd.tensor_scalar(nprobs[:, u, 0:W], probs[:, u, 0:W], rsums[:, u, 0:1], 1.0, ALU.mult, ALU.mult)
                nc.gpsimd.tensor_scalar(nprobs[:, u, W:3 * W], probs[:, u, W:3 * W], rsums[:, u, 1:2], 1.0,
                                        ALU.mult, ALU.mult).then_inc(norm_done, 1)

            for s in (norm_done, turned):
                e.sem_inc(s, AHEAD)
            doers = {"slot": slot, "normalise": normalise, "once": None}
            take_turn("pool", 0, (0,), doers)
            with e.Fori(1, B) as b:
                take_turn("pool", b, (0, 1), doers)
            take_turn("pool", B, (1,), doers)

            def low_w1(c, par, n=P):
                e.wait_ge(w1_hi_done, c + 1)
                nc.gpsimd.tensor_tensor(w1_lo[:, par, :, 0:n], w1_raw[:, :, bass.ds(c * P, n)],
                                        w1_hi[:, par, :, 0:n].bitcast(F32), ALU.subtract).then_inc(w1_done, 1)

            def low_w2(c, par, n=P):
                e.wait_ge(w2_hi_done, c + 1)
                nc.gpsimd.tensor_tensor(w2_lo[0:n, par, :], w2_raw[0:n, bass.ds(c, 1), :].rearrange("p a c -> p (a c)"),
                                        w2_hi[0:n, par, :].bitcast(F32), ALU.subtract).then_inc(w2_done, 1)

            low_w1(0, 0), low_w1(1, 1)
            low_w2(0, 0), low_w2(1, 1)
            with e.Fori(0, (NC - 3) // 2) as cc:
                for par in range(2):
                    low_w1(2 * cc + par + 2, par)
                    low_w2(2 * cc + par + 2, par)
            low_w1(NC - 1, 0, LAST)
            low_w2(NC - 1, 0, LAST)


def once_order(engine, steps):
    return [n for w in sorted(ONCE_AT[engine], key=ONCE_AT[engine].get) for n in steps.get(w, [w])]


ORDER = {
    "pe": once_order("pe", {"ctx turned": ["xwT", "ctxT 0", "ctxT 1"],
                            "ctx projected": [f"xp {a} {h}" for a in range(2) for h in range(2)]})
    + [f"{w} {b}" for w in ("x1T", "xm") for b in range(B)] + ["smallT"]
    + [f"x2T {b}" for b in range(B)] + ["router", "gatesT"] + [f"y {u}" for u in range(NT // 2)],
    "act": once_order("act", {"ctx turned": ["xwT", "ctxT 0"], "ctx projected": ["xqT 0", "xqT 1"]})
    + ["std 1"] + [f"x1T {b}" for b in range(B)] + ["smallT", "std 2"] + [f"x2T {b}" for b in range(B)]
    + ["sig", "yT 0", "yT 1", "std 3 0", "std 3 1"],
    "dve": once_order("dve", {"ctx turned": ["ctxT 1"], "ctx projected": ["xkT 0", "xkT 1"],
                              **{f"e_norm {b}": [f"e_rsum {b}", f"e_norm {b}"] for b in range(B)}})
    + ["b1 cleared"] + [f"{w} 1 {t}" for w in ("stats", "aggr") for t in range(NT)] + ["var 1"]
    + ["rstd 1"] + [f"x1 {t}" for t in range(NT)] + [f"xres {b}" for b in range(B)] + ["gates ready"]
    + [f"{w} 2 {t}" for w in ("stats", "aggr") for t in range(NT)] + ["var 2", "rstd 2"] + [f"x2 {t}" for t in range(NT)]
    + ["x2T_hi 0", "x2T_hi 1", "x2T_lo", "choice", "best", "best four", "taken", "chosen", "open", "gate sum", "gate clip", "gate rsum",
       "gates", "gatesT", "yT 0", "yT 1"]
    + [n for q in range(2) for n in [f"yres {u}" for u in range(2 * q, 2 * q + 2)] + [f"{w} 3 {t}" for w in ("stats", "aggr") for t in range(4 * q, 4 * q + 4)] + [f"var 3 {q}"]]
    + [n for q in range(2) for n in [f"rstd 3 {q}"] + [f"x3 {t}" for t in range(4 * q, 4 * q + 4)]],
}

_INS = ["x", "ctx_1024", "L0_attn_q_kernel", "L0_attn_k_kernel", "L0_attn_v_kernel", "L0_attn_out_kernel",
        "L0_xattn_Wq", "L0_xattn_bq", "L0_xattn_Wk", "L0_xattn_bk", "L0_ffn_shared_w1", "L0_ffn_shared_b1",
        "L0_ffn_shared_w2", "L0_ffn_shared_b2", "L0_ffn_routed_w1", "L0_ffn_routed_b1", "L0_ffn_routed_w2",
        "L0_ffn_routed_b2", "L0_ffn_centroids", "L0_ffn_bias"]


def kernel(**inputs):
    import concourse.bacc as bacc
    from concourse.bass_utils import run_bass_kernel_spmd

    nc = bacc.Bacc("TRN2", target_bir_lowering=False, num_devices=1)
    cos_c, sin_c = rope_tables()
    consts = {"cos_c": cos_c, "sin_c": sin_c, "mask_c": window_mask(), "ident_c": np.eye(P, dtype=np.float32)}
    arrays, args = {}, []
    for name, a in [(n, inputs[n]) for n in _INS] + list(consts.items()):
        a = np.ascontiguousarray(a)
        arrays[f"in_{name}"] = a
        args.append(nc.dram_tensor(f"in_{name}", a.shape, mybir.dt.from_np(a.dtype), kind="ExternalInput").ap())
    out = nc.dram_tensor("out", (B, T, C), F32, kind="ExternalOutput").ap()
    gates_d = nc.dram_tensor("gates_d", (NE * FF // GB, N), F32, kind="Internal").ap()
    decoder_layer(nc, *args, out, gates_d)
    r = run_bass_kernel_spmd(nc, [arrays], core_ids=[0])
    return r.results[0]["out"]
```

```python
from contextlib import ExitStack

import numpy as np

import concourse.bass as bass
from concourse import mybir

F32 = mybir.dt.float32
F32R = mybir.dt.float32r
ALU = mybir.AluOpType
ACT = mybir.ActivationFunctionType
AX = mybir.AxisListType

P = 128
B, T, C = 4, 256, 256
KC = C // P
TT = T // P
NT = B * TT
H, HK, D = 16, 4, 128
G = H // HK
W = 128
SCALE = float(1.0 / np.sqrt(D))
MASKED = -1e30
CX = 128
NS, NR, KR, FF = 2, 16, 4, 176
NE = NS + NR
F = NE * FF
NC = -(-F // P)
LAST = F - (NC - 1) * P
GB = 16
EPS = 1e-5
THETA = 10000.0
N = B * T
HALF = 512
NEVER = -3e38
I32 = mybir.dt.int32
RSQRT_BITS = 0x5F3759DF
NEWTON = 3
NEWTON_STEPS = 2 + 3 * NEWTON

SLOT_AT = {"x0": -2.5, "x1": -2.5, "q0": -1.25, "k0": -1, "q1": -0.75, "q2": -0.5, "q3": 1.75,
           "k1": 2.75, "q4": 4.75, "v1": 5.5, "v0": 6.5, "q5": 7.25, "q6": 7.75, "q7": 11,
           "n": 25.5, "m0": 26.5, "m1": 26.75, "y": 29.25}
WINDOW = -2.5


def in_window(at):
    w = int((at - WINDOW) // H)
    return w, at - H * w


SLOTS = sorted(SLOT_AT, key=lambda s: in_window(SLOT_AT[s])[1])
NSLOT = len(SLOTS)
LATE = [s for s in SLOTS if in_window(SLOT_AT[s])[0] == 1]
FILLS = [(turn, s) for turn in range(B + 1) for s in SLOTS if (turn if s in LATE else turn < B)]
ROPES = [s for s in SLOTS if s[0] in "kq"]
NROPE = len(ROPES)
SPLITS = [s for s in SLOTS if s[0] in "xv"]
NSPLIT = len(SPLITS)
LAST_M = [s for s in SLOTS if s[0] == "m"][-1]
LAST_V = [s for s in SLOTS if s[0] == "v"][-1]
RING = 2
AHEAD = RING
WORK_AT = {
    "pe": {"score": 0, "slot": 0, "turn": 3, "values0": 7.25, "values1": 9, "out0": 9.25,
           "out1": 11},
    "act": {"slot": 0, "exp": 0.75, "probs_hi": 3, "heads_hi0": 7.25, "heads_hi1": 9.25},
    "dve": {"slot": 0, "top": -0.5, "recip": 0.75, "probs_lo": 3, "heads_lo0": 7.25, "heads_lo1": 9,
            "residual": 22.75, "moments 1": 23, "moments 2": 26.75, "normed 1": 24.25,
            "normed 2": 27.5},
    "pool": {"slot": 0, "normalise": 0.5, "norm 1": 22.75, "norm 2": 26.75},
}
LATER = {"act": {"y": -0.25}, "dve": {"n": -0.5, "m0": -0.75, "m1": -0.25, "y": -0.25}}
PIECE_NAMES = ["q0", "k", "q1", "q2", "v", "q3", "o0", "o1", "o2", "o3"]
PIECE_AT = dict(zip(PIECE_NAMES, (-2.1, -2.05, -0.9, 2.2, 3.1, 5.4, 6.6, 8.1, 10.1, 12.1)))
ONCE_AT = {
    "pe": {"ctx turned": -2.4, "ctx projected": -2, "energy 0": -0.9, "energy 1": -0.85,
           "energy 2": 0.2, "energy 3": 0.25, "attT 0": 1.1, "attT 1": 1.15, "attT 2": 2.1,
           "attT 3": 2.15, "small turned": 4.1},
    "act": {"ctx turned": -2.35, "ctx projected": -2, "e_exp 0": -0.3, "e_exp 1": -0.25,
            "e_exp 2": 0.8, "e_exp 3": 0.85, "attT 0": 1.3, "attT 1": 1.35, "attT 2": 2.5,
            "attT 3": 2.55, "small turned": 4.3},
    "dve": {"ctx turned": -2.35, "ctx projected": -1.95, "e_top 0": -0.7, "e_top 1": -0.65,
            "e_top 2": 0.3, "e_top 3": 0.35, "e_norm 0": -0.1, "e_norm 1": -0.05, "e_norm 2": 1.7,
            "e_norm 3": 1.75, "small turned": 4.35},
    "pool": {},
}


def window_order(engine):
    events = []
    for work, lag in WORK_AT[engine].items():
        if work == "slot":
            events += [(SLOT_AT[s] + lag + LATER.get(engine, {}).get(s, 0), work, s) for s in SLOTS if engine != "pool" or s in ROPES]
        elif work == "residual" or " " in work:
            events.append((lag, work, 0))
        elif work[-1] in "01":
            events += [(G * g + lag, work, g) for g in range(HK)]
        else:
            events += [(h + lag, work, h) for h in range(H)]
    turns = [(in_window(at)[1], in_window(at)[0], work, of) for at, work, of in events]
    assert all(window in (0, 1) for _, window, _, _ in turns), engine
    turns += [(at, "once", name, 0) for name, at in ONCE_AT[engine].items()]
    if engine in ("act", "dve"):
        turns += [(at, "once", "piece", PIECE_NAMES.index(name)) for name, at in PIECE_AT.items()]
    return [(window, work, of) for _, window, work, of in sorted(turns, key=lambda e: e[0])]


def take_turn(engine, b, windows, doers):
    for window, work, of in window_order(engine):
        if window not in windows:
            continue
        if window == "once":
            doers["once"](work, of)
        else:
            doers[work](b - window, of)


def slot_count(b, s):
    turn = b + (s in LATE)
    if isinstance(turn, int):
        return FILLS.index((turn, s)) + 1
    return NSLOT * turn - len(LATE) + SLOTS.index(s) + 1


def freed_count(b, s):
    turn, n = b + (s in LATE), SLOTS.index(s)
    if isinstance(turn, int):
        before = [i for i, (_, other) in enumerate(FILLS[:slot_count(b, s) - 1]) if (n - SLOTS.index(other)) % 2 == 0]
        return before[-1] + 1 if before else 0
    return NSLOT * turn - len(LATE) + max(n - 1, 0)


def rope_count(b, s):
    return NROPE * b + ROPES.index(s) + 1


def split_count(b, s):
    return NSPLIT * b + SPLITS.index(s) + 1


def head_count(b, h):
    return H * b + h + 1 + AHEAD


def place(engine, name):
    return ORDER[engine].index(name) + 1


def pv_count(b, g, blk):
    return 2 * HK * b + 2 * g + blk + 2


def rope_tables():
    fraction = np.arange(0, D, 2, dtype=np.float32) / np.float32(D)
    timescale = np.float32(THETA) ** fraction
    angle = np.arange(T, dtype=np.float32)[:, None] / timescale[None, :]
    cos, sin = np.cos(angle).T, np.sin(angle).T
    cos_t = np.concatenate([cos, cos], 0)
    sin_t = np.concatenate([-sin, sin], 0)
    two = lambda a: np.ascontiguousarray(np.concatenate([a, a], 1), dtype=np.float32)
    return two(cos_t), two(sin_t)


def window_mask():
    p, j = np.arange(W)[:, None], np.arange(2 * W)[None, :]
    return np.where((j >= p) & (j <= p + W), np.float32(0), np.float32(MASKED)).astype(np.float32)


def decoder_layer(nc, x, ctx_in, wq, wk, wv, wo, xwq, xbq, xwk, xbk, sw1, sb1, sw2, sb2,
                  rw1, rb1, rw2, rb2, cent, gbias, cos_c, sin_c, mask_c, ident_c, out, gates_d):
    es = ExitStack()
    with es:
        def sb(name, shape, dt=F32, where=es):
            return where.enter_context(nc.sbuf_tensor(name, shape, dt))

        def sem(name):
            return es.enter_context(nc.semaphore(name))

        bank = [es.enter_context(nc.psum_tensor(f"bank{i}", [P, HALF], F32)) for i in range(8)]
        proj_bank, score_bank, prob_bank = bank[0:2], bank[2:4], bank[4:6]
        pv_bank, attn_bank = bank[6], bank[7]

        ident = sb("ident", [P, P])
        res = sb("res", [P, NT, C])
        attT = sb("attT", [P, B, KC, T])
        xln = sb("xln", [P, TT, C])
        x1T = sb("x1T", [P, KC, T])
        moments = sb("moments", [P, TT, 2])
        bn = sb("bn", [P, TT, 6])
        var_eps = sb("var_eps", [P, TT])
        half_neg = sb("half_neg", [P, TT])
        newton = sb("newton", [P, 2, TT])
        factor = sb("factor", [P, TT])
        root = sb("root", [P, TT])
        unused = sb("unused", [P, 1])
        two_ident = sb("two_ident", [P, P], F32R)
        cent_sb = sb("cent_sb", [NR, C])
        centT_hi = sb("centT_hi", [P, KC, NR], F32R)
        centT_lo = sb("centT_lo", [P, KC, NR], F32R)
        gbias_sb = sb("gbias_sb", [P, NR])
        b2_rows = sb("b2_rows", [NR + NS, C])
        b1_rows = sb("b1_rows", [NC, P])
        b1_cols = sb("b1_cols", [P, NC])
        ln_stats = sb("ln_stats", [P, NT, 6])
        ln_mv = sb("ln_mv", [P, NT, 2])
        ln_var = sb("ln_var", [P, NT])
        ln_shift = sb("ln_shift", [P, NT])
        ln_std = sb("ln_std", [P, NT])
        ln_rstd = sb("ln_rstd", [P, NT])

        att = ExitStack()
        stage = sb("stage", [P, 4, 1024], F32, att)
        wq_hi = sb("wq_hi", [P, KC, H * D], F32R, att)
        wq_lo = sb("wq_lo", [P, KC, H * D], F32R, att)
        wk_hi = sb("wk_hi", [P, KC, HK * D], F32R, att)
        wk_lo = sb("wk_lo", [P, KC, HK * D], F32R, att)
        wv_hi = sb("wv_hi", [P, KC, HK * D], F32R, att)
        wv_lo = sb("wv_lo", [P, KC, HK * D], F32R, att)
        xb = sb("xb", [P, TT, C], F32, att)
        cross = ExitStack()
        ctx_sb = sb("ctx_sb", [P, NT, CX], F32, cross)
        xw = sb("xw", [P, 2, CX], F32, cross)
        xb_cols = sb("xb_cols", [P, 2], F32, cross)
        ctxT = sb("ctxT", [P, N], F32, cross)
        xwT = sb("xwT", [P, 2, D], F32, cross)
        xqT = sb("xqT", [P, N], F32, cross)
        xkT = sb("xkT", [P, N], F32, cross)
        e_ntop = sb("e_ntop", [P, B, 2], F32, cross)
        e_exp = sb("e_exp", [P, B, 2, T], F32, cross)
        e_sum = sb("e_sum", [P, B, 2], F32, cross)
        e_rsum = sb("e_rsum", [P, B, 2], F32, cross)
        cross.close()
        wo_hi = sb("wo_hi", [P, H, C], F32R, att)
        wo_lo = sb("wo_lo", [P, H, C], F32R, att)
        cos_t = sb("cos_t", [P, HALF], F32, att)
        sin_t = sb("sin_t", [P, HALF], F32, att)
        mask = sb("mask", [P, 2 * W], F32, att)
        xT_hi = sb("xT_hi", [P, KC, T], F32R, att)
        xT_lo = sb("xT_lo", [P, KC, T], F32R, att)
        keyT = sb("keyT", [P, HK, T], F32, att)
        queryT = sb("queryT", [P, 4, 2, T], F32, att)
        v_hi = sb("v_hi", [P, TT, HK * D], F32R, att)
        v_lo = sb("v_lo", [P, TT, HK * D], F32R, att)
        swapped = sb("swapped", [P, 2, HALF], F32, att)
        by_cos = sb("by_cos", [P, 2, HALF], F32, att)
        by_sin = sb("by_sin", [P, 2, HALF], F32, att)
        scores = sb("scores", [P, 2, 3 * W], F32, att)
        top = sb("top", [P, 2, 2], F32, att)
        ntop = sb("ntop", [P, 2, 2], F32, att)
        probs = sb("probs", [P, RING, 3 * W], F32, att)
        psums = sb("psums", [P, RING, 2], F32, att)
        rsums = sb("rsums", [P, RING, 2], F32, att)
        nprobs = sb("nprobs", [P, RING, 3 * W], F32, att)
        pT_hi = sb("pT_hi", [P, 2, 3, G, W], F32R, att)
        pT_lo = sb("pT_lo", [P, 2, 3, G, W], F32R, att)
        oT_hi = sb("oT_hi", [P, 2, HALF], F32R, att)
        oT_lo = sb("oT_lo", [P, 2, HALF], F32R, att)
        att.close()

        x2T_hi = sb("x2T_hi", [P, KC, N], F32R)
        x2T_lo = sb("x2T_lo", [P, KC, N], F32R)
        w1_raw = sb("w1_raw", [P, KC, F])
        w2_raw = sb("w2_raw", [P, NC, C])
        assert 2 * KC * N == 4096 and KC * F + NC * C <= 2 * KC * (H + 2 * HK) * D + TT * C
        sigT = sb("sigT", [NR, N])
        SC = NR + 4
        choice = sb("choice", [P, NT, SC])
        taken = sb("taken", [P, NT, SC])
        best = sb("best", [P, NT, 8])
        chosen = sb("chosen", [P, NT, NR])
        gate_sum = sb("gate_sum", [P, NT])
        gate_rsum = sb("gate_rsum", [P, NT])
        gates = sb("gates", [P, NT, NR])
        gatesT = sb("gatesT", [NR + NS, N])
        w1_hi = sb("w1_hi", [P, 2, KC, P], F32R)
        w1_lo = sb("w1_lo", [P, 2, KC, P], F32R)
        w2_hi = sb("w2_hi", [P, 2, C], F32R)
        w2_lo = sb("w2_lo", [P, 2, C], F32R)
        gate_rows = sb("gate_rows", [P, 2, N])
        hid = sb("hid", [P, 2, N])
        hid_hi = sb("hid_hi", [P, 2, N], F32R)
        hid_lo = sb("hid_lo", [P, 2, N], F32R)
        yT = sb("yT", [P, KC, N])
        x3 = sb("x3", [P, NT, C])

        ld_ident, ld_tables, ld_res = sem("ld_ident"), sem("ld_tables"), sem("ld_res")
        ld_xb = sem("ld_xb")
        ld_stage = [sem(f"ld_stage{i}") for i in range(4)]
        w_hi, w_lo = sem("w_hi"), sem("w_lo")
        projected, emptied = sem("projected"), sem("emptied")
        swap_done, rope_mul, rope_add = sem("swap_done"), sem("rope_mul"), sem("rope_add")
        split_hi = sem("split_hi")
        scored, score_read, top_done = sem("scored"), sem("score_read"), sem("top_done")
        exp_done, rsum_done, norm_done = sem("exp_done"), sem("rsum_done"), sem("norm_done")
        turned, pT_hi_done, pT_done = sem("turned"), sem("pT_hi_done"), sem("pT_done")
        pv_done, oT_hi_done, oT_done = sem("pv_done"), sem("oT_hi_done"), sem("oT_done")
        attn_done, res_done = sem("attn_done"), sem("res_done")
        stats_done, aggr_done, moments_done = sem("stats_done"), sem("aggr_done"), sem("moments_done")
        newton_done, ln_done, m_added = sem("newton_done"), sem("ln_done"), sem("m_added")
        root_done, inverted = sem("root_done"), sem("inverted")
        x2_hi_done, two_done = sem("x2_hi_done"), sem("two_done")
        ld_ctx, ld_w1, ld_w2, ld_small = sem("ld_ctx"), sem("ld_w1"), sem("ld_w2"), sem("ld_small")
        pe, act, dve = sem("pe_step"), sem("act_step"), sem("dve_step")
        gates_out, ld_gates = sem("gates_out"), [sem("ld_gates0"), sem("ld_gates1")]
        w1_hi_done, w1_done = sem("w1_hi_done"), sem("w1_done")
        w2_hi_done, w2_done = sem("w2_hi_done"), sem("w2_done")
        z_done, relu_done, gated, hid_hi_done, hid_done = (
            sem("z_done"), sem("relu_done"), sem("gated"), sem("hid_hi_done"), sem("hid_done"))
        y_done = sem("y_done")
        stored = sem("stored")
        dve_passed, pool_passed, act_passed = sem("dve_passed"), sem("pool_passed"), sem("act_passed")

        x_tiles = x.rearrange("b (t p) c -> p (b t) c", p=P)
        wq_v = wq.rearrange("(k p) n -> p k n", p=P)
        wk_v = wk.rearrange("(k p) n -> p k n", p=P)
        wv_v = wv.rearrange("(k p) n -> p k n", p=P)
        wo_v = wo.rearrange("(h p) n -> p h n", p=P)
        ctx_v = ctx_in.rearrange("b (t p) c -> p (b t) c", p=P)
        out_v = out.rearrange("b (t p) c -> p (b t) c", p=P)

        def heads4(t, j):
            return t[:, :, j * HALF:(j + 1) * HALF]
        by_name = {"k": (wk_v, wk_hi[:], wk_lo[:], KC), "v": (wv_v, wv_hi[:], wv_lo[:], KC)}
        for j in range(4):
            by_name[f"q{j}"] = (heads4(wq_v, j), heads4(wq_hi, j), heads4(wq_lo, j), KC)
            by_name[f"o{j}"] = (wo_v[:, 4 * j:4 * j + 4, :], wo_hi[:, 4 * j:4 * j + 4, :],
                                wo_lo[:, 4 * j:4 * j + 4, :], 4)
        PIECES = [by_name[name] for name in PIECE_NAMES]

        def piece_count(name):
            return PIECE_NAMES.index(name) + 1

        def stage_view(n):
            return stage[:, n % 4, :].rearrange("p (k n) -> p k n", k=PIECES[n][3])

        UNGATED = NS * FF // P

        def half_count(c, h):
            if isinstance(c, int) and c < UNGATED:
                return 2 * h + c + 1
            return 2 * c + h + 1

        def gate_count(c, h):
            return 2 * c + (h + 1 - 2 * UNGATED)

        def is_last(b, g, blk):
            return isinstance(b, int) and b == B - 1 and g == HK - 1 and blk == 1

        def pv_of(b, g, blk):
            return score_bank[1] if is_last(b, g, blk) else pv_bank

        E_BANK = [6, 7, 4, 5]

        block = es.enter_context(nc.Block())

        @block.sync
        def _(sp):
            SF = NS * FF
            full, part = SF // P, SF % P
            first = P - part
            mid = NC - 1 - (full + 1)

            def small_loads():
                sp.dma_start(cent_sb[:], cent).then_inc(ld_small, 16)
                sp.dma_start(gbias_sb[:], gbias.rearrange("(a n) -> a n", a=1).broadcast_to((P, NR))).then_inc(ld_small, 16)
                sp.dma_start(b2_rows[0:NR, :], rb2).then_inc(ld_small, 16)
                sp.dma_start(b2_rows[NR:NR + NS, :], sb2).then_inc(ld_small, 16)
                sp.wait_ge(dve, place("dve", "b1 cleared"))
                s_b, r_b = sb1.rearrange("e f -> (e f)"), rb1.rearrange("e f -> (e f)")
                row = lambda a: a.rearrange("(n p) -> n p", n=1)
                sp.dma_start(b1_rows[0:full, :], s_b[0:full * P].rearrange("(n p) -> n p", p=P)).then_inc(ld_small, 16)
                sp.dma_start(b1_rows[full:full + 1, 0:part], row(s_b[full * P:SF])).then_inc(ld_small, 16)
                sp.dma_start(b1_rows[full:full + 1, part:P], row(r_b[0:first])).then_inc(ld_small, 16)
                sp.dma_start(b1_rows[full + 1:NC - 1, :],
                             r_b[first:first + mid * P].rearrange("(n p) -> n p", p=P)).then_inc(ld_small, 16)
                sp.dma_start(b1_rows[NC - 1:NC, 0:LAST], row(r_b[first + mid * P:NR * FF])).then_inc(ld_small, 16)

            sp.dma_start(xb[:], x[0].rearrange("(t p) c -> p t c", p=P)).then_inc(ld_xb, 16)
            sp.dma_start(ident[:], ident_c).then_inc(ld_ident, 16)
            sp.dma_start(xw[:, 0, :], xwq).then_inc(ld_ctx, 16)
            sp.dma_start(xw[:, 1, :], xwk).then_inc(ld_ctx, 16)
            sp.dma_start(xb_cols[:, 0:1], xbq.rearrange("(d a) -> d a", a=1)).then_inc(ld_ctx, 16)
            sp.dma_start(xb_cols[:, 1:2], xbk.rearrange("(d a) -> d a", a=1)).then_inc(ld_ctx, 16)
            sp.dma_start(ctx_sb[:], ctx_v).then_inc(ld_ctx, 16)
            for n in range(4):
                sp.dma_start(stage_view(n), PIECES[n][0]).then_inc(ld_stage[n % 4], 16)
                if n == 1:
                    sp.dma_start(cos_t[:], cos_c).then_inc(ld_tables, 16)
                    sp.dma_start(sin_t[:], sin_c).then_inc(ld_tables, 16)
                    sp.dma_start(mask[:], mask_c).then_inc(ld_tables, 16)
            for n in range(4, len(PIECES)):
                if n == 6:
                    small_loads()
                sp.wait_ge(w_lo, n - 3)
                sp.dma_start(stage_view(n), PIECES[n][0]).then_inc(ld_stage[n % 4], 16)
            sp.dma_start(res[:], x_tiles).then_inc(ld_res, 16)

            def load_next_x(b):
                sp.wait_ge(projected, slot_count(b, "x1"))
                sp.dma_start(xb[:], x[bass.ds(b + 1, 1)].rearrange("a (t p) c -> p (a t) c", p=P)).then_inc(ld_xb, 16)

            load_next_x(0)
            with sp.Fori(1, B - 1) as b:
                load_next_x(b)

            sp.wait_ge(projected, max(slot_count(B - 1, s) for s in SLOTS if s[0] in "xkqv"))
            s1 = sw1.rearrange("e (k p) f -> p k e f", p=P)
            r1 = rw1.rearrange("e (k p) f -> p k e f", p=P)
            w1_v = w1_raw[:].rearrange("p k (e f) -> p k e f", f=FF)
            for k in range(KC):
                sp.dma_start(w1_v[:, k, 0:NS], s1[:, k]).then_inc(ld_w1, 16)
                sp.dma_start(w1_v[:, k, NS:NE], r1[:, k]).then_inc(ld_w1, 16)
            s2 = sw2.rearrange("e f c -> (e f) c")
            r2 = rw2.rearrange("e f c -> (e f) c")
            sp.dma_start(w2_raw[:, 0:full, :], s2[0:full * P].rearrange("(n p) c -> p n c", p=P)).then_inc(ld_w2, 16)
            sp.dma_start(w2_raw[0:part, full, :], s2[full * P:SF]).then_inc(ld_w2, 16)
            sp.dma_start(w2_raw[part:P, full, :], r2[0:first]).then_inc(ld_w2, 16)
            sp.dma_start(w2_raw[:, full + 1:NC - 1, :],
                         r2[first:first + mid * P].rearrange("(n p) c -> p n c", p=P)).then_inc(ld_w2, 16)
            sp.dma_start(w2_raw[0:LAST, NC - 1, :], r2[first + mid * P:NR * FF]).then_inc(ld_w2, 16)
            sp.wait_ge(dve, place("dve", "gatesT"))
            rows = FF // GB
            spread = lambda a, n: a.rearrange("e (r t) -> e r t", r=1).broadcast_to((n, rows, N))
            sp.dma_start(gates_d[0:NS * rows].rearrange("(e r) t -> e r t", r=rows),
                         spread(gatesT[NR:NR + NS, :], NS)).then_inc(gates_out, 16)
            sp.dma_start(gates_d[NS * rows:NE * rows].rearrange("(e r) t -> e r t", r=rows),
                         spread(gatesT[0:NR, :], NR)).then_inc(gates_out, 16)
            sp.wait_ge(gates_out, 32)

            def load_gates(c, par, n=P):
                src = gates_d[bass.ds(c * (P // GB), n // GB), :]
                src = src.rearrange("e (r t) -> e r t", r=1).broadcast_to((n // GB, GB, N))
                sp.dma_start(gate_rows[0:n, par, :], src).then_inc(ld_gates[par], 16)

            load_gates(2, 0)
            load_gates(3, 1)
            with sp.Fori(1, (NC - 3) // 2) as cc:
                for par in range(2):
                    sp.wait_ge(gated, gate_count(2 * cc + par, 1))
                    load_gates(2 * cc + par + 2, par)
            sp.wait_ge(gated, gate_count(NC - 3, 1))
            load_gates(NC - 1, (NC - 1) % 2, LAST)

            for t in (0, 2, 1, 3, 4, 6, 5, 7):
                if t % 4 < 2:
                    sp.wait_ge(dve, place("dve", f"x3 {t}"))
                else:
                    sp.wait_ge(act, place("act", f"x3 {t}"))
                sp.dma_start(out_v[:, t, :], x3[:, t, :]).then_inc(stored, 16)
            sp.wait_ge(stored, 16 * NT)

        @block.tensor
        def _(e):
            def three(o, sh, sl, mh, ml, first, last, **kw):
                nc.tensor.matmul(o, sh, mh, start=first, stop=False, **kw)
                nc.tensor.matmul(o, sh, ml, start=False, stop=False, **kw)
                return nc.tensor.matmul(o, sl, mh, start=False, stop=last, **kw)

            z_bank = [[bank[2], bank[3]], [bank[4], bank[5]]]
            y_bank = [[bank[6], bank[7]], [bank[0], bank[1]]]

            def router(h):
                cols = slice(h * HALF, (h + 1) * HALF)
                for k in range(KC):
                    mm = three(bank[6 + h][0:NR, :], centT_hi[:, k, :], centT_lo[:, k, :],
                               x2T_hi[:, k, cols], x2T_lo[:, k, cols], k == 0, k == KC - 1)
                step(mm, f"router {h}")

            def hidden_half(c, par, h, n=P):
                cols = slice(h * HALF, (h + 1) * HALF)
                for k in range(KC):
                    mm = three(z_bank[par][h][0:n, :], w1_hi[:, par, k, 0:n], w1_lo[:, par, k, 0:n],
                               x2T_hi[:, k, cols], x2T_lo[:, k, cols], k == 0, k == KC - 1)
                mm.then_inc(z_done, 1)

            def hidden(c, par, n=P):
                e.wait_ge(w1_done, c + 1)
                hidden_half(c, par, 0, n), hidden_half(c, par, 1, n)

            def slot(b, s):
                n, kind, j = SLOTS.index(s), s[0], int(s[1:] or 0)
                o = proj_bank[n % 2]
                if not (isinstance(b, int) and freed_count(b, s) == 0):
                    e.wait_ge(emptied, freed_count(b, s))
                if kind == "x":
                    e.wait_ge(ld_xb, 16 * (b + 1))
                    for t in range(TT):
                        mm = nc.tensor.transpose(o[:, t * P:(t + 1) * P], xb[:, t, j * P:(j + 1) * P], ident[:])
                elif kind in "ny":
                    if isinstance(b, int) and b == B - 1:
                        if kind == "n":
                            e.wait_ge(emptied, slot_count(B - 2, "y"))
                            e.wait_ge(oT_done, pv_count(B - 1, HK - 1, 1))
                            router(0)
                        else:
                            e.wait_ge(w1_done, 2)
                            hidden_half(0, 0, 0), hidden_half(1, 1, 0)
                    e.wait_ge(ln_done, 2 * b + (1 if kind == "n" else 2))
                    for k in range(KC):
                        for t in range(TT):
                            mm = nc.tensor.transpose(o[:, k * T + t * P:k * T + (t + 1) * P],
                                                     xln[:, t, k * P:(k + 1) * P], ident[:])
                elif kind == "m":
                    e.wait_ge(emptied, slot_count(b, "n"))
                    for k in range(KC):
                        mm = nc.tensor.matmul(o[:, 0:C], x1T[:, k, j * P:(j + 1) * P],
                                              attT[:, bass.ds(b, 1), k, :].rearrange("p a r -> p (a r)"),
                                              start=k == 0, stop=k == KC - 1)
                elif kind == "v":
                    e.wait_ge(w_lo, piece_count("v"))
                    for k in range(KC):
                        tok = slice(j * P, (j + 1) * P)
                        mm = three(o[:], xT_hi[:, k, tok], xT_lo[:, k, tok], wv_hi[:, k, :], wv_lo[:, k, :],
                                   k == 0, k == KC - 1)
                else:
                    wh, wl = (wk_hi, wk_lo) if kind == "k" else (wq_hi, wq_lo)
                    e.wait_ge(w_lo, piece_count("k" if kind == "k" else f"q{j // 2}"))
                    e.wait_ge(emptied, slot_count(b, "x1"))
                    for a in range(2):
                        for k in range(KC):
                            f = slice((2 * j + a) * D, (2 * j + a + 1) * D)
                            mm = three(o[:, a * T:(a + 1) * T], wh[:, k, f], wl[:, k, f],
                                       xT_hi[:, k, :], xT_lo[:, k, :], k == 0, k == KC - 1)
                mm.then_inc(projected, 1)

            def score(b, h):
                s = h // 2
                needed = max((f"q{s}", f"k{h // 8}"), key=ROPES.index)
                e.wait_ge(rope_add, rope_count(b, needed))
                e.wait_ge(score_read, head_count(b, h - 2))
                q = queryT[:, s % 4, h % 2, :]
                o = score_bank[h % 2]
                nc.tensor.matmul(o[:, 0:W], q[:, 0:W], keyT[:, h // G, 0:W], start=True, stop=True)
                nc.tensor.matmul(o[:, W:3 * W], q[:, W:2 * W], keyT[:, h // G, :],
                                 start=True, stop=True).then_inc(scored, 1)

            def turn(b, h):
                if isinstance(b, int) and b == 0 and h == 0:
                    after("act", "attT 3")
                e.wait_ge(norm_done, head_count(b, h))
                e.wait_ge(pT_done, head_count(b, h - 2))
                for k in range(3):
                    mm = nc.tensor.transpose(prob_bank[h % 2][:, k * W:(k + 1) * W],
                                             nprobs[:, h % RING, k * W:(k + 1) * W], ident[:])
                mm.then_inc(turned, 1)

            def values(b, g, blk):
                e.wait_ge(pT_done, head_count(b, G * g + G - 1))
                e.wait_ge(emptied, slot_count(b, LAST_V))
                if not is_last(b, g, blk):
                    e.wait_ge(oT_done, pv_count(b, g, blk) - 1)
                f = slice(g * D, (g + 1) * D)
                kinds = [0] if blk == 0 else [1, 2]
                for kind in kinds:
                    t = 0 if kind < 2 else 1
                    mm = three(pv_of(b, g, blk)[:], v_hi[:, t, f], v_lo[:, t, f],
                               pT_hi[:, g % 2, kind, :, :].rearrange("p a q -> p (a q)"),
                               pT_lo[:, g % 2, kind, :, :].rearrange("p a q -> p (a q)"),
                               kind == kinds[0], kind == kinds[-1])
                mm.then_inc(pv_done, 1)

            def project_out(b, g, blk):
                if isinstance(b, int) and b == 0 and g == 0 and blk == 0:
                    after("dve", "centT_lo")
                if g == 0 and blk == 0:
                    e.wait_ge(res_done, b + 1)
                e.wait_ge(w_lo, piece_count(f"o{g}"))
                e.wait_ge(oT_done, pv_count(b, g, blk))
                for a in range(G):
                    q = slice(a * W, (a + 1) * W)
                    mm = three(attn_bank[:, blk * C:(blk + 1) * C], oT_hi[:, blk, q], oT_lo[:, blk, q],
                               wo_hi[:, G * g + a, :], wo_lo[:, G * g + a, :],
                               g == 0 and blk == 0 and a == 0, g == HK - 1 and a == G - 1,
                               skip_group_check=True)
                if g == HK - 1 and blk == 1:
                    mm.then_inc(attn_done, 1)

            n = [0]

            def step(mm, name):
                assert ORDER["pe"][n[0]] == name, (ORDER["pe"][n[0]], name)
                n[0] += 1
                mm.then_inc(pe, 1)

            def after(engine, name):
                e.wait_ge({'act': act, 'dve': dve}[engine], place(engine, name))

            def once(work, of):
                if work == "ctx turned":
                    e.wait_ge(ld_ctx, 16 * 5)
                    for a in range(2):
                        mm = nc.tensor.transpose(bank[3][:, a * D:(a + 1) * D], xw[:, a, :], ident[:])
                    step(mm, "xwT")
                    for h in range(2):
                        for t in range(4):
                            mm = nc.tensor.transpose(bank[6 + h][:, t * P:(t + 1) * P], ctx_sb[:, 4 * h + t, :], ident[:])
                        step(mm, f"ctxT {h}")
                elif work == "ctx projected":
                    after("act", "ctxT 0"), after("dve", "ctxT 1")
                    for a in range(2):
                        for h in range(2):
                            mm = nc.tensor.matmul(bank[4 + 2 * a + h][:], xwT[:, a, :], ctxT[:, h * HALF:(h + 1) * HALF],
                                                  start=True, stop=True)
                            step(mm, f"xp {a} {h}")
                elif work[:-2] == "energy":
                    c = int(work[-1])
                    after("act", "xqT 1"), after("dve", "xkT 1")
                    for t in range(TT):
                        r = slice(c * T + t * P, c * T + (t + 1) * P)
                        mm = nc.tensor.matmul(bank[E_BANK[c]][:, t * T:(t + 1) * T], xqT[:, r],
                                              xkT[:, c * T:(c + 1) * T], start=True, stop=True)
                    step(mm, work)
                elif work == "small turned":
                    e.wait_ge(ld_small, 16 * 9)
                    after("act", "attT 3")
                    for k in range(KC):
                        nc.tensor.transpose(bank[7][:, k * NR:(k + 1) * NR],
                                            cent_sb[:, k * P:(k + 1) * P], ident[0:NR, 0:NR])
                    mm = nc.tensor.transpose(bank[7][:, 64:64 + NC], b1_rows[:], ident[0:NC, 0:NC])
                    step(mm, "smallT")
                else:
                    c = int(work[-1])
                    after("dve", f"e_norm {c}")
                    for k in range(KC):
                        for t in range(TT):
                            mm = nc.tensor.transpose(bank[E_BANK[c]][:, k * T + t * P:k * T + (t + 1) * P],
                                                     e_exp[:, c, t, k * P:(k + 1) * P], ident[:])
                    step(mm, work)

            doers = {"slot": slot, "score": score, "turn": turn, "once": once,
                     "values0": lambda b, g: values(b, g, 0), "values1": lambda b, g: values(b, g, 1),
                     "out0": lambda b, g: project_out(b, g, 0), "out1": lambda b, g: project_out(b, g, 1)}
            e.wait_ge(ld_ident, 16)
            take_turn("pe", 0, (0, "once"), doers)
            with e.Fori(1, B) as b:
                take_turn("pe", b, (0, 1), doers)
            take_turn("pe", B, (1,), doers)

            def output(c, par, n=P, first=False, last=False):
                e.wait_ge(w2_done, c + 1)
                for h in range(2):
                    e.wait_ge(hid_done, half_count(c, h))
                    cols = slice(h * HALF, (h + 1) * HALF)
                    for d in range(KC):
                        f = slice(d * P, (d + 1) * P)
                        mm = three(y_bank[d][h][:], w2_hi[0:n, par, f], w2_lo[0:n, par, f],
                                   hid_hi[0:n, par, cols], hid_lo[0:n, par, cols], first, last,
                                   skip_group_check=True)
                    if last:
                        step(mm, f"y sum {h}")
                if not last:
                    mm.then_inc(y_done, 1)

            e.wait_ge(emptied, slot_count(B - 1, "y"))
            e.wait_ge(res_done, B + 1)
            router(1)
            hidden_half(0, 0, 1)
            after("act", "sig 1")
            for t in range(NT):
                mm = nc.tensor.transpose(bank[0][:, t * NR:(t + 1) * NR], sigT[:, t * P:(t + 1) * P], ident[0:NR, 0:NR])
            step(mm, "scores turned")
            hidden_half(1, 1, 1)
            after("dve", "choice")
            output(0, 0, first=True)
            after("dve", "gates")
            e.wait_ge(relu_done, 4)
            for t in range(NT):
                mm = nc.tensor.transpose(z_bank[1][t // 4][0:NR, (t % 4) * P:(t % 4 + 1) * P], gates[:, t, :], ident[:])
            step(mm, "gatesT")
            hidden(2, 0)
            output(1, 1)
            after("dve", "gatesT")
            hidden(3, 1)
            for d in range(KC):
                for h in range(2):
                    nc.tensor.matmul(y_bank[d][h][:], b2_rows[:, d * P:(d + 1) * P],
                                     gatesT[:, h * HALF:(h + 1) * HALF], start=False, stop=False,
                                     skip_group_check=True)
            with e.Fori(1, (NC - 3) // 2) as cc:
                for par in range(2):
                    output(2 * cc + par, par)
                    e.wait_ge(relu_done, 2 * (2 * cc + par + 1))
                    hidden(2 * cc + par + 2, par)
            output(NC - 3, (NC - 3) % 2)
            e.wait_ge(relu_done, 2 * (NC - 2))
            hidden(NC - 1, (NC - 1) % 2, LAST)
            output(NC - 2, (NC - 2) % 2)
            e.wait_ge(two_done, 1)
            for h in range(2):
                cols = slice(h * HALF, (h + 1) * HALF)
                for d in range(KC):
                    for part in (x2T_hi, x2T_lo):
                        nc.tensor.matmul(y_bank[d][h][:], two_ident[:], part[:, d, cols], start=False, stop=False,
                                         skip_group_check=True)
            output(NC - 1, (NC - 1) % 2, LAST, last=True)
            for t in range(NT):
                if t == 0:
                    after("act", "yT 0")
                if t == 4:
                    after("act", "yT 1")
                for d in range(KC):
                    mm = nc.tensor.transpose(bank[2 + t // 2][:, (t % 2) * C + d * P:(t % 2) * C + (d + 1) * P],
                                             yT[:, d, t * P:(t + 1) * P], ident[:])
                if t % 2:
                    step(mm, f"y {t // 2}")

        @block.scalar
        def _(e):
            def piece(n):
                e.wait_ge(ld_stage[n % 4], 16 * (n // 4 + 1))
                nc.scalar.copy(PIECES[n][1], stage_view(n)).then_inc(w_hi, 1)

            def split_w1(c, par, n=P):
                nc.scalar.copy(w1_hi[:, par, :, 0:n], w1_raw[:, :, bass.ds(c * P, n)]).then_inc(w1_hi_done, 1)

            def split_w2(c, par, n=P):
                nc.scalar.copy(w2_hi[0:n, par, :], w2_raw[0:n, bass.ds(c, 1), :].rearrange("p a c -> p (a c)")).then_inc(w2_hi_done, 1)

            def relu(c, par, h, n=P):
                e.wait_ge(z_done, half_count(c, h))
                e.sem_inc(act_passed, 1)
                nc.scalar.activation(hid[0:n, par, h * HALF:(h + 1) * HALF], bank[2 + 2 * par + h][0:n, :], ACT.Relu,
                                     bias=b1_cols[0:n, bass.ds(c, 1)]).then_inc(relu_done, 1)

            def hid_high(c, par, h, n=P):
                if isinstance(c, int) and c < UNGATED:
                    e.wait_ge(relu_done, half_count(c, h))
                else:
                    e.wait_ge(gated, gate_count(c, h))
                cols = slice(h * HALF, (h + 1) * HALF)
                nc.scalar.copy(hid_hi[0:n, par, cols], hid[0:n, par, cols]).then_inc(hid_hi_done, 1)

            def last_root(which):
                if which == 0:
                    nc.scalar.activation(unused[:], ident[:, 0:1], ACT.Sqrt)
                e.wait_ge(moments_done, 2 * (B - 1) + which + 1)
                nc.scalar.activation(root[:], var_eps[:], ACT.Sqrt).then_inc(root_done, 1)

            def score_sigmoid(h):
                after(f"router {h}")
                step(nc.scalar.activation(sigT[:, h * HALF:(h + 1) * HALF], bank[6 + h][0:NR, :], ACT.Sigmoid), f"sig {h}")

            def slot(b, s):
                n, kind, j = SLOTS.index(s), s[0], int(s[1:] or 0)
                if kind == "n" and isinstance(b, int) and b == B - 1:
                    last_root(0)
                    e.wait_ge(res_done, B + 1)
                    e.wait_ge(ld_w1, 16 * 4)
                    e.wait_ge(ld_w2, 16 * 5)
                    split_w1(0, 0), split_w1(1, 1)
                    split_w2(0, 0), split_w2(1, 1)
                if kind in "nm":
                    return
                if kind == "y" and isinstance(b, int) and b == B - 1:
                    last_root(1)
                    score_sigmoid(0)
                o = proj_bank[n % 2]
                e.wait_ge(projected, slot_count(b, s))
                if kind == "x":
                    nc.scalar.copy(xT_hi[:, j, :], o[:, 0:T]).then_inc(split_hi, 1)
                elif kind == "y":
                    e.wait_ge(w_lo, len(PIECES))
                    e.sem_inc(act_passed, 1)
                    nc.scalar.copy(x2T_hi[:, :, bass.ds(b * T, T)],
                                   o[:].rearrange("p (k t) -> p k t", k=KC)).then_inc(x2_hi_done, 1)
                    if isinstance(b, int) and b == B - 1:
                        relu(0, 0, 0)
                        hid_high(0, 0, 0)
                        relu(1, 1, 0)
                        hid_high(1, 1, 0)
                elif kind == "v":
                    nc.scalar.copy(v_hi[:, j, :], o[:]).then_inc(split_hi, 1)
                else:
                    r = ROPES.index(s)
                    if not (isinstance(b, int) and b == 0 and r < 2):
                        e.wait_ge(rope_mul, rope_count(b, s) - 2)
                    half = D // 2
                    nc.scalar.copy(swapped[0:half, r % 2, :], o[half:D, :])
                    nc.scalar.copy(swapped[half:D, r % 2, :], o[0:half, :]).then_inc(swap_done, 1)

            def softmax_exp(b, h):
                u, w = h % 2, h % RING
                e.wait_ge(top_done, head_count(b, h))
                e.wait_ge(norm_done, head_count(b, h - RING))
                nc.scalar.activation(probs[:, w, 0:W], scores[:, u, 0:W], ACT.Exp, bias=ntop[:, u, 0:1],
                                     scale=SCALE, accum_out=psums[:, w, 0:1])
                nc.scalar.activation(probs[:, w, W:3 * W], scores[:, u, W:3 * W], ACT.Exp, bias=ntop[:, u, 1:2],
                                     scale=SCALE, accum_out=psums[:, w, 1:2]).then_inc(exp_done, 1)

            def probs_hi(b, h):
                e.wait_ge(turned, head_count(b, h))
                nc.scalar.copy(pT_hi[:, (h // G) % 2, :, h % G, :],
                               prob_bank[h % 2][:, 0:3 * W].rearrange("p (k q) -> p k q", k=3)).then_inc(pT_hi_done, 1)

            def heads_hi(b, g, blk):
                e.wait_ge(pv_done, pv_count(b, g, blk))
                nc.scalar.copy(oT_hi[:, blk, :], pv_of(b, g, blk)[:]).then_inc(oT_hi_done, 1)

            n = [0]

            def step(ins, name):
                assert ORDER["act"][n[0]] == name, (ORDER["act"][n[0]], name)
                n[0] += 1
                ins.then_inc(act, 1)

            def after(name):
                e.wait_ge(pe, place("pe", name))

            def after_dve(name):
                e.wait_ge(dve, place("dve", name))

            def once(work, of):
                if work == "piece":
                    piece(of)
                elif work == "ctx turned":
                    after("xwT")
                    step(nc.scalar.copy(xwT[:].rearrange("p a d -> p (a d)"), bank[3][:, 0:2 * D]), "xwT")
                    after("ctxT 0")
                    step(nc.scalar.copy(ctxT[:, 0:HALF], bank[6][:]), "ctxT 0")
                elif work == "ctx projected":
                    for h in range(2):
                        after(f"xp 0 {h}")
                        step(nc.scalar.activation(xqT[:, h * HALF:(h + 1) * HALF], bank[4 + h][:], ACT.Identity,
                                                  bias=xb_cols[:, 0:1]), f"xqT {h}")
                elif work[:-2] == "e_exp":
                    c = int(work[-1])
                    after_dve(f"e_top {c}")
                    for t in range(TT):
                        ins = nc.scalar.activation(e_exp[:, c, t, :], bank[E_BANK[c]][:, t * T:(t + 1) * T], ACT.Exp,
                                                   bias=e_ntop[:, c, t:t + 1], accum_out=e_sum[:, c, t:t + 1])
                    step(ins, work)
                elif work == "small turned":
                    after("smallT")
                    nc.scalar.copy(centT_hi[:].rearrange("p k r -> p (k r)"), bank[7][:, 0:KC * NR])
                    step(nc.scalar.copy(b1_cols[:], bank[7][:, 64:64 + NC]), "smallT")
                    nc.scalar.activation(two_ident[:], ident[:], ACT.Copy, scale=2.0).then_inc(two_done, 1)
                else:
                    c = int(work[-1])
                    after(work)
                    step(nc.scalar.copy(attT[:, c, :, :].rearrange("p k r -> p (k r)"), bank[E_BANK[c]][:]), work)

            for s in (exp_done, pT_hi_done):
                e.sem_inc(s, AHEAD)
            for s in (oT_hi_done, pv_done):
                e.sem_inc(s, 1)
            doers = {"slot": slot, "exp": softmax_exp, "probs_hi": probs_hi, "once": once,
                     "heads_hi0": lambda b, g: heads_hi(b, g, 0), "heads_hi1": lambda b, g: heads_hi(b, g, 1)}
            take_turn("act", 0, (0, "once"), doers)
            with e.Fori(1, B) as b:
                take_turn("act", b, (0, 1), doers)
            take_turn("act", B, (1,), doers)

            def high_parts(c, par, nxt=None, n=P, n_next=P):
                relu(c, par, 0, n), relu(c, par, 1, n)
                if nxt is not None:
                    split_w1(nxt, 1 - par, n_next)
                hid_high(c, par, 0, n), hid_high(c, par, 1, n)
                if nxt is not None:
                    e.wait_ge(y_done, nxt - 1)
                    split_w2(nxt, 1 - par, n_next)

            score_sigmoid(1)
            relu(0, 0, 1)
            hid_high(0, 0, 1)
            relu(1, 1, 1)
            hid_high(1, 1, 1)
            split_w1(2, 0)
            e.wait_ge(y_done, 1)
            split_w2(2, 0)
            high_parts(2, 0, 3)
            with e.Fori(1, (NC - 3) // 2) as cc:
                for par in range(2):
                    high_parts(2 * cc + par + 1, 1 - par, 2 * cc + par + 2)
            high_parts(NC - 2, 1, NC - 1, n_next=LAST)
            high_parts(NC - 1, 0, n=LAST)
            nc.scalar.activation(unused[:], ident[:, 0:1], ACT.Sqrt)

            for h in range(2):
                after(f"y sum {h}")
                nc.scalar.copy(yT[:, 0, h * HALF:(h + 1) * HALF], bank[6 + h][:])
                step(nc.scalar.copy(yT[:, 1, h * HALF:(h + 1) * HALF], bank[h][:]), f"yT {h}")
            for q in range(2):
                after_dve(f"var 3 {q}")
                step(nc.scalar.activation(ln_std[:, 4 * q:4 * q + 4], ln_var[:, 4 * q:4 * q + 4], ACT.Sqrt), f"std 3 {q}")
                after_dve(f"shift 3 {q}")
                for t in (4 * q + 2, 4 * q + 3):
                    step(nc.scalar.activation(x3[:, t, :], bank[2 + t // 2][:, (t % 2) * C:(t % 2 + 1) * C], ACT.Identity,
                                              bias=ln_shift[:, t:t + 1], scale=ln_rstd[:, t:t + 1]), f"x3 {t}")

        @block.vector
        def _(e):
            low = lambda o, full, hi: nc.vector.tensor_tensor(o, full, hi.bitcast(F32), ALU.subtract)

            def piece(n):
                e.wait_ge(w_hi, n + 1)
                low(PIECES[n][2], stage_view(n), PIECES[n][1]).then_inc(w_lo, 1)

            def gate(c, par, h, n=P):
                e.wait_ge(relu_done, half_count(c, h))
                if h == 0:
                    e.wait_ge(ld_gates[par], 8 * (c - par))
                cols = slice(h * HALF, (h + 1) * HALF)
                nc.vector.tensor_tensor(hid[0:n, par, cols], hid[0:n, par, cols], gate_rows[0:n, par, cols],
                                        ALU.mult).then_inc(gated, 1)

            def hid_low(c, par, h, n=P):
                e.wait_ge(hid_hi_done, half_count(c, h))
                cols = slice(h * HALF, (h + 1) * HALF)
                low(hid_lo[0:n, par, cols], hid[0:n, par, cols], hid_hi[0:n, par, cols]).then_inc(hid_done, 1)

            def slot(b, s):
                n, kind, j = SLOTS.index(s), s[0], int(s[1:] or 0)
                o = proj_bank[n % 2]
                if kind == "y":
                    e.wait_ge(x2_hi_done, b + 1)
                    tokens = bass.ds(b * T, T)
                    low(x2T_lo[:, :, tokens], o[:].rearrange("p (k t) -> p k t", k=KC), x2T_hi[:, :, tokens]).then_inc(emptied, 1)
                    if isinstance(b, int) and b == B - 1:
                        hid_low(0, 0, 0), hid_low(1, 1, 0)
                    return
                if kind == "n":
                    e.wait_ge(projected, slot_count(b, s))
                    nc.vector.tensor_copy(x1T[:].rearrange("p k t -> p (k t)"), o[:]).then_inc(emptied, 1)
                    if isinstance(b, int) and b == B - 1:
                        nc.vector.memset(choice[:, :, NR:SC], NEVER)
                        step(nc.vector.memset(gatesT[:], 1.0), "gates ready")
                    return
                if kind == "m":
                    e.wait_ge(projected, slot_count(b, s))
                    nc.vector.tensor_tensor(xln[:, j, :], o[:, 0:C], xln[:, j, :], ALU.add).then_inc(emptied, 1)
                    return
                if kind in "xv":
                    e.wait_ge(split_hi, split_count(b, s))
                    if kind == "x":
                        low(xT_lo[:, j, :], o[:, 0:T], xT_hi[:, j, :]).then_inc(emptied, 1)
                    else:
                        low(v_lo[:, j, :], o[:], v_hi[:, j, :]).then_inc(emptied, 1)
                    return
                r = ROPES.index(s)
                if isinstance(b, int) and b == 0 and r == 0:
                    e.wait_ge(ld_tables, 48)
                e.wait_ge(swap_done, rope_count(b, s))
                if not (isinstance(b, int) and b == 0 and r < 2):
                    e.wait_ge(rope_add, rope_count(b, s) - 2)
                nc.vector.tensor_tensor(by_cos[:, r % 2, :], o[:], cos_t[:], ALU.mult).then_inc(emptied, 1)
                nc.vector.tensor_tensor(by_sin[:, r % 2, :], swapped[:, r % 2, :], sin_t[:], ALU.mult).then_inc(rope_mul, 1)

            def mask_and_top(b, h):
                u = h % 2
                e.wait_ge(scored, H * b + h + 1)
                e.wait_ge(exp_done, head_count(b, h - 2))
                e.sem_inc(dve_passed, 1)
                o = score_bank[u]
                nc.vector.tensor_tensor_reduce(scores[:, u, 0:W], o[:, 0:W], mask[:, W:2 * W], 1.0, NEVER,
                                               ALU.add, ALU.max, top[:, u, 0:1])
                nc.vector.tensor_tensor_reduce(scores[:, u, W:3 * W], o[:, W:3 * W], mask[:], 1.0, NEVER,
                                               ALU.add, ALU.max, top[:, u, 1:2]).then_inc(score_read, 1)
                e.wait_ge(score_read, head_count(b, h))
                nc.vector.tensor_scalar(ntop[:, u, :], top[:, u, :], -SCALE, None, ALU.mult).then_inc(top_done, 1)

            def recip(b, h):
                e.wait_ge(exp_done, head_count(b, h))
                nc.vector.reciprocal(rsums[:, h % RING, :], psums[:, h % RING, :]).then_inc(rsum_done, 1)

            def probs_lo(b, h):
                e.wait_ge(pT_hi_done, head_count(b, h))
                g = (h // G) % 2
                low(pT_lo[:, g, :, h % G, :], prob_bank[h % 2][:, 0:3 * W].rearrange("p (k q) -> p k q", k=3),
                    pT_hi[:, g, :, h % G, :]).then_inc(pT_done, 1)

            def heads_lo(b, g, blk):
                e.wait_ge(oT_hi_done, pv_count(b, g, blk))
                low(oT_lo[:, blk, :], pv_of(b, g, blk)[:], oT_hi[:, blk, :]).then_inc(oT_done, 1)

            def residual(b, _):
                e.wait_ge(attn_done, b + 1)
                if not (isinstance(b, int) and b == 0):
                    e.wait_ge(projected, slot_count(b - 1, "y"))
                nc.vector.tensor_tensor(xln[:], attn_bank[:].rearrange("p (t c) -> p t c", t=TT),
                                        res[:, bass.ds(b * TT, TT), :], ALU.add).then_inc(res_done, 1)

            def moments_of(b, which):
                m = 2 * b + which
                if which == 0:
                    e.wait_ge(res_done, b + 2)
                else:
                    e.wait_ge(emptied, slot_count(b, LAST_M))
                e.sem_inc(dve_passed, 1)
                for t in range(TT):
                    ins = nc.vector.bn_stats(bn[:, t, :], xln[:, t, :])
                ins.then_inc(stats_done, 1)
                e.wait_ge(stats_done, m + 1)
                if which or not (isinstance(b, int) and b == 0):
                    e.wait_ge(ln_done, m)
                e.sem_inc(dve_passed, 1)
                for t in range(TT):
                    ins = nc.vector.bn_aggr(moments[:, t, :], bn[:, t, :])
                ins.then_inc(aggr_done, 1)
                e.wait_ge(aggr_done, m + 1)
                var = moments[:, :, 1:2].rearrange("p t a -> p (t a)")
                nc.vector.tensor_scalar(var_eps[:], var, EPS, 1.0, ALU.add, ALU.mult)
                nc.vector.tensor_scalar(half_neg[:], var, EPS, -0.5, ALU.add, ALU.mult).then_inc(moments_done, 1)

            def normed(b, which):
                m = 2 * b + which
                if isinstance(b, int) and b == B - 1:
                    e.wait_ge(root_done, which + 1)
                    nc.vector.reciprocal(newton[:, 0, :], root[:]).then_inc(inverted, 1)
                    e.wait_ge(inverted, which + 1)
                else:
                    e.wait_ge(newton_done, NEWTON_STEPS * (m + 1))
                e.sem_inc(dve_passed, 1)
                for t in range(TT):
                    ins = nc.vector.tensor_scalar(xln[:, t, :], xln[:, t, :], moments[:, t, 0:1],
                                                  newton[:, 0, t:t + 1], ALU.subtract, ALU.mult)
                ins.then_inc(ln_done, 1)

            n = [0]

            def step(ins, name):
                assert ORDER["dve"][n[0]] == name, (ORDER["dve"][n[0]], name)
                n[0] += 1
                ins.then_inc(dve, 1)

            def after(name):
                e.wait_ge(pe, place("pe", name))

            def after_act(name):
                e.wait_ge(act, place("act", name))

            def settle():
                e.wait_ge(dve, n[0])

            def once(work, of):
                if work == "piece":
                    piece(of)
                elif work == "ctx turned":
                    after("ctxT 1")
                    step(nc.vector.tensor_copy(ctxT[:, HALF:N], bank[7][:]), "ctxT 1")
                elif work == "ctx projected":
                    for h in range(2):
                        after(f"xp 1 {h}")
                        step(nc.vector.tensor_scalar(xkT[:, h * HALF:(h + 1) * HALF], bank[6 + h][:], xb_cols[:, 1:2], None,
                                                     ALU.add), f"xkT {h}")
                elif work == "small turned":
                    after_act("smallT")
                    step(low(centT_lo[:].rearrange("p k r -> p (k r)"), bank[7][:, 0:KC * NR],
                             centT_hi[:].rearrange("p k r -> p (k r)")), "centT_lo")
                elif work[:-2] == "e_top":
                    c = int(work[-1])
                    after(f"energy {c}")
                    step(nc.vector.tensor_reduce(e_ntop[:, c, :], bank[E_BANK[c]][:].rearrange("p (t s) -> p t s", t=TT),
                                                 AX.X, ALU.max, negate=True), work)
                else:
                    c = int(work[-1])
                    after_act(f"e_exp {c}")
                    step(nc.vector.reciprocal(e_rsum[:, c, :], e_sum[:, c, :]), f"e_rsum {c}")
                    settle()
                    for t in range(TT):
                        ins = nc.vector.tensor_scalar(e_exp[:, c, t, :], e_exp[:, c, t, :], e_rsum[:, c, t:t + 1], None,
                                                      ALU.mult)
                    step(ins, work)

            for s in (score_read, top_done, rsum_done, pT_done):
                e.sem_inc(s, AHEAD)
            for s in (oT_done, res_done):
                e.sem_inc(s, 1)
            doers = {"slot": slot, "top": mask_and_top, "recip": recip, "probs_lo": probs_lo, "once": once,
                     "heads_lo0": lambda b, g: heads_lo(b, g, 0), "heads_lo1": lambda b, g: heads_lo(b, g, 1),
                     "residual": residual, "moments 1": lambda b, _: moments_of(b, 0),
                     "moments 2": lambda b, _: moments_of(b, 1),
                     "normed 1": lambda b, _: normed(b, 0), "normed 2": lambda b, _: normed(b, 1)}
            step(nc.vector.memset(b1_rows[:], 0.0), "b1 cleared")
            take_turn("dve", 0, (0, "once"), doers)
            e.wait_ge(ld_res, 16)
            with e.Fori(1, B) as b:
                take_turn("dve", b, (0, 1), doers)
            take_turn("dve", B, (1,), doers)

            def y_tile(t):
                return bank[2 + t // 2][:, (t % 2) * C:(t % 2 + 1) * C]

            hid_low(0, 0, 1)

            after("scores turned")
            e.wait_ge(ld_small, 16 * 9)
            step(nc.vector.tensor_tensor(choice[:, :, 0:NR], bank[0][:, 0:NT * NR].rearrange("p (t r) -> p t r", r=NR),
                                         gbias_sb[:].rearrange("p (a r) -> p a r", a=1).broadcast_to((P, NT, NR)), ALU.add), "choice")
            settle()
            for t in range(NT):
                ins = nc.vector.max(best[:, t, :], choice[:, t, 0:NR])
            step(ins, "best")
            settle()
            step(nc.vector.memset(best[:, :, KR:8], NEVER), "best four")
            settle()
            for t in range(NT):
                ins = nc.vector.match_replace(taken[:, t, :], best[:, t, :], choice[:, t, :], -NEVER)
            step(ins, "taken")
            settle()
            step(nc.vector.tensor_tensor(chosen[:], taken[:, :, 0:NR], choice[:, :, 0:NR], ALU.not_equal), "chosen")
            settle()
            step(nc.vector.tensor_tensor(gates[:], chosen[:], choice[:, :, 0:NR], ALU.mult), "open")
            settle()
            step(nc.vector.tensor_reduce(gate_sum[:], gates[:], AX.X, ALU.add), "gate sum")
            settle()
            step(nc.vector.tensor_scalar(gate_sum[:], gate_sum[:], 1e-8, None, ALU.max), "gate clip")
            settle()
            step(nc.vector.reciprocal(gate_rsum[:], gate_sum[:]), "gate rsum")
            settle()
            step(nc.vector.tensor_tensor(gates[:], gates[:], gate_rsum[:].rearrange("p (t a) -> p t a", a=1).broadcast_to((P, NT, NR)),
                                         ALU.mult), "gates")
            hid_low(1, 1, 1)
            after("gatesT")
            for h in range(2):
                ins = nc.vector.tensor_copy(gatesT[0:NR, h * HALF:(h + 1) * HALF], bank[4 + h][0:NR, :])
            step(ins, "gatesT")

            def low_parts(c, par, n=P):
                gate(c, par, 0, n), gate(c, par, 1, n)
                hid_low(c, par, 0, n), hid_low(c, par, 1, n)

            low_parts(2, 0)
            with e.Fori(1, (NC - 3) // 2) as cc:
                for par in range(2):
                    low_parts(2 * cc + par + 1, 1 - par)
            low_parts(NC - 2, 1)
            low_parts(NC - 1, 0, LAST)

            def final_stats(q):
                for t in range(4 * q, 4 * q + 4):
                    if t % 2 == 0:
                        after(f"y {t // 2}")
                    step(nc.vector.bn_stats(ln_stats[:, t, :], y_tile(t)), f"stats 3 {t}")

            def final_var(q):
                a, z = 4 * q, 4 * q + 4
                settle()
                for t in range(a, z):
                    step(nc.vector.bn_aggr(ln_mv[:, t, :], ln_stats[:, t, :]), f"aggr 3 {t}")
                settle()
                step(nc.vector.tensor_scalar(ln_var[:, a:z], ln_mv[:, a:z, 1:2].rearrange("p t a -> p (t a)"),
                                             EPS, None, ALU.add), f"var 3 {q}")

            def final_norm(q):
                a, z = 4 * q, 4 * q + 4
                after_act(f"std 3 {q}")
                step(nc.vector.reciprocal(ln_rstd[:, a:z], ln_std[:, a:z]), f"rstd 3 {q}")
                settle()
                step(nc.vector.scalar_tensor_tensor(ln_shift[:, a:z], ln_mv[:, a:z, 0:1].rearrange("p t a -> p (t a)"), -1.0,
                                                    ln_rstd[:, a:z], ALU.mult, ALU.mult), f"shift 3 {q}")
                for t in (a, a + 1):
                    step(nc.vector.tensor_scalar(x3[:, t, :], y_tile(t), ln_mv[:, t, 0:1], ln_rstd[:, t:t + 1],
                                                 ALU.subtract, ALU.mult), f"x3 {t}")

            final_stats(0), final_var(0)
            final_stats(1), final_norm(0)
            final_var(1), final_norm(1)

        @block.gpsimd
        def _(e):
            def slot(b, s):
                if s[0] not in "kq":
                    return
                r, j = ROPES.index(s), int(s[1])
                o = keyT[:, 2 * j:2 * j + 2, :] if s[0] == "k" else queryT[:, j % 4, :, :]
                e.wait_ge(rope_mul, rope_count(b, s))
                nc.gpsimd.tensor_tensor(o.rearrange("p a t -> p (a t)"), by_cos[:, r % 2, :], by_sin[:, r % 2, :],
                                        ALU.add).then_inc(rope_add, 1)

            def normalise(b, h):
                u = h % RING
                e.wait_ge(rsum_done, head_count(b, h))
                e.wait_ge(turned, head_count(b, h - RING))
                e.sem_inc(pool_passed, 1)
                nc.gpsimd.tensor_scalar(nprobs[:, u, 0:W], probs[:, u, 0:W], rsums[:, u, 0:1], 1.0, ALU.mult, ALU.mult)
                nc.gpsimd.tensor_scalar(nprobs[:, u, W:3 * W], probs[:, u, W:3 * W], rsums[:, u, 1:2], 1.0,
                                        ALU.mult, ALU.mult).then_inc(norm_done, 1)

            def low_w1(c, par, n=P):
                e.wait_ge(w1_hi_done, c + 1)
                nc.gpsimd.tensor_tensor(w1_lo[:, par, :, 0:n], w1_raw[:, :, bass.ds(c * P, n)],
                                        w1_hi[:, par, :, 0:n].bitcast(F32), ALU.subtract).then_inc(w1_done, 1)

            def low_w2(c, par, n=P):
                e.wait_ge(w2_hi_done, c + 1)
                nc.gpsimd.tensor_tensor(w2_lo[0:n, par, :], w2_raw[0:n, bass.ds(c, 1), :].rearrange("p a c -> p (a c)"),
                                        w2_hi[0:n, par, :].bitcast(F32), ALU.subtract).then_inc(w2_done, 1)

            def layer_norm(b, which):
                if isinstance(b, int) and b == B - 1:
                    if which == 1:
                        low_w1(0, 0), low_w1(1, 1)
                        low_w2(0, 0), low_w2(1, 1)
                    return
                m = 2 * b + which
                done = [0]

                def settled(ins):
                    done[0] += 1
                    ins.then_inc(newton_done, 1)
                    e.wait_ge(newton_done, NEWTON_STEPS * m + done[0])
                e.wait_ge(moments_done, m + 1)
                e.sem_inc(pool_passed, 1)
                y, yv = newton[:, 0, :], newton[:, 1, :]
                settled(nc.gpsimd.tensor_scalar(y.bitcast(I32), var_eps[:].bitcast(I32), -0.5, float(RSQRT_BITS),
                                                ALU.mult, ALU.add))
                settled(nc.gpsimd.tensor_tensor(yv, y, half_neg[:], ALU.mult))
                for _ in range(NEWTON):
                    settled(nc.gpsimd.tensor_tensor(factor[:], y, yv, ALU.mult))
                    e.sem_inc(pool_passed, 1)
                    settled(nc.gpsimd.tensor_scalar(factor[:], factor[:], 1.5, 1.0, ALU.add, ALU.mult))
                    settled(nc.gpsimd.tensor_tensor(newton[:], newton[:],
                                                    factor[:].rearrange("p (a t) -> p a t", a=1).broadcast_to((P, 2, TT)),
                                                    ALU.mult))
                assert done[0] == NEWTON_STEPS

            for s in (norm_done, turned):
                e.sem_inc(s, AHEAD)
            doers = {"slot": slot, "normalise": normalise, "norm 1": lambda b, _: layer_norm(b, 0),
                     "norm 2": lambda b, _: layer_norm(b, 1)}
            take_turn("pool", 0, (0,), doers)
            with e.Fori(1, B) as b:
                take_turn("pool", b, (0, 1), doers)
            take_turn("pool", B, (1,), doers)

            with e.Fori(0, (NC - 3) // 2) as cc:
                for par in range(2):
                    low_w1(2 * cc + par + 2, par)
                    low_w2(2 * cc + par + 2, par)
            low_w1(NC - 1, 0, LAST)
            low_w2(NC - 1, 0, LAST)


def once_order(engine, steps):
    return [n for w in sorted(ONCE_AT[engine], key=ONCE_AT[engine].get) for n in steps.get(w, [w])]


ORDER = {
    "pe": once_order("pe", {"ctx turned": ["xwT", "ctxT 0", "ctxT 1"],
                            "ctx projected": [f"xp {a} {h}" for a in range(2) for h in range(2)],
                            "small turned": ["smallT"]})
    + ["router 0", "router 1", "scores turned", "gatesT", "y sum 0", "y sum 1"] + [f"y {u}" for u in range(NT // 2)],
    "act": once_order("act", {"ctx turned": ["xwT", "ctxT 0"], "ctx projected": ["xqT 0", "xqT 1"],
                              "small turned": ["smallT"]})
    + ["sig 0", "sig 1", "yT 0", "yT 1", "std 3 0", "x3 2", "x3 3", "std 3 1", "x3 6", "x3 7"],
    "dve": ["b1 cleared"] + once_order("dve", {"ctx turned": ["ctxT 1"], "ctx projected": ["xkT 0", "xkT 1"],
                              "small turned": ["centT_lo"],
                              **{f"e_norm {b}": [f"e_rsum {b}", f"e_norm {b}"] for b in range(B)}})
    + ["gates ready", "choice", "best", "best four", "taken", "chosen", "open", "gate sum", "gate clip", "gate rsum",
       "gates", "gatesT"]
    + [f"stats 3 {t}" for t in range(4)] + [f"aggr 3 {t}" for t in range(4)] + ["var 3 0"]
    + [f"stats 3 {t}" for t in range(4, 8)] + ["rstd 3 0", "shift 3 0", "x3 0", "x3 1"]
    + [f"aggr 3 {t}" for t in range(4, 8)] + ["var 3 1", "rstd 3 1", "shift 3 1", "x3 4", "x3 5"],
}

_INS = ["x", "ctx_1024", "L0_attn_q_kernel", "L0_attn_k_kernel", "L0_attn_v_kernel", "L0_attn_out_kernel",
        "L0_xattn_Wq", "L0_xattn_bq", "L0_xattn_Wk", "L0_xattn_bk", "L0_ffn_shared_w1", "L0_ffn_shared_b1",
        "L0_ffn_shared_w2", "L0_ffn_shared_b2", "L0_ffn_routed_w1", "L0_ffn_routed_b1", "L0_ffn_routed_w2",
        "L0_ffn_routed_b2", "L0_ffn_centroids", "L0_ffn_bias"]


def kernel(**inputs):
    import concourse.bacc as bacc
    from concourse.bass_utils import run_bass_kernel_spmd

    nc = bacc.Bacc("TRN2", target_bir_lowering=False, num_devices=1)
    cos_c, sin_c = rope_tables()
    consts = {"cos_c": cos_c, "sin_c": sin_c, "mask_c": window_mask(), "ident_c": np.eye(P, dtype=np.float32)}
    arrays, args = {}, []
    for name, a in [(n, inputs[n]) for n in _INS] + list(consts.items()):
        a = np.ascontiguousarray(a)
        arrays[f"in_{name}"] = a
        args.append(nc.dram_tensor(f"in_{name}", a.shape, mybir.dt.from_np(a.dtype), kind="ExternalInput").ap())
    out = nc.dram_tensor("out", (B, T, C), F32, kind="ExternalOutput").ap()
    gates_d = nc.dram_tensor("gates_d", (NE * FF // GB, N), F32, kind="Internal").ap()
    decoder_layer(nc, *args, out, gates_d)
    r = run_bass_kernel_spmd(nc, [arrays], core_ids=[0])
    return r.results[0]["out"]
```
